# Optimizing a Trainium2 kernel written in Bass

```python
import numpy as np
import jax
import jax.numpy as jnp

def _softmax(x, axis=-1):
    return jax.nn.softmax(x, axis=axis)

def _gelu(x):
    return jax.nn.gelu(x, approximate=True)

def _silu(x):
    return jax.nn.silu(x)

def _sigmoid(x):
    return jax.nn.sigmoid(x)

def _layernorm(x, axis=-1, eps=1e-05):
    m = jnp.mean(x, axis=axis, keepdims=True)
    v = jnp.var(x, axis=axis, keepdims=True)
    return (x - m) / jnp.sqrt(v + eps)

def _scatter_add(tgt, idx, src, axis=0):
    return tgt.at[idx].add(src)

def _segment_sum(src, seg, n):
    return jax.ops.segment_sum(src, seg, n)
kernel_name = 'mk_prb_d2_jaxref_r8_61ae59'

def setup_inputs(seed: int=0):
    np.random.seed(seed)
    _w = jnp.asarray

    def _L0_attn_setup():
        import jax, jax.numpy as jnp
        import numpy as np
        B, L, D = (8, 512, 128)
        H, f, K = (2, 128, 16)
        d = H * f
        TTT_BASE_LR = 1.0

        def _ln(x, g, b, eps=1e-06):
            mu = x.mean(-1, keepdims=True)
            var = ((x - mu) ** 2).mean(-1, keepdims=True)
            return g * (x - mu) * jax.lax.rsqrt(var + eps) + b

        def _ln_fused_l2_bwd(x, target, g, b, eps=1e-06):
            Dh = x.shape[-1]
            mu = x.mean(-1, keepdims=True)
            var = ((x - mu) ** 2).mean(-1, keepdims=True)
            std = jnp.sqrt(var + eps)
            xh = (x - mu) / std
            gy = (g * xh + b - target) * g
            return (Dh * gy - gy.sum(-1, keepdims=True) - xh * (gy * xh).sum(-1, keepdims=True)) / (Dh * std)

        def _ttt_linear(h, wq, wk, wv, wo, W1, b1, ttt_ln_w, ttt_ln_b, lr_w, lr_b, tok_idx, post_w, post_b):
            Bb, Ll, dm = h.shape
            nm = Ll // K

            def heads(w):
                return (h @ w).reshape(Bb, nm, K, H, f).transpose(0, 3, 1, 2, 4)
            XQ, XK, XV = (heads(wq), heads(wk), heads(wv))
            Xm = h.reshape(Bb, nm, K, dm)
            ttt_lr = jax.nn.sigmoid(jnp.einsum('bnkc,hoc->bhnko', Xm, lr_w) + lr_b[None, :, None, None, None])
            ttt_lr_eta = TTT_BASE_LR * ttt_lr.transpose(0, 1, 2, 4, 3) / f
            token_idx = jnp.maximum(1.0 / jnp.arange(1, K + 1, dtype=jnp.float32) + tok_idx, 0.0)
            eta = token_idx[None, None, None, :, None] * ttt_lr_eta
            gw = ttt_ln_w[:, None, :]
            gb = ttt_ln_b[:, None, :]

            def step(carry, inp):
                W1c, b1c = carry
                xq, xk, xv, et = inp
                Z1 = xk @ W1c + b1c
                grad = _ln_fused_l2_bwd(Z1, xv - xk, gw, gb)
                Attn = jnp.tril(xq @ jnp.swapaxes(xk, -1, -2))
                b1_bar = b1c - jnp.tril(et) @ grad
                Z1_bar = xq @ W1c - et * Attn @ grad + b1_bar
                last_eta = et[:, :, -1, :, None]
                W1n = W1c - jnp.swapaxes(last_eta * xk, -1, -2) @ grad
                b1n = b1c - (last_eta * grad).sum(-2, keepdims=True)
                return ((W1n, b1n), xq + _ln(Z1_bar, gw, gb))
            carry0 = (jnp.broadcast_to(W1[None], (Bb, H, f, f)), jnp.broadcast_to(b1[None], (Bb, H, 1, f)))
            xs = tuple((a.transpose(2, 0, 1, 3, 4) for a in (XQ, XK, XV, eta)))
            _, outs = jax.lax.scan(step, carry0, xs)
            out = outs.transpose(1, 0, 3, 2, 4).reshape(Bb, Ll, dm)
            out = _ln(out, post_w, post_b, eps=1e-05)
            return out @ wo
        key = jax.random.key(seed)
        ks = jax.random.split(key, 16)
        s = 0.02
        return {'x': jax.random.normal(ks[0], (B, L, D), jnp.float32), 'down_w': jax.random.normal(ks[1], (D, d), jnp.float32) * s, 'down_b': jnp.zeros((d,), jnp.float32), 'up_w': jax.random.normal(ks[2], (d, D), jnp.float32) * s, 'up_b': jnp.zeros((D,), jnp.float32), 'wq': jax.random.normal(ks[3], (d, d), jnp.float32) * s, 'wk': jax.random.normal(ks[4], (d, d), jnp.float32) * s, 'wv': jax.random.normal(ks[5], (d, d), jnp.float32) * s, 'wo': jax.random.normal(ks[6], (d, d), jnp.float32) * s, 'W1': jax.random.normal(ks[7], (H, f, f), jnp.float32) * s, 'b1': jnp.zeros((H, 1, f), jnp.float32), 'ttt_ln_w': jnp.ones((H, f), jnp.float32), 'ttt_ln_b': jnp.zeros((H, f), jnp.float32), 'lr_w': jax.random.normal(ks[8], (H, 1, d), jnp.float32) * s, 'lr_b': jnp.zeros((H,), jnp.float32), 'tok_idx': jnp.zeros((K,), jnp.float32), 'post_w': jnp.ones((d,), jnp.float32), 'post_b': jnp.zeros((d,), jnp.float32), 'ln_w': jnp.ones((d,), jnp.float32), 'ln_b': jnp.zeros((d,), jnp.float32)}
    _L0_attn_in = _L0_attn_setup()

    def _L0_ffn_setup():
        import jax, jax.numpy as jnp
        import numpy as np
        B, S, DIM = (4, 512, 128)
        BASE_COUPLING = 0.1
        NUM_CYCLES = 3

        def _gelu(x):
            return jax.nn.gelu(x, approximate=False)

        def _coupling_net(h, w1, b1, w2, b2, w3, b3, w4, b4):
            h = _gelu(h @ w1 + b1)
            h = _gelu(h @ w2 + b2)
            h = _gelu(h @ w3 + b3)
            return jax.nn.sigmoid(h @ w4 + b4)

        def _global_net(h, w1, b1, w2, b2, w3, b3):
            h = _gelu(h @ w1 + b1)
            h = _gelu(h @ w2 + b2)
            return jax.nn.sigmoid(h @ w3 + b3)

        def _twist(x):
            o_r, o_i, p_r, p_i = jnp.split(x, 4, axis=-1)
            return jnp.concatenate([p_r, -p_i, -o_r, o_i], axis=-1)
        key = jax.random.key(seed)
        ks = jax.random.split(key, 9)
        d = DIM

        def w(k, fan_in, fan_out):
            return jax.random.normal(k, (fan_in, fan_out), dtype=jnp.float32) / np.sqrt(fan_in).astype(np.float32)
        inp = {'x': jax.random.normal(ks[0], (B, S, d), dtype=jnp.float32)}
        cn_dims = [(d, d), (d, d // 2), (d // 2, d // 4), (d // 4, 1)]
        for i, (a, b) in enumerate(cn_dims):
            inp[f'cn_w{i + 1}'] = w(ks[1 + i], a, b)
            inp[f'cn_b{i + 1}'] = jnp.zeros((b,), dtype=jnp.float32)
        gc_dims = [(d, d // 2), (d // 2, d // 4), (d // 4, 1)]
        for i, (a, b) in enumerate(gc_dims):
            inp[f'gc_w{i + 1}'] = w(ks[5 + i], a, b)
            inp[f'gc_b{i + 1}'] = jnp.zeros((b,), dtype=jnp.float32)
        inp['adaptive_range'] = jnp.full((1,), 0.2, dtype=jnp.float32)
        return inp
    _L0_ffn_in = _L0_ffn_setup()

    def _L1_attn_setup():
        import jax, jax.numpy as jnp
        import numpy as np
        D_MODEL = 128
        HIDDEN = 256
        D_STATE = 16
        KERN = 3
        BATCH = 2
        SEQ = 256

        def _layernorm(x, g, b, eps=1e-05):
            m = jnp.mean(x, axis=-1, keepdims=True)
            v = jnp.var(x, axis=-1, keepdims=True)
            return (x - m) * jax.lax.rsqrt(v + eps) * g + b
        key = jax.random.key(seed)
        ks = jax.random.split(key, 10)
        w_scale = 0.02
        return {'x': jax.random.normal(ks[0], (BATCH, SEQ, D_MODEL), jnp.float32), 'W_x': jax.random.normal(ks[1], (HIDDEN, D_MODEL), jnp.float32) * w_scale, 'b_x': jnp.zeros((HIDDEN,), jnp.float32), 'W_g': jax.random.normal(ks[2], (HIDDEN, D_MODEL), jnp.float32) * w_scale, 'b_g': jnp.zeros((HIDDEN,), jnp.float32), 'conv_w': jax.random.normal(ks[3], (HIDDEN, 1, KERN), jnp.float32) * 0.3, 'conv_b': jnp.zeros((HIDDEN,), jnp.float32), 'A_raw': jax.random.normal(ks[4], (HIDDEN, D_STATE), jnp.float32), 'B_ssm': jax.random.normal(ks[5], (HIDDEN, D_STATE), jnp.float32), 'C_ssm': jax.random.normal(ks[6], (HIDDEN, D_STATE), jnp.float32), 'W_dt': jax.random.normal(ks[7], (HIDDEN, D_MODEL), jnp.float32) * w_scale, 'b_dt': jnp.zeros((HIDDEN,), jnp.float32), 'W_out': jax.random.normal(ks[8], (D_MODEL, HIDDEN), jnp.float32) * w_scale, 'b_out': jnp.zeros((D_MODEL,), jnp.float32), 'ln_g': jnp.ones((D_MODEL,), jnp.float32), 'ln_b': jnp.zeros((D_MODEL,), jnp.float32)}
    _L1_attn_in = _L1_attn_setup()

    def _L1_ffn_setup():
        import jax, jax.numpy as jnp
        import numpy as np
        NUM_EXPERTS = 8
        TOP_K = 2
        D_MODEL = 128
        EXPERT_CAP = 64
        B, S = (4, 256)
        key = jax.random.key(seed)
        ks = jax.random.split(key, 4)
        scale = 1.0 / np.sqrt(D_MODEL)
        x = jax.random.normal(ks[0], (B, S, D_MODEL), dtype=jnp.float32)
        gate_w = jax.random.normal(ks[1], (D_MODEL, NUM_EXPERTS), dtype=jnp.float32) * scale
        w1 = jax.random.normal(ks[2], (NUM_EXPERTS, D_MODEL, EXPERT_CAP), dtype=jnp.float32) * scale
        b1 = jnp.zeros((NUM_EXPERTS, EXPERT_CAP), dtype=jnp.float32)
        w2 = jax.random.normal(ks[3], (NUM_EXPERTS, EXPERT_CAP, D_MODEL), dtype=jnp.float32) * (1.0 / np.sqrt(EXPERT_CAP))
        b2 = jnp.zeros((NUM_EXPERTS, D_MODEL), dtype=jnp.float32)
        return {'x': x, 'gate_w': gate_w, 'w1': w1, 'b1': b1, 'w2': w2, 'b2': b2}
    _L1_ffn_in = _L1_ffn_setup()
    _d = {'L0_attn_x': _L0_attn_in['x'], 'L0_attn_down_w': _L0_attn_in['down_w'], 'L0_attn_down_b': _L0_attn_in['down_b'], 'L0_attn_up_w': _L0_attn_in['up_w'], 'L0_attn_up_b': _L0_attn_in['up_b'], 'L0_attn_wq': _L0_attn_in['wq'], 'L0_attn_wk': _L0_attn_in['wk'], 'L0_attn_wv': _L0_attn_in['wv'], 'L0_attn_wo': _L0_attn_in['wo'], 'L0_attn_W1': _L0_attn_in['W1'], 'L0_attn_b1': _L0_attn_in['b1'], 'L0_attn_ttt_ln_w': _L0_attn_in['ttt_ln_w'], 'L0_attn_ttt_ln_b': _L0_attn_in['ttt_ln_b'], 'L0_attn_lr_w': _L0_attn_in['lr_w'], 'L0_attn_lr_b': _L0_attn_in['lr_b'], 'L0_attn_tok_idx': _L0_attn_in['tok_idx'], 'L0_attn_post_w': _L0_attn_in['post_w'], 'L0_attn_post_b': _L0_attn_in['post_b'], 'L0_attn_ln_w': _L0_attn_in['ln_w'], 'L0_attn_ln_b': _L0_attn_in['ln_b'], 'L0_ffn_cn_w1': _L0_ffn_in['cn_w1'], 'L0_ffn_cn_b1': _L0_ffn_in['cn_b1'], 'L0_ffn_cn_w2': _L0_ffn_in['cn_w2'], 'L0_ffn_cn_b2': _L0_ffn_in['cn_b2'], 'L0_ffn_cn_w3': _L0_ffn_in['cn_w3'], 'L0_ffn_cn_b3': _L0_ffn_in['cn_b3'], 'L0_ffn_cn_w4': _L0_ffn_in['cn_w4'], 'L0_ffn_cn_b4': _L0_ffn_in['cn_b4'], 'L0_ffn_gc_w1': _L0_ffn_in['gc_w1'], 'L0_ffn_gc_b1': _L0_ffn_in['gc_b1'], 'L0_ffn_gc_w2': _L0_ffn_in['gc_w2'], 'L0_ffn_gc_b2': _L0_ffn_in['gc_b2'], 'L0_ffn_gc_w3': _L0_ffn_in['gc_w3'], 'L0_ffn_gc_b3': _L0_ffn_in['gc_b3'], 'L0_ffn_adaptive_range': _L0_ffn_in['adaptive_range'], 'L1_attn_W_x': _L1_attn_in['W_x'], 'L1_attn_b_x': _L1_attn_in['b_x'], 'L1_attn_W_g': _L1_attn_in['W_g'], 'L1_attn_b_g': _L1_attn_in['b_g'], 'L1_attn_conv_w': _L1_attn_in['conv_w'], 'L1_attn_conv_b': _L1_attn_in['conv_b'], 'L1_attn_A_raw': _L1_attn_in['A_raw'], 'L1_attn_B_ssm': _L1_attn_in['B_ssm'], 'L1_attn_C_ssm': _L1_attn_in['C_ssm'], 'L1_attn_W_dt': _L1_attn_in['W_dt'], 'L1_attn_b_dt': _L1_attn_in['b_dt'], 'L1_attn_W_out': _L1_attn_in['W_out'], 'L1_attn_b_out': _L1_attn_in['b_out'], 'L1_attn_ln_g': _L1_attn_in['ln_g'], 'L1_attn_ln_b': _L1_attn_in['ln_b'], 'L1_ffn_gate_w': _L1_ffn_in['gate_w'], 'L1_ffn_w1': _L1_ffn_in['w1'], 'L1_ffn_b1': _L1_ffn_in['b1'], 'L1_ffn_w2': _L1_ffn_in['w2'], 'L1_ffn_b2': _L1_ffn_in['b2']}
    _x0 = _d['L0_attn_x']
    _d['L0_attn_x'] = jax.random.normal(jax.random.fold_in(jax.random.key(seed), 1), (4, 512, 128), dtype=_x0.dtype)
    del _x0
    return _d

def reference(L0_attn_x, L0_attn_down_w, L0_attn_down_b, L0_attn_up_w, L0_attn_up_b, L0_attn_wq, L0_attn_wk, L0_attn_wv, L0_attn_wo, L0_attn_W1, L0_attn_b1, L0_attn_ttt_ln_w, L0_attn_ttt_ln_b, L0_attn_lr_w, L0_attn_lr_b, L0_attn_tok_idx, L0_attn_post_w, L0_attn_post_b, L0_attn_ln_w, L0_attn_ln_b, L0_ffn_cn_w1, L0_ffn_cn_b1, L0_ffn_cn_w2, L0_ffn_cn_b2, L0_ffn_cn_w3, L0_ffn_cn_b3, L0_ffn_cn_w4, L0_ffn_cn_b4, L0_ffn_gc_w1, L0_ffn_gc_b1, L0_ffn_gc_w2, L0_ffn_gc_b2, L0_ffn_gc_w3, L0_ffn_gc_b3, L0_ffn_adaptive_range, L1_attn_W_x, L1_attn_b_x, L1_attn_W_g, L1_attn_b_g, L1_attn_conv_w, L1_attn_conv_b, L1_attn_A_raw, L1_attn_B_ssm, L1_attn_C_ssm, L1_attn_W_dt, L1_attn_b_dt, L1_attn_W_out, L1_attn_b_out, L1_attn_ln_g, L1_attn_ln_b, L1_ffn_gate_w, L1_ffn_w1, L1_ffn_b1, L1_ffn_w2, L1_ffn_b2):

    def _L0_attn_ref(x, down_w, down_b, up_w, up_b, wq, wk, wv, wo, W1, b1, ttt_ln_w, ttt_ln_b, lr_w, lr_b, tok_idx, post_w, post_b, ln_w, ln_b):
        import jax, jax.numpy as jnp
        import numpy as np
        B, L, D = (8, 512, 128)
        H, f, K = (2, 128, 16)
        d = H * f
        TTT_BASE_LR = 1.0

        def _ln(x, g, b, eps=1e-06):
            mu = x.mean(-1, keepdims=True)
            var = ((x - mu) ** 2).mean(-1, keepdims=True)
            return g * (x - mu) * jax.lax.rsqrt(var + eps) + b

        def _ln_fused_l2_bwd(x, target, g, b, eps=1e-06):
            Dh = x.shape[-1]
            mu = x.mean(-1, keepdims=True)
            var = ((x - mu) ** 2).mean(-1, keepdims=True)
            std = jnp.sqrt(var + eps)
            xh = (x - mu) / std
            gy = (g * xh + b - target) * g
            return (Dh * gy - gy.sum(-1, keepdims=True) - xh * (gy * xh).sum(-1, keepdims=True)) / (Dh * std)

        def _ttt_linear(h, wq, wk, wv, wo, W1, b1, ttt_ln_w, ttt_ln_b, lr_w, lr_b, tok_idx, post_w, post_b):
            Bb, Ll, dm = h.shape
            nm = Ll // K

            def heads(w):
                return (h @ w).reshape(Bb, nm, K, H, f).transpose(0, 3, 1, 2, 4)
            XQ, XK, XV = (heads(wq), heads(wk), heads(wv))
            Xm = h.reshape(Bb, nm, K, dm)
            ttt_lr = jax.nn.sigmoid(jnp.einsum('bnkc,hoc->bhnko', Xm, lr_w) + lr_b[None, :, None, None, None])
            ttt_lr_eta = TTT_BASE_LR * ttt_lr.transpose(0, 1, 2, 4, 3) / f
            token_idx = jnp.maximum(1.0 / jnp.arange(1, K + 1, dtype=jnp.float32) + tok_idx, 0.0)
            eta = token_idx[None, None, None, :, None] * ttt_lr_eta
            gw = ttt_ln_w[:, None, :]
            gb = ttt_ln_b[:, None, :]

            def step(carry, inp):
                W1c, b1c = carry
                xq, xk, xv, et = inp
                Z1 = xk @ W1c + b1c
                grad = _ln_fused_l2_bwd(Z1, xv - xk, gw, gb)
                Attn = jnp.tril(xq @ jnp.swapaxes(xk, -1, -2))
                b1_bar = b1c - jnp.tril(et) @ grad
                Z1_bar = xq @ W1c - et * Attn @ grad + b1_bar
                last_eta = et[:, :, -1, :, None]
                W1n = W1c - jnp.swapaxes(last_eta * xk, -1, -2) @ grad
                b1n = b1c - (last_eta * grad).sum(-2, keepdims=True)
                return ((W1n, b1n), xq + _ln(Z1_bar, gw, gb))
            carry0 = (jnp.broadcast_to(W1[None], (Bb, H, f, f)), jnp.broadcast_to(b1[None], (Bb, H, 1, f)))
            xs = tuple((a.transpose(2, 0, 1, 3, 4) for a in (XQ, XK, XV, eta)))
            _, outs = jax.lax.scan(step, carry0, xs)
            out = outs.transpose(1, 0, 3, 2, 4).reshape(Bb, Ll, dm)
            out = _ln(out, post_w, post_b, eps=1e-05)
            return out @ wo
        h = jax.nn.silu(x @ down_w + down_b)
        h = _ttt_linear(h, wq, wk, wv, wo, W1, b1, ttt_ln_w, ttt_ln_b, lr_w, lr_b, tok_idx, post_w, post_b)
        h = _ln(h, ln_w, ln_b, eps=1e-05)
        return h @ up_w + up_b

    def _L0_ffn_ref(x, cn_w1, cn_b1, cn_w2, cn_b2, cn_w3, cn_b3, cn_w4, cn_b4, gc_w1, gc_b1, gc_w2, gc_b2, gc_w3, gc_b3, adaptive_range):
        import jax, jax.numpy as jnp
        import numpy as np
        B, S, DIM = (4, 512, 128)
        BASE_COUPLING = 0.1
        NUM_CYCLES = 3

        def _gelu(x):
            return jax.nn.gelu(x, approximate=False)

        def _coupling_net(h, w1, b1, w2, b2, w3, b3, w4, b4):
            h = _gelu(h @ w1 + b1)
            h = _gelu(h @ w2 + b2)
            h = _gelu(h @ w3 + b3)
            return jax.nn.sigmoid(h @ w4 + b4)

        def _global_net(h, w1, b1, w2, b2, w3, b3):
            h = _gelu(h @ w1 + b1)
            h = _gelu(h @ w2 + b2)
            return jax.nn.sigmoid(h @ w3 + b3)

        def _twist(x):
            o_r, o_i, p_r, p_i = jnp.split(x, 4, axis=-1)
            return jnp.concatenate([p_r, -p_i, -o_r, o_i], axis=-1)
        global_context = x.mean(axis=1, keepdims=True)
        gf = _global_net(global_context, gc_w1, gc_b1, gc_w2, gc_b2, gc_w3, gc_b3)
        out = x
        for _ in range(NUM_CYCLES):
            tf = _coupling_net(out, cn_w1, cn_b1, cn_w2, cn_b2, cn_w3, cn_b3, cn_w4, cn_b4)
            combined = 0.7 * gf + 0.3 * tf
            coupling = BASE_COUPLING + adaptive_range * (combined - 0.5) * 2.0
            out = out + coupling * _twist(out)
        return out

    def _L1_attn_ref(x, W_x, b_x, W_g, b_g, conv_w, conv_b, A_raw, B_ssm, C_ssm, W_dt, b_dt, W_out, b_out, ln_g, ln_b):
        import jax, jax.numpy as jnp
        import numpy as np
        D_MODEL = 128
        HIDDEN = 256
        D_STATE = 16
        KERN = 3
        BATCH = 2
        SEQ = 256

        def _layernorm(x, g, b, eps=1e-05):
            m = jnp.mean(x, axis=-1, keepdims=True)
            v = jnp.var(x, axis=-1, keepdims=True)
            return (x - m) * jax.lax.rsqrt(v + eps) * g + b
        u = jnp.einsum('bld,hd->blh', x, W_x) + b_x
        g = jax.nn.sigmoid(jnp.einsum('bld,hd->blh', x, W_g) + b_g)
        pad = conv_w.shape[-1] // 2
        h = jax.lax.conv_general_dilated(jnp.transpose(u, (0, 2, 1)), conv_w, window_strides=(1,), padding=[(pad, pad)], feature_group_count=conv_w.shape[0], dimension_numbers=('NCH', 'OIH', 'NCH')) + conv_b[None, :, None]
        h = jnp.transpose(h, (0, 2, 1))
        u = u * g + h * (1.0 - g)
        dt = jax.nn.softplus(jnp.einsum('bld,hd->blh', x, W_dt) + b_dt).mean(axis=(0, 1))
        dt = jnp.clip(dt, 0.001, 2.0)
        A = -jax.nn.softplus(A_raw)
        A_d = jnp.exp(A * dt[:, None])
        B_d = (A_d - 1.0) / (A + 1e-06) * B_ssm
        Bsz, L, H = u.shape
        S = A_d.shape[1]

        def step(carry, u_t):
            new = A_d[None] * carry + B_d[None] * u_t[:, :, None]
            y_t = jnp.einsum('bhs,hs->bh', new, C_ssm)
            return (new, y_t)
        init = jnp.zeros((Bsz, H, S), dtype=u.dtype)
        _, ys = jax.lax.scan(step, init, jnp.transpose(u, (1, 0, 2)))
        y = jnp.transpose(ys, (1, 0, 2))
        out = jnp.einsum('blh,dh->bld', y, W_out) + b_out
        return _layernorm(x + out, ln_g, ln_b)

    def _L1_ffn_ref(x, gate_w, w1, b1, w2, b2):
        import jax, jax.numpy as jnp
        import numpy as np
        NUM_EXPERTS = 8
        TOP_K = 2
        D_MODEL = 128
        EXPERT_CAP = 64
        B, S = (4, 256)
        Bx, Sx, D = x.shape
        xt = x.reshape(-1, D)
        gates = jax.nn.softmax(xt @ gate_w, axis=-1)
        topk_g, topk_i = jax.lax.top_k(gates, TOP_K)
        tok_w = topk_g.sum(axis=-1)
        sel = (topk_i[:, :, None] == jnp.arange(NUM_EXPERTS)[None, None, :]).any(axis=1)
        h = jax.nn.gelu(jnp.einsum('nd,edh->enh', xt, w1) + b1[:, None, :], approximate=False)
        y = jnp.einsum('enh,ehd->end', h, w2) + b2[:, None, :]
        out = jnp.einsum('end,ne,n->nd', y, sel.astype(x.dtype), tok_w)
        return out.reshape(Bx, Sx, D)
    x = L0_attn_x
    xn = _layernorm(x, axis=-1)
    x = x + _L0_attn_ref(xn, L0_attn_down_w, L0_attn_down_b, L0_attn_up_w, L0_attn_up_b, L0_attn_wq, L0_attn_wk, L0_attn_wv, L0_attn_wo, L0_attn_W1, L0_attn_b1, L0_attn_ttt_ln_w, L0_attn_ttt_ln_b, L0_attn_lr_w, L0_attn_lr_b, L0_attn_tok_idx, L0_attn_post_w, L0_attn_post_b, L0_attn_ln_w, L0_attn_ln_b) + _L0_ffn_ref(xn, L0_ffn_cn_w1, L0_ffn_cn_b1, L0_ffn_cn_w2, L0_ffn_cn_b2, L0_ffn_cn_w3, L0_ffn_cn_b3, L0_ffn_cn_w4, L0_ffn_cn_b4, L0_ffn_gc_w1, L0_ffn_gc_b1, L0_ffn_gc_w2, L0_ffn_gc_b2, L0_ffn_gc_w3, L0_ffn_gc_b3, L0_ffn_adaptive_range)
    xn = _layernorm(x, axis=-1)
    x = x + _L1_attn_ref(xn, L1_attn_W_x, L1_attn_b_x, L1_attn_W_g, L1_attn_b_g, L1_attn_conv_w, L1_attn_conv_b, L1_attn_A_raw, L1_attn_B_ssm, L1_attn_C_ssm, L1_attn_W_dt, L1_attn_b_dt, L1_attn_W_out, L1_attn_b_out, L1_attn_ln_g, L1_attn_ln_b) + _L1_ffn_ref(xn, L1_ffn_gate_w, L1_ffn_w1, L1_ffn_b1, L1_ffn_w2, L1_ffn_b2)
    return x

_drawn_inputs = setup_inputs


def setup_inputs(seed=0):
    import zlib

    import numpy as np

    out = dict(_drawn_inputs(seed))
    spreads = {'L0_attn_down_b': (0.0, 0.1),
     'L0_attn_up_b': (0.0, 0.1),
     'L0_attn_b1': (0.0, 0.1),
     'L0_attn_ttt_ln_w': (1.0, 0.2),
     'L0_attn_ttt_ln_b': (0.0, 0.1),
     'L0_attn_lr_b': (0.0, 0.619),
     'L0_attn_tok_idx': (0.0, 0.1),
     'L0_attn_post_w': (1.0, 0.2),
     'L0_attn_post_b': (0.0, 0.27),
     'L0_attn_ln_w': (1.0, 0.2),
     'L0_attn_ln_b': (0.0, 0.31),
     'L0_ffn_cn_b1': (0.0, 0.8),
     'L0_ffn_cn_b2': (0.0, 2.0),
     'L0_ffn_cn_b3': (0.0, 2.0),
     'L0_ffn_gc_b1': (0.0, 0.8),
     'L0_ffn_gc_b2': (0.0, 2.0),
     'L1_attn_b_x': (0.0, 0.1),
     'L1_attn_b_g': (0.0, 2.0),
     'L1_attn_conv_b': (0.0, 0.1),
     'L1_attn_b_dt': (0.0, 2.0),
     'L1_attn_b_out': (0.0, 0.271),
     'L1_attn_ln_g': (1.0, 0.2),
     'L1_attn_ln_b': (0.0, 0.1),
     'L1_ffn_b1': (0.0, 0.438),
     'L1_ffn_b2': (0.0, 0.286)}
    factors = {'L0_attn_wk': 2.718,
     'L0_attn_wv': 2.9,
     'L0_attn_lr_w': 43.291,
     'L0_ffn_cn_w1': 4.453,
     'L0_ffn_cn_w2': 4.321,
     'L0_ffn_cn_w3': 4.164,
     'L0_ffn_cn_w4': 2.778,
     'L0_ffn_gc_w1': 64.0,
     'L0_ffn_gc_w2': 49.464,
     'L0_ffn_gc_w3': 8.0,
     'L1_attn_W_g': 8.0,
     'L1_attn_W_dt': 64.0}
    for name, (base, spread) in spreads.items():
        noise = np.random.default_rng([zlib.crc32(name.encode()), seed]).standard_normal(out[name].shape)
        drawn = base * np.exp(spread * noise) if base else spread * noise
        out[name] = jnp.asarray(drawn.astype(out[name].dtype))
    for name, factor in factors.items():
        out[name] = (out[name] * factor).astype(out[name].dtype)
    return out
```

```python
from contextlib import ExitStack

import concourse.bass as bass
import numpy as np
from concourse import mybir

F32 = mybir.dt.float32
U32 = mybir.dt.uint32
ACT = mybir.ActivationFunctionType
ALU = mybir.AluOpType
AX = mybir.AxisListType.X

P = 128
B, L, D = 4, 512, 128
TOK = B * L
NT = TOK // P
TPB = L // P
H, F, K = 2, 128, 16
HD = H * F
STEPS = L // K
RC = 3 * F + 1
BW = 3 * K
NG = 32
TC = 32
NCH = L // TC
NS = 16
NE = 8
EH = 64

CONSTS = [("ident", P), ("twist", P), ("tri", P), ("blk", P), ("inv", P), ("head", 2), ("expo", 1),
          ("ramp1", TC), ("ramp0", TC), ("mask4", 4), ("iota8", NE), ("pick", 4 * P), ("ones", P),
          ("eps6", 1), ("eps5", 1), ("quad", 4), ("headT", P)]


def constant_columns():
    at, n = {}, 0
    for name, width in CONSTS:
        at[name] = (n, n + width)
        n += width
    return at, n


def constants():
    at, n = constant_columns()
    c = np.zeros((P, n), np.float32)
    p, q = np.arange(P)[:, None], np.arange(P)[None, :]

    def put(name, v):
        a, b = at[name]
        c[:, a:b] = v

    same = (p // K) == (q // K)
    put("ident", p == q)
    tw = np.zeros((P, P))
    for dst, src, sign in ((0, 2, 1), (1, 3, -1), (2, 0, -1), (3, 1, 1)):
        for i in range(32):
            tw[32 * src + i, 32 * dst + i] = sign
    put("twist", tw)
    put("tri", same & (p <= q))
    put("blk", same)
    put("inv", 1.0 / (q % K + 1) + 0.0 * p)
    put("head", (p // K) % H == np.arange(H)[None, :])
    put("expo", TC - 1 - p % TC)
    put("ramp1", np.arange(1, TC + 1)[None, :] + 0.0 * p)
    put("ramp0", np.arange(TC)[None, :] + 0.0 * p)
    put("mask4", (p // NS) % 4 == np.arange(4)[None, :])
    put("iota8", np.arange(NE)[None, :] + 0.0 * p)
    pick = np.zeros((P, 4, P))
    for e in range(NE):
        pick[e, e // 2, EH * (e % 2):EH * (e % 2) + EH] = 1
    put("pick", pick.reshape(P, -1))
    put("ones", 1.0)
    put("eps6", 1e-6)
    put("eps5", 1e-5)
    put("quad", p // 32 == np.arange(4)[None, :])
    put("headT", (q // K) % H == p)
    return c


class Chain:

    def __init__(self, eng, sem):
        self.eng, self.sem, self.n = eng, sem, 0

    def mark(self, ins):
        self.n += 1
        ins.then_inc(self.sem, 1)

    def link(self, ins):
        self.mark(ins)
        self.eng.wait_ge(self.sem, self.n)


def build(nc, a, const, out):
    ctx = ExitStack()
    with ctx, nc.allow_non_contiguous_dma(reason="bias columns and token regrouping"):
        at, ncol = constant_columns()
        taken = set()

        def unique(name):
            while name in taken:
                name += "_"
            taken.add(name)
            return name

        def sb(name, shape, dt=F32, c=ctx):
            return c.enter_context(nc.sbuf_tensor(unique(name), shape, dt))

        def sem(name, c=ctx):
            return c.enter_context(nc.semaphore(unique(name)))

        bank = [ctx.enter_context(nc.psum_tensor(f"bank{i}", [P, 512], F32)) for i in range(8)]
        cst = sb("cst", [P, ncol])

        def con(name, rows=P):
            lo, hi = at[name]
            return cst[0:rows, lo:hi]

        rows_d = nc.dram_tensor("rows_scratch", (STEPS, B, H, K, RC + 3), F32).ap()
        attn_d = nc.dram_tensor("attn_scratch", (STEPS, B, H, K, F), F32).ap()

        xt = sb("xt", [P, NT, D])
        ffnT = sb("ffnT", [P, TOK])
        wo = sb("wo", [P, 2, HD])
        wo_bias = sb("wo_bias", [1, HD])
        up = sb("up", [P, 2, D])
        up_bias = sb("up_bias", [1, D])
        lna_d = nc.dram_tensor("lna_scratch", (HD, NS), F32).ap()

        with ExitStack() as late:
            layer0_in(nc, a, const, out, locals())
            ttt(nc, a, locals())
        xn1, xn1T = sb("xn1", [P, NT, D]), sb("xn1T", [P, TOK])
        layer0_out(nc, a, locals())
        layer1(nc, a, out, locals())
    return nc


def layer0_in(nc, a, const, out, g):
    sb, sem, con, bank = g["sb"], g["sem"], g["con"], g["bank"]
    cst, xt, ffnT, rows_d = g["cst"], g["xt"], g["ffnT"], g["rows_d"]
    wo, wo_bias, up, up_bias = g["wo"], g["wo_bias"], g["up"], g["up_bias"]
    with ExitStack() as c:
        xnT = sb("xnT", [P, TOK], c=c)
        hT = sb("hT", [P, 2, TOK], c=c)
        xn = sb("xn", [P, NT, D], c=c)
        down = sb("down", [P, HD], c=c)
        down_b = sb("down_b", [P, 2], c=c)
        w4 = sb("w4", [P, 2, H, RC], c=c)
        wv = sb("wv", [P, 2, HD], c=c)
        lrb = sb("lrb", [P, H], c=c)
        post_w, post_b = sb("post_w", [P, 2], c=c), sb("post_b", [P, 2], c=c)
        ln_w, ln_b = sb("ln_w", [P, 2], c=c), sb("ln_b", [P, 2], c=c)
        wo_raw, up_raw = sb("wo_raw", [P, 2, HD], c=c), sb("up_raw", [P, 2, D], c=c)
        upb_raw = sb("upb_raw", [1, D], c=c)
        cw1, cw2 = sb("cw1", [P, 128], c=c), sb("cw2", [P, 64], c=c)
        cw3, cw4 = sb("cw3", [64, 32], c=c), sb("cw4", [32, 1], c=c)
        cw4r = sb("cw4r", [32, P], c=c)
        cb1, cb2, cb3 = sb("cb1", [P, 1], c=c), sb("cb2", [64, 1], c=c), sb("cb3", [32, 1], c=c)
        cb4, gb3 = sb("cb4", [P, 1], c=c), sb("gb3", [P, 1], c=c)
        gw1, gw2, gw3 = sb("gw1", [P, 64], c=c), sb("gw2", [64, 32], c=c), sb("gw3", [32, 1], c=c)
        gw3r = sb("gw3r", [32, P], c=c)
        gb1, gb2 = sb("gb1", [64, 1], c=c), sb("gb2", [32, 1], c=c)
        arange = sb("arange", [P, 1], c=c)
        half_b4, half_gb3 = sb("half_b4", [P, 1], c=c), sb("half_gb3", [P, 1], c=c)
        stats, mv = sb("stats", [P, NT, 6], c=c), sb("mv", [P, NT, 2], c=c)
        std, rstd = sb("std", [P, NT], c=c), sb("rstd", [P, NT], c=c)

        x_in = [sem(f"x_in{b}", c) for b in range(B)]
        w_in = sem("w_in", c)
        stats_done, std_done, xn_done = sem("stats_done", c), sem("std_done", c), sem("xn_done", c)
        xnT_mm, xnT_done = sem("xnT_mm", c), sem("xnT_done", c)
        v_chain = sem("v_chain", c)
        bias_mm = sem("bias_mm", c)
        weights_ready = sem("weights_ready", c)
        loads = []

        def load(eng, dst, src):
            eng.dma_start(dst, src).then_inc(w_in, 16)
            loads.append(1)

        col = lambda v, n: v.rearrange("(k p) -> p k", k=n)
        with nc.Block() as block:
            @block.sync
            def _(sp):
                for b in range(B):
                    sp.dma_start(xt[:, b * TPB:(b + 1) * TPB, :],
                                 a["L0_attn_x"][b].rearrange("(n p) d -> p n d", p=P)).then_inc(x_in[b], 16)
                sp.dma_start(cst[:], const).then_inc(w_in, 16)
                loads.append(1)
                for h in range(H):
                    hs = slice(h * F, h * F + F)
                    load(sp, w4[:, :, h, 0:F], a["L0_attn_wk"][:, hs].rearrange("(k p) f -> p k f", k=2))
                    load(sp, w4[:, :, h, 2 * F:3 * F], a["L0_attn_wq"][:, hs].rearrange("(k p) f -> p k f", k=2))
                    load(sp, w4[:, :, h, 3 * F], col(a["L0_attn_lr_w"][h, 0], 2))
                load(sp, wv[:], a["L0_attn_wv"].rearrange("(k p) f -> p k f", k=2))
                load(sp, lrb[:], a["L0_attn_lr_b"].partition_broadcast(P))
                for dst, name in ((down_b, "down_b"), (post_w, "post_w"), (post_b, "post_b"), (ln_w, "ln_w"), (ln_b, "ln_b")):
                    load(sp, dst[:], col(a["L0_attn_" + name], 2))
                load(sp, upb_raw[:], a["L0_attn_up_b"].rearrange("(o d) -> o d", o=1))

            @block.scalar
            def _(act):
                load(act, down[:], a["L0_attn_down_w"])
                load(act, wo_raw[:], a["L0_attn_wo"].rearrange("(k p) f -> p k f", k=2))
                load(act, up_raw[:], a["L0_attn_up_w"].rearrange("(k p) f -> p k f", k=2))
                for dst, name in ((cw1, "cn_w1"), (cw2, "cn_w2"), (cw3, "cn_w3"), (cw4, "cn_w4"),
                                  (gw1, "gc_w1"), (gw2, "gc_w2"), (gw3, "gc_w3")):
                    load(act, dst[:], a["L0_ffn_" + name])
                for dst, name in ((cb1, "cn_b1"), (cb2, "cn_b2"), (cb3, "cn_b3"), (gb1, "gc_b1"), (gb2, "gc_b2")):
                    load(act, dst[:], a["L0_ffn_" + name].rearrange("(p o) -> p o", o=1))
                for dst, name in ((cb4, "cn_b4"), (gb3, "gc_b3"), (arange, "adaptive_range")):
                    load(act, dst[:], a["L0_ffn_" + name].partition_broadcast(P))
                act.wait_ge(w_in, 16 * len(loads))
                for b in range(B):
                    act.wait_ge(stats_done, b + 1)
                    s = slice(b * TPB, (b + 1) * TPB)
                    act.activation(std[:, s], mv[:, s, 1], ACT.Sqrt, bias=con("eps5")).then_inc(std_done, 1)

            @block.vector
            def _(dve):
                ch = Chain(dve, v_chain)
                for b in range(B):
                    dve.wait_ge(x_in[b], 16)
                    for i in range(b * TPB, (b + 1) * TPB):
                        ch.mark(nc.vector.bn_stats(stats[:, i, :], xt[:, i, :]))
                    dve.wait_ge(v_chain, ch.n)
                    for i in range(b * TPB, (b + 1) * TPB):
                        last = nc.vector.bn_aggr(mv[:, i, :], stats[:, i, :])
                        if i == (b + 1) * TPB - 1:
                            last.then_inc(stats_done, 1)
                        else:
                            ch.mark(last)
                    dve.wait_ge(stats_done, b + 1)
                for b in range(B):
                    s = slice(b * TPB, (b + 1) * TPB)
                    dve.wait_ge(std_done, b + 1)
                    ch.link(nc.vector.reciprocal(rstd[:, s], std[:, s]))
                    for i in range(b * TPB, (b + 1) * TPB):
                        nc.vector.tensor_scalar(xn[:, i, :], xt[:, i, :], mv[:, i, 0:1], rstd[:, i:i + 1],
                                                ALU.subtract, ALU.mult).then_inc(xn_done, 1)
                dve.wait_ge(w_in, 16 * len(loads))
                for h in range(H):
                    ch.mark(nc.vector.tensor_tensor(w4[:, :, h, F:2 * F], w4[:, :, h, 0:F],
                                                    wv[:, :, h * F:h * F + F], ALU.subtract))
                for k in range(2):
                    ch.mark(nc.vector.tensor_scalar(wo[:, k, :], wo_raw[:, k, :], post_w[:, k:k + 1], None, ALU.mult))
                    ch.mark(nc.vector.tensor_scalar(up[:, k, :], up_raw[:, k, :], ln_w[:, k:k + 1], None, ALU.mult))
                ch.mark(nc.vector.tensor_copy(cw4r[:], cw4[:, 0:1].broadcast_to([32, P])))
                ch.mark(nc.vector.tensor_copy(gw3r[:], gw3[:, 0:1].broadcast_to([32, P])))
                ch.mark(nc.vector.tensor_scalar(half_b4[:], cb4[:], 0.5, None, ALU.mult))
                ch.mark(nc.vector.tensor_scalar(half_gb3[:], gb3[:], 0.5, None, ALU.mult))
                dve.wait_ge(bias_mm, 1)
                ch.mark(nc.vector.tensor_copy(wo_bias[:], bank[6][0:1, 0:HD]))
                dve.wait_ge(bias_mm, 2)
                ch.mark(nc.vector.tensor_tensor(up_bias[:], bank[7][0:1, 0:D], upb_raw[:], ALU.add))
                for b in range(B):
                    dve.wait_ge(xnT_mm, b + 1)
                    ch.mark(nc.vector.tensor_copy(xnT[:, b * L:(b + 1) * L], bank[b][:, :]))

            @block.tensor
            def _(pe):
                pe.wait_ge(w_in, 16 * len(loads))
                for k in range(2):
                    mm = nc.tensor.matmul(bank[6][0:1, 0:HD], post_b[:, k:k + 1], wo_raw[:, k, :],
                                          start=(k == 0), stop=(k == 1))
                mm.then_inc(bias_mm, 1)
                for k in range(2):
                    mm = nc.tensor.matmul(bank[7][0:1, 0:D], ln_b[:, k:k + 1], up_raw[:, k, :],
                                          start=(k == 0), stop=(k == 1))
                mm.then_inc(bias_mm, 1)
                for b in range(B):
                    pe.wait_ge(xn_done, TPB * (b + 1))
                    for i in range(TPB):
                        mm = nc.tensor.transpose(bank[b][:, i * P:(i + 1) * P], xn[:, b * TPB + i, :], con("ident"))
                    mm.then_inc(xnT_mm, 1)

        with ExitStack() as c1:
            sig = sb("sig", [P, 2, 512], c=c1)
            stage = sb("stage", [P, 2, H, RC], c=c1)
            down_mm, sig_done, hT_done = sem("down_mm", c1), sem("sig_done", c1), sem("hT_done", c1)
            proj_mm = [sem(f"proj_mm{h}", c1) for h in range(H)]
            lr_done = sem("lr_done", c1)
            stage_done = [sem(f"stage_done{h}", c1) for h in range(H)]
            stored = [sem(f"rows_stored{p}", c1) for p in range(2)]
            with nc.Block() as block:
                @block.tensor
                def _(pe):
                    for n in range(8):
                        t, m = divmod(n, 2)
                        if n >= 4:
                            pe.wait_ge(hT_done, n - 3)
                        nc.tensor.matmul(bank[n % 4][:, :], down[:, m * P:(m + 1) * P], xnT[:, t * 512:(t + 1) * 512],
                                         start=True, stop=True).then_inc(down_mm, 1)
                    for i in range(NT):
                        pe.wait_ge(hT_done, 8 if i // 4 == 3 else 2 * (i // 4) + 2)
                        if i == 0:
                            pe.wait_ge(hT_done, 4)
                        for h in range(H):
                            if i >= 2:
                                pe.wait_ge(stage_done[h], i - 1)
                                pe.wait_ge(lr_done, 2 * (i - 1))
                            for k in range(2):
                                mm = nc.tensor.matmul(bank[4 + 2 * h + i % 2][:, 0:RC], hT[:, k, i * P:(i + 1) * P],
                                                      w4[:, k, h, :], start=(k == 0), stop=(k == 1))
                            mm.then_inc(proj_mm[h], 1)

                @block.scalar
                def _(act):
                    for n in range(8):
                        act.wait_ge(down_mm, n + 1)
                        if n >= 2:
                            act.wait_ge(hT_done, n - 1)
                        act.activation(sig[:, n % 2, :], bank[n % 4][:, :], ACT.Sigmoid,
                                       bias=down_b[:, n % 2:n % 2 + 1]).then_inc(sig_done, 1)
                    for i in range(NT):
                        act.wait_ge(proj_mm[0], i + 1)
                        if i >= 2:
                            act.wait_ge(stored[i % 2], 32 * (i // 2))
                        act.activation(stage[:, i % 2, 0, 0:3 * F], bank[4 + i % 2][:, 0:3 * F],
                                       ACT.Copy).then_inc(stage_done[0], 1)
                        for h in range(H):
                            if h == 1:
                                act.wait_ge(stage_done[1], i + 1)
                            act.activation(stage[:, i % 2, h, 3 * F:RC], bank[4 + 2 * h + i % 2][:, 3 * F:RC],
                                           ACT.Sigmoid, bias=lrb[:, h:h + 1]).then_inc(lr_done, 1)

                @block.vector
                def _(dve):
                    for n in range(8):
                        t, m = divmod(n, 2)
                        dve.wait_ge(sig_done, n + 1)
                        nc.vector.scalar_tensor_tensor(out=hT[:, m, t * 512:(t + 1) * 512], in0=bank[n % 4][:, :],
                                                       scalar=down_b[:, m:m + 1], in1=sig[:, n % 2, :],
                                                       op0=ALU.add, op1=ALU.mult).then_inc(hT_done, 1)
                    for i in range(NT):
                        dve.wait_ge(proj_mm[1], i + 1)
                        if i >= 2:
                            dve.wait_ge(stored[i % 2], 32 * (i // 2))
                        nc.vector.tensor_copy(stage[:, i % 2, 1, 0:3 * F],
                                              bank[6 + i % 2][:, 0:3 * F]).then_inc(stage_done[1], 1)

                @block.sync
                def _(sp):
                    for i in range(NT):
                        b, t0 = i // TPB, (i % TPB) * (P // K)
                        sp.wait_ge(stage_done[0], i + 1)
                        sp.wait_ge(stage_done[1], i + 1)
                        sp.wait_ge(lr_done, 2 * (i + 1))
                        for h in range(H):
                            sp.dma_start(rows_d[t0:t0 + P // K, b, h, :, 0:RC],
                                         stage[:, i % 2, h, :]).then_inc(stored[i % 2], 16)
                    for p in range(2):
                        sp.wait_ge(stored[p], 32 * (NT // 2))

        with ExitStack() as c1:
            N = 512
            h1, h2 = sb("h1", [P, 4, N], c=c1), sb("h2", [64, 4, N], c=c1)
            h3, tanh = sb("h3", [32, 4, N], c=c1), sb("tanh", [P, 4, N], c=c1)
            coup, move = sb("coup", [P, 4, N], c=c1), sb("move", [P, 4, N], c=c1)
            mean = sb("mean", [P, B], c=c1)
            g1, g2, gf = sb("g1", [64, B], c=c1), sb("g2", [32, B], c=c1), sb("gf", [P, B], c=c1)
            beta, alpha, a0 = sb("beta", [P, 1], c=c1), sb("alpha", [P, B], c=c1), sb("a0", [P, 1], c=c1)
            mean_done, gc_mm, gc_act = sem("mean_done", c1), sem("gc_mm", c1), sem("gc_act", c1)
            layer_mm = [sem(f"cn_mm{n}", c1) for n in range(4)]
            layer_act = [sem(f"cn_act{n}", c1) for n in range(4)]
            twist_mm, moved, coupled, upd = sem("twist_mm", c1), sem("moved", c1), sem("coupled", c1), sem("upd", c1)
            vc = sem("vc", c1)
            CYC = 3
            with nc.Block() as block:
                @block.tensor
                def _(pe):
                    pe.wait_ge(mean_done, 1)
                    nc.tensor.matmul(bank[6][0:64, 0:B], gw1[:], mean[:], start=True, stop=True).then_inc(gc_mm, 1)
                    pe.wait_ge(gc_act, 1)
                    nc.tensor.matmul(bank[6][0:32, 0:B], gw2[:], g1[:], start=True, stop=True).then_inc(gc_mm, 1)
                    pe.wait_ge(gc_act, 2)
                    nc.tensor.matmul(bank[6][:, 0:B], gw3r[:], g2[:], start=True, stop=True).then_inc(gc_mm, 1)
                    for cyc in range(CYC):
                        for n in range(4):
                            for b in range(B):
                                j = cyc * B + b
                                src = (xnT if cyc == 0 else ffnT)[:, b * N:(b + 1) * N]
                                if n == 0:
                                    if cyc:
                                        pe.wait_ge(upd, j - B + 1)
                                    rhs, lhs, m = src, cw1[:], 128
                                    if cyc:
                                        pe.wait_ge(layer_act[3], j - B + 1)
                                else:
                                    pe.wait_ge(layer_act[n - 1], j + 1)
                                    rhs = (h1[:, b, :], h2[:, b, :], h3[:, b, :])[n - 1]
                                    lhs, m = ((cw2[:], 64), (cw3[:], 32), (cw4r[:], 128))[n - 1]
                                nc.tensor.matmul(bank[b][0:m, :], lhs, rhs, start=True, stop=True).then_inc(layer_mm[n], 1)
                                if n == 0:
                                    if j == 0:
                                        pe.wait_ge(gc_act, 3)
                                    nc.tensor.matmul(bank[4 + b][:, :], con("twist"), src, start=True, stop=True).then_inc(twist_mm, 1)

                @block.scalar
                def _(act):
                    act.wait_ge(gc_mm, 1)
                    act.activation(g1[:], bank[6][0:64, 0:B], ACT.Gelu, bias=gb1[:]).then_inc(gc_act, 1)
                    act.wait_ge(gc_mm, 2)
                    act.activation(g2[:], bank[6][0:32, 0:B], ACT.Gelu, bias=gb2[:]).then_inc(gc_act, 1)
                    act.wait_ge(gc_mm, 3)
                    act.activation(gf[:], bank[6][:, 0:B], ACT.Tanh, bias=half_gb3[:], scale=0.5).then_inc(gc_act, 1)
                    for cyc in range(CYC):
                        for n in range(4):
                            for b in range(B):
                                j = cyc * B + b
                                act.wait_ge(layer_mm[n], j + 1)
                                dst, bias, m = ((h1, cb1, 128), (h2, cb2, 64), (h3, cb3, 32), (tanh, half_b4, 128))[n]
                                if n == 3 and cyc:
                                    act.wait_ge(coupled, j - B + 1)
                                if n < 3:
                                    act.activation(dst[:, b, :], bank[b][0:m, :], ACT.Gelu, bias=bias[:]).then_inc(layer_act[n], 1)
                                else:
                                    act.activation(dst[:, b, :], bank[b][0:m, :], ACT.Tanh, bias=bias[:],
                                                   scale=0.5).then_inc(layer_act[n], 1)

                @block.vector
                def _(dve):
                    ch = Chain(dve, vc)
                    ch.link(nc.vector.tensor_reduce(mean[:], xnT[:, :].rearrange("p (b l) -> p b l", b=B), AX, ALU.add))
                    nc.vector.tensor_scalar(mean[:], mean[:], 1.0 / L, None, ALU.mult).then_inc(mean_done, 1)
                    ch.mark(nc.vector.tensor_scalar(beta[:], arange[:], 0.3, None, ALU.mult))
                    dve.wait_ge(gc_act, 3)
                    ch.link(nc.vector.tensor_scalar(alpha[:], gf[:], 0.7, None, ALU.mult))
                    ch.link(nc.vector.tensor_scalar(alpha[:], alpha[:], arange[:, 0:1], 0.1, ALU.mult, ALU.add))
                    for cyc in range(CYC):
                        for b in range(B):
                            j = cyc * B + b
                            src = (xnT if cyc == 0 else ffnT)[:, b * N:(b + 1) * N]
                            dve.wait_ge(layer_act[3], j + 1)
                            if cyc:
                                dve.wait_ge(upd, j - B + 1)
                            nc.vector.tensor_scalar(coup[:, b, :], tanh[:, b, :], beta[:, 0:1], alpha[:, b:b + 1],
                                                    ALU.mult, ALU.add).then_inc(coupled, 1)
                            dve.wait_ge(coupled, j + 1)
                            dve.wait_ge(twist_mm, j + 1)
                            nc.vector.tensor_tensor(move[:, b, :], bank[4 + b][:, :], coup[:, b, :],
                                                    ALU.mult).then_inc(moved, 1)
                            dve.wait_ge(moved, j + 1)
                            nc.vector.tensor_tensor(ffnT[:, b * N:(b + 1) * N], src, move[:, b, :],
                                                    ALU.add).then_inc(upd, 1)


def wait(eng, s, v):
    if not (isinstance(v, int) and v <= 0):
        eng.wait_ge(s, v)


def run_steps(eng, step):
    step(0, 0)
    step(1, 1)
    with eng.Fori(2, STEPS - 2, 2) as t:
        step(t, 0)
        step(t + 1, 1)
    step(STEPS - 2, 0)
    step(STEPS - 1, 1, last=True)


def ttt(nc, a, g):
    sb, sem, con, bank = g["sb"], g["sem"], g["con"], g["bank"]
    rows_d, attn_d = g["rows_d"], g["attn_d"]
    zbank, zbar_bank, bias_bank, prep_bank = bank[4], bank[5], bank[6], bank[7]
    W, R2 = F, 2 * F
    with ExitStack() as c:
        rows = sb("rows", [P, 2, RC], c=c)
        kt, qt = sb("kt", [P, 2, B * BW], c=c), sb("qt", [P, 2, B * BW], c=c)
        kd = sb("kd", [P, P], c=c)
        pm = sb("pm", [P, 2, P], c=c)
        cc, xkm = sb("cc", [P, 2, F], c=c), sb("xkm", [P, 2, B * H, F], c=c)
        xqb, xg, ob = sb("xqb", [P, 2, F], c=c), sb("xg", [P, F], c=c), sb("ob", [P, 2, F], c=c)
        gd = sb("gd", [P, F], c=c)
        w_sb, bias_sb = sb("w_sb", [P, B, H, F], c=c), sb("bias_sb", [P, F], c=c)
        w0, w0c = sb("w0", [P, H, F], c=c), sb("w0c", [P, H, F], c=c)
        wmean = sb("wmean", [P, H], c=c)
        head_rows = sb("head_rows", [H, 3 * F], c=c)
        gr, gbr, g2, ggb, bias0 = (sb(n, [P, F], c=c) for n in ("gr", "gbr", "g2", "ggb", "bias0"))
        bmean = sb("bmean", [P, 1], c=c)
        tok, ti = sb("tok", [P, K], c=c), sb("ti", [P, K], c=c)
        tim, blkt = sb("tim", [P, P], c=c), sb("blkt", [P, P], c=c)
        st, mv, std = sb("zst", [P, 6], c=c), sb("zmv", [P, 2], c=c), sb("zstd", [P, 1], c=c)
        bst, bmv, bstd = sb("bst", [P, 6], c=c), sb("bmv", [P, 2], c=c), sb("bstd", [P, 1], c=c)
        r, rr, r2, brs = (sb(n, [P, 1], c=c) for n in ("zr", "zrr", "zr2", "brs"))
        m1s, m1, es, sc = (sb(n, [P, 1], c=c) for n in ("m1s", "m1", "es", "sc"))
        pz, gy, junk, wz = (sb(n, [P, F], c=c) for n in ("pz", "gy", "junk", "wz"))
        grad, xhb = sb("grad", [P, F], c=c), sb("xhb", [P, 2, F], c=c)

        ld, setup = sem("ttt_loads", c), sem("ttt_setup", c)
        head_mm, zeroed = sem("head_mm", c), sem("zeroed", c)
        rows_in = [sem(f"rows_in{p}", c) for p in range(2)]
        ob_out = [sem(f"ob_out{p}", c) for p in range(2)]
        tr_mm, kt_done, gram_mm, pm_done = (sem(n, c) for n in ("tr_mm", "kt_done", "gram_mm", "pm_done"))
        z_mm, var_done, std_done, grad_done = (sem(n, c) for n in ("z_mm", "var_done", "std_done", "grad_done"))
        upd_mm, bias_mm, zbar_mm = (sem(n, c) for n in ("upd_mm", "bias_mm_t", "zbar_mm"))
        wa_done, wd_done, bc_done = (sem(n, c) for n in ("wa_done", "wd_done", "bc_done"))
        bvar_done, bstd_done, xhb_done = (sem(n, c) for n in ("bvar_done", "bstd_done", "xhb_done"))
        cc_done, xkm_done, xqb_done, ob_done = (sem(n, c) for n in ("cc_done", "xkm_done", "xqb_done", "ob_done"))
        gd_done, xg_done, rr_done = sem("gd_done", c), sem("xg_done", c), sem("rr_done", c)
        v_order, waited = sem("v_order", c), sem("waited", c)

        with nc.Block() as block:
            @block.sync
            def _(sp):
                for n, name in enumerate(("ttt_ln_w", "ttt_ln_b")):
                    sp.dma_start(head_rows[:, n * F:(n + 1) * F], a["L0_attn_" + name]).then_inc(ld, 16)
                sp.dma_start(head_rows[:, 2 * F:3 * F], a["L0_attn_b1"].rearrange("h o f -> h (o f)")).then_inc(ld, 16)
                sp.dma_start(tok[:], a["L0_attn_tok_idx"].partition_broadcast(P)).then_inc(ld, 16)
                sp.dma_start(w0[:], a["L0_attn_W1"].rearrange("h f g -> f h g")).then_inc(ld, 16)

            @block.tensor
            def _(pe):
                pe.wait_ge(ld, 80)
                nc.tensor.matmul(prep_bank[:, 0:3 * F], con("headT", H), head_rows[:], start=True, stop=True).then_inc(head_mm, 1)

            @block.gpsimd
            def _(pool):
                nc.gpsimd.memset(kt[:], 0.0).then_inc(zeroed, 1)
                nc.gpsimd.memset(qt[:], 0.0).then_inc(zeroed, 1)

            @block.vector
            def _(dve):
                ch = Chain(dve, setup)
                dve.wait_ge(ld, 80)
                ch.link(nc.vector.tensor_tensor(ti[:], con("inv")[:, 0:K], tok[:], ALU.add))
                ch.link(nc.vector.tensor_scalar(ti[:], ti[:], 0.0, None, ALU.max))
                ch.mark(nc.vector.tensor_tensor(tim[:].rearrange("p (n k) -> p n k", k=K),
                                                con("tri").rearrange("p (n k) -> p n k", k=K),
                                                ti[:, None, :].broadcast_to([P, P // K, K]), ALU.mult))
                ch.mark(nc.vector.tensor_scalar(blkt[:], con("blk"), ti[:, K - 1:K], None, ALU.mult))
                ch.link(nc.vector.tensor_reduce(wmean[:], w0[:], AX, ALU.add))
                ch.link(nc.vector.tensor_scalar(wmean[:], wmean[:], 1.0 / F, None, ALU.mult))
                for h in range(H):
                    ch.mark(nc.vector.tensor_scalar(w0c[:, h, :], w0[:, h, :], wmean[:, h:h + 1], None, ALU.subtract))
                dve.wait_ge(head_mm, 1)
                ch.mark(nc.vector.tensor_copy(gr[:], prep_bank[:, 0:F]))
                ch.mark(nc.vector.tensor_copy(gbr[:], prep_bank[:, F:2 * F]))
                ch.link(nc.vector.tensor_reduce(bmean[:], prep_bank[:, 2 * F:3 * F], AX, ALU.add))
                ch.mark(nc.vector.tensor_tensor(g2[:], gr[:], gr[:], ALU.mult))
                ch.mark(nc.vector.tensor_tensor(ggb[:], gr[:], gbr[:], ALU.mult))
                ch.link(nc.vector.tensor_scalar(bmean[:], bmean[:], 1.0 / F, None, ALU.mult))
                ch.mark(nc.vector.tensor_scalar(bias0[:], prep_bank[:, 2 * F:3 * F], bmean[:, 0:1], None, ALU.subtract))

        with nc.Block() as block:
            @block.sync
            def _(sp):
                def step(t, p, last=False):
                    if isinstance(t, int):
                        src, dst = rows_d[t], attn_d[t - 2] if t >= 2 else None
                    else:
                        src, dst = rows_d[bass.ds(t, 1)], attn_d[bass.ds(t - 2, 1)]
                    src = src.rearrange("b h j c -> (b h j) c" if isinstance(t, int) else "t b h j c -> (t b h j) c")
                    wait(sp, tr_mm, t - 1)
                    wait(sp, rr_done, t - 1)
                    wait(sp, xqb_done, t - 1)
                    wait(sp, xkm_done, t - 1)
                    wait(sp, gd_done, t - 1)
                    sp.dma_start(rows[:, p, :], src[:, 0:RC]).then_inc(rows_in[p], 16)
                    if dst is not None:
                        store(t - 2, p, dst)

                def store(t, p, dst):
                    dst = dst.rearrange("b h j c -> (b h j) c" if isinstance(t, int) else "t b h j c -> (t b h j) c")
                    sp.wait_ge(ob_done, t + 1)
                    sp.dma_start(dst, ob[:, p, :]).then_inc(ob_out[p], 16)

                run_steps(sp, step)
                store(STEPS - 2, 0, attn_d[STEPS - 2])
                store(STEPS - 1, 1, attn_d[STEPS - 1])
                for p in range(2):
                    sp.wait_ge(ob_out[p], 16 * STEPS // 2)

            @block.tensor
            def _(pe):
                def prep(t, p):
                    pe.wait_ge(rows_in[p], 8 * t + (16 - 8 * p))
                    wait(pe, pm_done, t)
                    nc.tensor.transpose(prep_bank[:, 0:P], rows[:, p, 0:F], con("ident"))
                    nc.tensor.transpose(prep_bank[:, P:2 * P], rows[:, p, R2:3 * F], con("ident")).then_inc(tr_mm, 1)
                    pe.wait_ge(kt_done, t + 1)
                    queries = qt[:, p, :].rearrange("f (b k j) -> f b k j", b=B, k=3)[:, :, 0:3:2, :]
                    nc.tensor.matmul(prep_bank[:, R2:R2 + P], kd[:], queries, start=True, stop=True).then_inc(gram_mm, 1)

                def base(dst, v, p):
                    nc.tensor.matmul(dst[:, 0:F], con("ident"), bias_sb[:], start=True, stop=False, skip_group_check=True)
                    for b in range(B):
                        yield b
                        for h in range(H):
                            mm = nc.tensor.matmul(dst[32 * b:32 * b + 32, 0:F], v[:, p, b * BW + h * K:b * BW + h * K + 2 * K],
                                                  w_sb[:, b, h, :], start=False, stop=(h == 1), skip_group_check=True)
                    yield mm

                def step(t, p, last=False):
                    pe.wait_ge(bc_done, t + 1)
                    for b in base(zbank, kt, p):
                        if isinstance(b, int):
                            pe.wait_ge((wa_done, wd_done)[b % 2], 2 * t + 1 + b // 2)
                    b.then_inc(z_mm, 1)
                    wait(pe, xhb_done, t)
                    for b in base(zbar_bank, qt, p):
                        pass
                    if not last:
                        prep(t + 1, 1 - p)
                    pe.wait_ge(grad_done, t + 1)
                    pe.wait_ge(xkm_done, t + 1)
                    for b in range(B):
                        for h in range(H):
                            mm = nc.tensor.matmul(bank[b][:, h * F:(h + 1) * F], xkm[:, p, b * H + h, :], grad[:], start=False, stop=False, skip_group_check=True)
                        mm.then_inc(upd_mm, 1)
                    nc.tensor.matmul(bias_bank[:, 0:F], blkt[:], grad[:], start=False, stop=False,
                                     skip_group_check=True).then_inc(bias_mm, 1)
                    pe.wait_ge(pm_done, t + 1)
                    nc.tensor.matmul(zbar_bank[:, 0:F], pm[:, p, :], grad[:], start=False, stop=True,
                                     skip_group_check=True).then_inc(zbar_mm, 1)

                for b in range(B):
                    for h in range(H):
                        mm = nc.tensor.matmul(bank[b][:, h * F:(h + 1) * F], con("ident"), w0c[:, h, :],
                                              start=(h == 0), stop=False, skip_group_check=True)
                    mm.then_inc(upd_mm, 1)
                nc.tensor.matmul(bias_bank[:, 0:F], con("ident"), bias0[:], start=True, stop=False,
                                 skip_group_check=True).then_inc(bias_mm, 1)
                prep(0, 0)
                run_steps(pe, step)

            @block.scalar
            def _(act):
                def prep(t, p):
                    act.wait_ge(tr_mm, t + 1)
                    for n, v in enumerate((kt, qt)):
                        nc.scalar.activation(v[:, p, :].rearrange("f (b k j) -> f b k j", b=B, k=3)[:, :, 0:3:2, :],
                                                  prep_bank[:, n * P:(n + 1) * P].rearrange("f (b h j) -> f b h j", b=B, h=H),
                                                  ACT.Copy)
                    nc.scalar.activation(kd[:], prep_bank[:, 0:P], ACT.Copy).then_inc(kt_done, 1)

                def copies(t):
                    for b in (0, 2):
                        act.wait_ge(upd_mm, 4 * t + 5 + b)
                        nc.scalar.activation(w_sb[:, b, :, :], bank[b][:, 0:H * F].rearrange("f (h g) -> f h g", h=H),
                                             ACT.Copy).then_inc(wa_done, 1)
                    act.wait_ge(bias_mm, t + 2)
                    nc.scalar.activation(bias_sb[:], bias_bank[:, 0:F], ACT.Copy).then_inc(bc_done, 1)

                def step(t, p, last=False):
                    act.wait_ge(var_done, t + 1)
                    nc.scalar.activation(std[:], mv[:, 1:2], ACT.Sqrt, bias=con("eps6")).then_inc(std_done, 1)
                    if not last:
                        prep(t + 1, 1 - p)
                        copies(t)
                    act.wait_ge(bvar_done, t + 1)
                    nc.scalar.activation(bstd[:], bmv[:, 1:2], ACT.Sqrt, bias=con("eps6")).then_inc(bstd_done, 1)

                act.wait_ge(zeroed, 2)
                copies(-1)
                prep(0, 0)
                run_steps(act, step)

            @block.gpsimd
            def _(pool):
                def prep(t, p):
                    pool.wait_ge(rows_in[p], 8 * t + (16 - 8 * p))
                    wait(pool, cc_done, t)
                    nc.gpsimd.tensor_tensor(gd[:], gr[:], rows[:, p, F:2 * F], ALU.mult).then_inc(gd_done, 1)
                    wait(pool, upd_mm, 4 * t)
                    nc.gpsimd.tensor_tensor(xkm[:, p, :, :], rows[:, p, 0:F][:, None, :].broadcast_to([P, B * H, F]),
                                            blkt[:, 0:P:K][:, :, None].broadcast_to([P, B * H, F]), ALU.mult).then_inc(xkm_done, 1)
                    pool.wait_ge(gd_done, t + 1)
                    wait(pool, grad_done, t - 1)
                    nc.gpsimd.tensor_tensor(cc[:, p, :], gd[:], ggb[:], ALU.add).then_inc(cc_done, 1)
                    wait(pool, ob_done, t - 1)
                    nc.gpsimd.tensor_tensor(xqb[:, p, :], rows[:, p, R2:3 * F], gbr[:], ALU.add).then_inc(xqb_done, 1)

                def output(t, p):
                    pool.wait_ge(xhb_done, t + 1)
                    wait(pool, ob_done, t)
                    nc.gpsimd.tensor_tensor(xg[:], xhb[:, p, :], gr[:], ALU.mult).then_inc(xg_done, 1)
                    pool.wait_ge(xg_done, t + 1)
                    pool.wait_ge(xqb_done, t + 1)
                    wait(pool, ob_out[p], 8 * t - 8 * p)
                    nc.gpsimd.tensor_tensor(ob[:, p, :], xg[:], xqb[:, p, :], ALU.add).then_inc(ob_done, 1)

                def step(t, p, last=False):
                    if not (isinstance(t, int) and t == 0):
                        output(t - 1, 1 - p)
                    if not last:
                        prep(t + 1, 1 - p)

                prep(0, 0)
                run_steps(pool, step)
                output(STEPS - 1, 1)

            @block.vector
            def _(dve):
                MARKS = 8

                def plain():
                    dve.sem_inc(waited, 1)

                def prep(t, p):
                    dve.wait_ge(gram_mm, t + 1)
                    wait(dve, zbar_mm, t - 1)
                    nc.vector.scalar_tensor_tensor(out=pm[:, p, :], in0=prep_bank[:, R2:R2 + P], scalar=1.0, in1=tim[:],
                                                   op0=ALU.add, op1=ALU.mult).then_inc(pm_done, 1)

                def copies(t):
                    for b in (1, 3):
                        dve.wait_ge(upd_mm, 4 * t + 5 + b)
                        nc.vector.tensor_copy(w_sb[:, b, :, :], bank[b][:, 0:H * F].rearrange("f (h g) -> f h g", h=H)).then_inc(wd_done, 1)

                def step(t, p, last=False):
                    n = [0]

                    def link(ins, hold=True):
                        n[0] += 1
                        ins.then_inc(v_order, 1)
                        if hold:
                            dve.wait_ge(v_order, MARKS * t + n[0])

                    z = zbank[:, 0:F]
                    dve.wait_ge(z_mm, t + 1)
                    link(nc.vector.bn_stats(st[:], z))
                    plain()
                    nc.vector.bn_aggr(mv[:], st[:]).then_inc(var_done, 1)
                    link(nc.vector.tensor_tensor(pz[:], z, g2[:], ALU.mult), hold=False)
                    dve.wait_ge(std_done, t + 1)
                    link(nc.vector.reciprocal(r[:], std[:]))
                    dve.wait_ge(cc_done, t + 1)
                    link(nc.vector.scalar_tensor_tensor(out=gy[:], in0=pz[:], scalar=r[:, 0:1], in1=cc[:, p, :],
                                                        op0=ALU.mult, op1=ALU.add, accum_out=m1s[:]), hold=False)
                    nc.vector.tensor_scalar(rr[:], rows[:, p, 3 * F:RC], r[:, 0:1], 1.0 / F, ALU.mult, ALU.mult).then_inc(rr_done, 1)
                    link(nc.vector.tensor_tensor(r2[:], r[:], r[:], ALU.mult))
                    link(nc.vector.tensor_tensor_reduce(junk[:], gy[:], z, 1.0, 0.0, ALU.mult, ALU.add, es[:]), hold=False)
                    link(nc.vector.tensor_scalar(m1[:], m1s[:], 1.0 / F, None, ALU.mult))
                    nc.vector.tensor_scalar(sc[:], es[:], r2[:, 0:1], 1.0 / F, ALU.mult, ALU.mult).then_inc(v_order, 1)
                    dve.wait_ge(v_order, MARKS * t + 8)
                    n[0] += 1
                    assert n[0] == MARKS
                    nc.vector.scalar_tensor_tensor(out=wz[:], in0=z, scalar=sc[:, 0:1], in1=gy[:],
                                                   op0=ALU.mult, op1=ALU.subtract).then_inc(wz_done, 1)
                    dve.wait_ge(wz_done, t + 1)
                    dve.wait_ge(rr_done, t + 1)
                    nc.vector.tensor_scalar(grad[:], wz[:], m1[:, 0:1], rr[:, 0:1], ALU.add, ALU.mult).then_inc(grad_done, 1)
                    if not last:
                        prep(t + 1, 1 - p)
                        copies(t)
                    zb = zbar_bank[:, 0:F]
                    dve.wait_ge(zbar_mm, t + 1)
                    nc.vector.bn_stats(bst[:], zb).then_inc(bst_done, 1)
                    dve.wait_ge(bst_done, t + 1)
                    plain()
                    nc.vector.bn_aggr(bmv[:], bst[:]).then_inc(bvar_done, 1)
                    dve.wait_ge(bstd_done, t + 1)
                    nc.vector.reciprocal(brs[:], bstd[:]).then_inc(brs_done, 1)
                    dve.wait_ge(brs_done, t + 1)
                    wait(dve, xg_done, t - 1)
                    nc.vector.tensor_scalar(xhb[:, p, :], zb, bmv[:, 0:1], brs[:, 0:1], ALU.subtract, ALU.mult).then_inc(xhb_done, 1)

                wz_done, bst_done, brs_done = sem("wz_done", c), sem("bst_done", c), sem("brs_done", c)
                copies(-1)
                prep(0, 0)
                run_steps(dve, step)


def layer0_out(nc, a, g):
    sb, sem, con, bank = g["sb"], g["sem"], g["con"], g["bank"]
    xt, ffnT, attn_d, xn1, xn1T = g["xt"], g["ffnT"], g["attn_d"], g["xn1"], g["xn1T"]
    wo, wo_bias, up, up_bias = g["wo"], g["wo_bias"], g["up"], g["up_bias"]
    with ExitStack() as c:
        at = sb("at", [P, NT, HD], c=c)
        yn, y2, tT = sb("yn", [P, 2, HD], c=c), sb("y2", [P, 2, HD], c=c), sb("tT", [P, 2, 2, HD], c=c)
        st, mv = sb("st", [P, 3, 6], c=c), sb("mv", [P, 2, 3, 2], c=c)
        std, rs = sb("std", [P, 2, 3], c=c), sb("rs", [P, 2, 3], c=c)
        at_in = [sem(f"at_in{b}", c) for b in range(B)]
        cleared, added, stats, var_done, std_done = (sem(n, c) for n in ("cleared", "added", "st_done", "var_d", "std_d"))
        rs_done, norm_done, tr_mm, cp_done, mm_done = (sem(n, c) for n in ("rs_d", "norm_d", "tr_d", "cp_d", "mm_d"))
        TURNS = NT + 6
        on = lambda n, s: 0 <= n - s < NT
        with nc.Block() as block:
            @block.sync
            def _(sp):
                for i in range(NT):
                    b, t0 = i // TPB, (i % TPB) * (P // K)
                    for h in range(H):
                        sp.dma_start(at[:, i, h * F:(h + 1) * F], attn_d[t0:t0 + P // K, b, h]).then_inc(at_in[b], 16)

            @block.vector
            def _(dve):
                nc.vector.memset(mv[:], 1.0).then_inc(cleared, 1)
                dve.wait_ge(cleared, 1)
                adds = marks = 0
                for n in range(TURNS):
                    p = n % 2
                    if n:
                        dve.wait_ge(mm_done, n)
                    if on(n, 0) and n % TPB == 0:
                        dve.wait_ge(at_in[n // TPB], 32 * TPB)
                    src = [(0, at[:, n, :] if on(n, 0) else None), (2, bank[2 + p][:, 0:HD]), (4, None)]
                    if on(n, 4):
                        i = n - 4
                        nc.vector.tensor_tensor(xt[:, i, :], xt[:, i, :], bank[4 + p][:, 0:D], ALU.add).then_inc(added, 1)
                        adds += 1
                        dve.wait_ge(added, adds)
                        src[2] = (4, xt[:, i, :])
                    for k, (s, v) in enumerate(src):
                        if on(n, s):
                            nc.vector.bn_stats(st[:, k, :], v).then_inc(stats, 1)
                            marks += 1
                    dve.wait_ge(stats, marks)
                    last = [k for k, (s, v) in enumerate(src) if on(n, s)]
                    for k in last:
                        ins = nc.vector.bn_aggr(mv[:, p, k, :], st[:, k, :])
                    if last:
                        ins.then_inc(var_done, 1)
                    else:
                        nc.vector.memset(mv[:, p, 0, :], 1.0).then_inc(var_done, 1)
                    dve.wait_ge(std_done, n + 1)
                    nc.vector.reciprocal(rs[:, p, :], std[:, p, :]).then_inc(rs_done, 1)
                    dve.wait_ge(rs_done, n + 1)
                    dst = (yn[:, p, :], y2[:, p, :], xn1[:, n - 4, :] if on(n, 4) else None)
                    ins = None
                    for k, (s, v) in enumerate(src):
                        if on(n, s):
                            ins = nc.vector.tensor_scalar(dst[k], v, mv[:, p, k, 0:1], rs[:, p, k:k + 1], ALU.subtract, ALU.mult)
                    if ins is None:
                        ins = nc.vector.memset(yn[:, p, :], 0.0)
                    ins.then_inc(norm_done, 1)

            @block.scalar
            def _(act):
                for n in range(TURNS):
                    p = n % 2
                    if n:
                        act.wait_ge(tr_mm, n)
                        ins = None
                        if on(n, 1):
                            ins = nc.scalar.activation(tT[:, p, 0, :], bank[p][:, 0:HD], ACT.Copy)
                        if on(n, 3):
                            ins = nc.scalar.activation(tT[:, p, 1, :], bank[p][:, HD:2 * HD], ACT.Copy)
                        if on(n, 5):
                            i = n - 5
                            ins = nc.scalar.activation(xn1T[:, i * P:(i + 1) * P], bank[6 + p][:, 0:P], ACT.Copy)
                        if ins is not None:
                            ins.then_inc(cp_done, 1)
                        else:
                            act.sem_inc(cp_done, 1)
                    act.wait_ge(var_done, n + 1)
                    nc.scalar.activation(std[:, p, :], mv[:, p, :, 1], ACT.Sqrt, bias=con("eps5")).then_inc(std_done, 1)

            @block.tensor
            def _(pe):
                for n in range(1, TURNS):
                    p = n % 2
                    if n >= 2:
                        pe.wait_ge(cp_done, n - 1)
                    ins = None
                    if on(n, 2):
                        dst = bank[2 + p][:, 0:HD]
                        nc.tensor.matmul(dst, con("ones", 1), wo_bias[:], start=True, stop=False)
                        for k in range(2):
                            ins = nc.tensor.matmul(dst, tT[:, 1 - p, 0, k * P:(k + 1) * P], wo[:, k, :], start=False, stop=(k == 1))
                    if on(n, 4):
                        i = n - 4
                        dst = bank[4 + p][:, 0:D]
                        nc.tensor.matmul(dst, con("ones", 1), up_bias[:], start=True, stop=False)
                        nc.tensor.matmul(dst, ffnT[:, i * P:(i + 1) * P], con("ident"), start=False, stop=False)
                        for k in range(2):
                            ins = nc.tensor.matmul(dst, tT[:, 1 - p, 1, k * P:(k + 1) * P], up[:, k, :], start=False, stop=(k == 1))
                    if ins is not None:
                        ins.then_inc(mm_done, 1)
                    else:
                        pe.sem_inc(mm_done, 1)
                    pe.wait_ge(norm_done, n)
                    ins = None
                    if on(n, 1):
                        for k in range(2):
                            ins = nc.tensor.transpose(bank[p][:, k * P:(k + 1) * P], yn[:, 1 - p, k * P:(k + 1) * P], con("ident"))
                    if on(n, 3):
                        for k in range(2):
                            ins = nc.tensor.transpose(bank[p][:, HD + k * P:HD + (k + 1) * P], y2[:, 1 - p, k * P:(k + 1) * P], con("ident"))
                    if on(n, 5):
                        ins = nc.tensor.transpose(bank[6 + p][:, 0:P], xn1[:, n - 5, :], con("ident"))
                    if ins is not None:
                        ins.then_inc(tr_mm, 1)
                    else:
                        pe.sem_inc(tr_mm, 1)


def layer1(nc, a, out, g):
    sb, sem, con, bank = g["sb"], g["sem"], g["con"], g["bank"]
    xt, xn1, xn1T = g["xt"], g["xn1"], g["xn1T"]
    A = lambda n: a["L1_attn_" + n]
    with ExitStack() as c:
        wT = sb("wT", [P, 3, HD], c=c)
        w_outT = sb("w_outT", [P, 2, D], c=c)
        out_b = sb("out_b", [1, D], c=c)
        uT = sb("uT", [P, 2, TOK], c=c)
        yT = uT
        dts = sb("dts", [P, 2, 2, B], c=c)
        lng, lnb = sb("lng", [P, D], c=c), sb("lnb", [P, D], c=c)
        a_raw, b_ssm, c_ssm = (sb(n, [P, 2, NS], c=c) for n in ("a_raw", "b_ssm", "c_ssm"))
        experts(nc, a, g)
        mixer_in(nc, a, g, locals())
        mixer(nc, a, g, locals())
        final(nc, a, out, g, locals())


def experts(nc, a, g):
    sb, sem, con, bank = g["sb"], g["sem"], g["con"], g["bank"]
    xt, xn1T = g["xt"], g["xn1T"]
    M = lambda n: a["L1_ffn_" + n]
    with ExitStack() as c:
        gate_w, w1 = sb("gate_w", [P, NE], c=c), sb("w1e", [P, 4, P], c=c)
        w2, b1, b2 = sb("w2e", [P, 4, D], c=c), sb("b1e", [P, 4], c=c), sb("b2e", [NE, D], c=c)
        lg, ex, gt = (sb(n, [P, NT, NE], c=c) for n in ("lg", "ex", "gt"))
        mx, sm, top = sb("mx", [P, NT], c=c), sb("sm", [P, NT], c=c), sb("top", [P, NT, 8], c=c)
        idx, idf = sb("idx", [P, NT, 8], U32, c=c), sb("idf", [P, NT, 8], c=c)
        gT = sb("gT", [NE, TOK], c=c)
        he, hg = sb("he", [P, 2, 512], c=c), sb("hg", [P, 4, 512], c=c)
        w_in, gate_mm, ex_done, gates_done, gt_mm, gT_done = (sem(n, c) for n in ("moe_w", "gate_mm", "ex_done", "gates_done", "gt_mm", "gT_done"))
        up_mm, pick_mm, he_done, hg_done, down_mm, y_done = (sem(n, c) for n in ("e_up", "e_pick", "he_done", "hg_done", "e_down", "y_done"))
        mx_done, order = sem("mx_done", c), sem("moe_order", c)
        with nc.Block() as block:
            @block.sync
            def _(sp):
                sp.dma_start(gate_w[:], M("gate_w")).then_inc(w_in, 16)
                for q in range(4):
                    sp.dma_start(w1[:, q, :].rearrange("d (e h) -> d e h", e=2),
                                 M("w1")[2 * q:2 * q + 2].rearrange("e d h -> d e h")).then_inc(w_in, 16)
                sp.dma_start(w2[:], M("w2").rearrange("(q e) h d -> (e h) q d", q=4)).then_inc(w_in, 16)
                sp.dma_start(b1[:], M("b1").rearrange("(q e) h -> (e h) q", q=4)).then_inc(w_in, 16)
                sp.dma_start(b2[:], M("b2")).then_inc(w_in, 16)

            @block.tensor
            def _(pe):
                pe.wait_ge(w_in, 16 * 8)
                for i in range(NT):
                    mm = nc.tensor.matmul(bank[7][:, i * NE:(i + 1) * NE], xn1T[:, i * P:(i + 1) * P], gate_w[:], start=True, stop=True)
                mm.then_inc(gate_mm, 1)
                pe.wait_ge(gates_done, 1)
                for i in range(NT):
                    if i >= 4:
                        pe.wait_ge(gT_done, i // 4)
                    mm = nc.tensor.transpose(bank[6][0:NE, (i % 4) * P:(i % 4 + 1) * P], gt[:, i, :], con("ident"))
                    if i % 4 == 3:
                        mm.then_inc(gt_mm, 1)
                pe.wait_ge(gT_done, 4)
                for t in range(4):
                    tok = slice(t * 512, t * 512 + 512)
                    for q in range(4):
                        n = 4 * t + q
                        if n >= 2:
                            pe.wait_ge(hg_done, n - 1)
                        nc.tensor.matmul(bank[n % 2][:, :], w1[:, q, :], xn1T[:, tok], start=True, stop=True).then_inc(up_mm, 1)
                        nc.tensor.matmul(bank[2 + n % 2][:, :], con("pick", NE)[:, q * P:(q + 1) * P], gT[:, tok],
                                         start=True, stop=True).then_inc(pick_mm, 1)
                    pe.wait_ge(hg_done, 4 * t + 4)
                    if t >= 2:
                        pe.wait_ge(y_done, 4 * (t - 1))
                    for i in range(4):
                        dst = bank[4 + t % 2][:, i * P:(i + 1) * P]
                        nc.tensor.matmul(dst, gT[:, t * 512 + i * P:t * 512 + (i + 1) * P], b2[:], start=True, stop=False)
                        for q in range(4):
                            mm = nc.tensor.matmul(dst, hg[:, q, i * P:(i + 1) * P], w2[:, q, :], start=False, stop=(q == 3))
                    mm.then_inc(down_mm, 1)

            @block.scalar
            def _(act):
                act.wait_ge(mx_done, 1)
                nc.scalar.activation(ex[:], lg[:], ACT.Exp).then_inc(ex_done, 1)
                for t in range(4):
                    for q in range(4):
                        n = 4 * t + q
                        act.wait_ge(up_mm, n + 1)
                        if n >= 2:
                            act.wait_ge(hg_done, n - 1)
                        nc.scalar.activation(he[:, n % 2, :], bank[n % 2][:, :], ACT.Gelu, bias=b1[:, q:q + 1]).then_inc(he_done, 1)

            @block.vector
            def _(dve):
                ch = Chain(dve, order)
                wide = lambda v: v[:, :, None].broadcast_to([P, NT, NE])
                dve.wait_ge(gate_mm, 1)
                logits = bank[7][:, 0:NT * NE].rearrange("p (i e) -> p i e", e=NE)
                ch.link(nc.vector.tensor_reduce(mx[:], logits, AX, ALU.max))
                nc.vector.tensor_tensor(lg[:], logits, wide(mx[:, :]), ALU.subtract).then_inc(mx_done, 1)
                dve.wait_ge(ex_done, 1)
                ch.link(nc.vector.tensor_reduce(sm[:], ex[:], AX, ALU.add))
                ch.link(nc.vector.reciprocal(sm[:], sm[:]))
                ch.link(nc.vector.tensor_tensor(ex[:], ex[:], wide(sm[:, :]), ALU.mult))
                for i in range(NT):
                    ch.mark(nc.vector.max(top[:, i, :], ex[:, i, :]))
                dve.wait_ge(order, ch.n)
                for i in range(NT):
                    ch.mark(nc.vector.max_index(idx[:, i, :], top[:, i, :], ex[:, i, :]))
                dve.wait_ge(order, ch.n)
                ch.link(nc.vector.tensor_copy(idf[:], idx[:]))
                iota = con("iota8")[:, None, :].broadcast_to([P, NT, NE])
                ch.mark(nc.vector.tensor_tensor(lg[:], iota, idf[:, :, 0:1].broadcast_to([P, NT, NE]), ALU.is_equal))
                ch.mark(nc.vector.tensor_tensor(gt[:], iota, idf[:, :, 1:2].broadcast_to([P, NT, NE]), ALU.is_equal))
                ch.link(nc.vector.tensor_tensor(sm[:], top[:, :, 0], top[:, :, 1], ALU.add))
                ch.link(nc.vector.tensor_tensor(gt[:], gt[:], lg[:], ALU.add))
                nc.vector.tensor_tensor(gt[:], gt[:], wide(sm[:, :]), ALU.mult).then_inc(gates_done, 1)
                for k in range(4):
                    dve.wait_ge(gt_mm, k + 1)
                    nc.vector.tensor_copy(gT[:, k * 512:(k + 1) * 512], bank[6][0:NE, :]).then_inc(gT_done, 1)
                for t in range(4):
                    for q in range(4):
                        n = 4 * t + q
                        dve.wait_ge(he_done, n + 1)
                        dve.wait_ge(pick_mm, n + 1)
                        if t:
                            dve.wait_ge(down_mm, t)
                        nc.vector.tensor_tensor(hg[:, q, :], he[:, n % 2, :], bank[2 + n % 2][:, :], ALU.mult).then_inc(hg_done, 1)
                    dve.wait_ge(down_mm, t + 1)
                    rows = xt[:, 4 * t:4 * t + 4, :].rearrange("p i d -> p (i d)")
                    nc.vector.tensor_tensor(rows, rows, bank[4 + t % 2][:, :], ALU.add).then_inc(y_done, 4)


def mixer_in(nc, a, g, l):
    sb, sem, con, bank = g["sb"], g["sem"], g["con"], g["bank"]
    xn1T, wT, w_outT, out_b, uT, dts = g["xn1T"], l["wT"], l["w_outT"], l["out_b"], l["uT"], l["dts"]
    A = l["A"]
    with ExitStack() as c:
        raw, raw_o = sb("raw", [P, 3, 2, D], c=c), sb("raw_o", [P, HD], c=c)
        bx, bg, bd, cb = (sb(n, [P, 2], c=c) for n in ("bx", "bg", "bd", "cb"))
        cw = sb("cw", [P, 2, 3], c=c)
        ub = sb("ub", [P, 2, L + 2], c=c)
        gate = sb("gate", [P, 2, L], c=c)
        c1, c2, c3, df = (sb(n, [P, 2, L], c=c) for n in ("c1", "c2", "c3", "df"))
        ab, rl = sb("ab", [P, 2 * B, L], c=c), sb("rl", [P, L], c=c)
        w_in, w_mm, w_done, pads = (sem(n, c) for n in ("mix_w", "mix_tr", "mix_cp", "pads"))
        u_mm, g_mm, dt_mm = sem("u_mm", c), sem("g_mm", c), sem("dt_mm", c)
        u_done, gate_done, conv_done, diff_done, gd_done, uT_done = (
            sem(n, c) for n in ("u_done", "gate_done", "conv_done", "diff_done", "gated_done", "uT_done"))
        abs_done, relu_done, exp_done, ln_done, order = (sem(n, c) for n in ("abs_done", "relu_done", "exp_done", "ln_done", "mix_order"))
        with nc.Block() as block:
            @block.sync
            def _(sp):
                for n, name in enumerate(("W_x", "W_g", "W_dt")):
                    sp.dma_start(raw[:, n, :, :], A(name).rearrange("(k p) d -> p k d", k=2)).then_inc(w_in, 16)
                sp.dma_start(raw_o[:], A("W_out")).then_inc(w_in, 16)
                for dst, name in ((bx, "b_x"), (bg, "b_g"), (bd, "b_dt"), (cb, "conv_b")):
                    sp.dma_start(dst[:], A(name).rearrange("(k p) -> p k", k=2)).then_inc(w_in, 16)
                sp.dma_start(cw[:], A("conv_w").rearrange("(k p) o w -> p k (o w)", k=2)).then_inc(w_in, 16)
                sp.dma_start(out_b[:], A("b_out").rearrange("(o d) -> o d", o=1)).then_inc(w_in, 16)
                for dst, name in ((l["lng"], "ln_g"), (l["lnb"], "ln_b")):
                    sp.dma_start(dst[:], A(name).partition_broadcast(P)).then_inc(w_in, 16)
                for dst, name in ((l["a_raw"], "A_raw"), (l["b_ssm"], "B_ssm"), (l["c_ssm"], "C_ssm")):
                    sp.dma_start(dst[:], A(name).rearrange("(k p) s -> p k s", k=2)).then_inc(w_in, 16)

            @block.tensor
            def _(pe):
                pe.wait_ge(w_in, 16 * 15)
                for n in range(4):
                    for k in range(2):
                        src = raw[:, n, k, :] if n < 3 else raw_o[:, k * P:(k + 1) * P]
                        mm = nc.tensor.transpose(bank[n][:, k * P:(k + 1) * P], src, con("ident"))
                    mm.then_inc(w_mm, 1)
                pe.wait_ge(w_done, 4)
                for n in range(2 * B):
                    b, k = divmod(n, 2)
                    if n >= 2:
                        pe.wait_ge(u_done, n - 1)
                    nc.tensor.matmul(bank[n % 2][:, :], wT[:, 0, k * P:(k + 1) * P], xn1T[:, b * L:(b + 1) * L],
                                     start=True, stop=True).then_inc(u_mm, 1)
                    if n >= 2:
                        pe.wait_ge(gate_done, n - 1)
                    nc.tensor.matmul(bank[2 + n % 2][:, :], wT[:, 1, k * P:(k + 1) * P], xn1T[:, b * L:(b + 1) * L],
                                     start=True, stop=True).then_inc(g_mm, 1)
                for n in range(2 * B):
                    b, k = divmod(n, 2)
                    if n >= 4:
                        pe.wait_ge(relu_done, n - 3)
                    nc.tensor.matmul(bank[4 + n % 4][:, :], wT[:, 2, k * P:(k + 1) * P], xn1T[:, b * L:(b + 1) * L],
                                     start=True, stop=True).then_inc(dt_mm, 1)

            @block.scalar
            def _(act):
                for n in range(4):
                    act.wait_ge(w_mm, n + 1)
                    dst = wT[:, n, :] if n < 3 else w_outT[:].rearrange("p k d -> p (k d)")
                    nc.scalar.activation(dst, bank[n][:, 0:HD], ACT.Copy).then_inc(w_done, 1)
                act.wait_ge(pads, 1)
                for n in range(2 * B):
                    k = n % 2
                    act.wait_ge(u_mm, n + 1)
                    if n >= 2:
                        act.wait_ge(conv_done, 3 * (n - 1))
                        act.wait_ge(diff_done, n - 1)
                    nc.scalar.activation(ub[:, n % 2, 1:L + 1], bank[n % 2][:, :], ACT.Identity, bias=bx[:, k:k + 1]).then_inc(u_done, 1)
                    act.wait_ge(g_mm, n + 1)
                    if n >= 2:
                        act.wait_ge(gd_done, n - 1)
                    nc.scalar.activation(gate[:, n % 2, :], bank[2 + n % 2][:, :], ACT.Sigmoid, bias=bg[:, k:k + 1]).then_inc(gate_done, 1)
                for n in range(2 * B):
                    b, k = divmod(n, 2)
                    act.wait_ge(dt_mm, n + 1)
                    nc.scalar.activation(ab[:, n, :], bank[4 + n % 4][:, :], ACT.Abs, bias=bd[:, k:k + 1]).then_inc(abs_done, 1)
                    if n:
                        act.wait_ge(relu_done, n)
                    nc.scalar.activation(rl[:], bank[4 + n % 4][:, :], ACT.Relu, bias=bd[:, k:k + 1],
                                         accum_out=dts[:, 0, k, b:b + 1]).then_inc(relu_done, 1)
                for n in range(2 * B):
                    act.wait_ge(abs_done, n + 1)
                    nc.scalar.activation(ab[:, n, :], ab[:, n, :], ACT.Exp, scale=-1.0).then_inc(exp_done, 1)
                for n in range(2 * B):
                    b, k = divmod(n, 2)
                    act.wait_ge(exp_done, n + 1)
                    if n:
                        act.wait_ge(ln_done, n)
                    else:
                        act.wait_ge(relu_done, 2 * B)
                    nc.scalar.activation(rl[:], ab[:, n, :], ACT.Ln, bias=1.0, accum_out=dts[:, 1, k, b:b + 1]).then_inc(ln_done, 1)

            def blend(n):
                b, k = divmod(n, 2)
                nc.vector.wait_ge(gd_done, n + 1)
                nc.vector.tensor_tensor(uT[:, k, b * L:(b + 1) * L], c3[:, n % 2, :], df[:, n % 2, :], ALU.add).then_inc(uT_done, 1)

            @block.vector
            def _(dve):
                nc.vector.memset(ub[:], 0.0).then_inc(pads, 1)
                dve.wait_ge(w_in, 16 * 15)
                for n in range(2 * B):
                    b, k = divmod(n, 2)
                    p = n % 2
                    dve.wait_ge(u_done, n + 1)
                    if n >= 2:
                        dve.wait_ge(uT_done, n - 1)
                    nc.vector.tensor_scalar(c1[:, p, :], ub[:, p, 0:L], cw[:, k, 0:1], cb[:, k:k + 1], ALU.mult, ALU.add).then_inc(conv_done, 1)
                    dve.wait_ge(conv_done, 3 * n + 1)
                    nc.vector.scalar_tensor_tensor(out=c2[:, p, :], in0=ub[:, p, 1:L + 1], scalar=cw[:, k, 1:2], in1=c1[:, p, :],
                                                   op0=ALU.mult, op1=ALU.add).then_inc(conv_done, 1)
                    dve.wait_ge(conv_done, 3 * n + 2)
                    nc.vector.scalar_tensor_tensor(out=c3[:, p, :], in0=ub[:, p, 2:L + 2], scalar=cw[:, k, 2:3], in1=c2[:, p, :],
                                                   op0=ALU.mult, op1=ALU.add).then_inc(conv_done, 1)
                    if n:
                        blend(n - 1)
                blend(2 * B - 1)

            @block.gpsimd
            def _(pool):
                for n in range(2 * B):
                    p = n % 2
                    pool.wait_ge(conv_done, 3 * n + 3)
                    if n >= 2:
                        pool.wait_ge(uT_done, n - 1)
                    nc.gpsimd.tensor_tensor(df[:, p, :], ub[:, p, 1:L + 1], c3[:, p, :], ALU.subtract).then_inc(diff_done, 1)
                    pool.wait_ge(diff_done, n + 1)
                    pool.wait_ge(gate_done, n + 1)
                    nc.gpsimd.tensor_tensor(df[:, p, :], df[:, p, :], gate[:, p, :], ALU.mult).then_inc(gd_done, 1)


def mixer(nc, a, g, l):
    sb, sem, con, bank = g["sb"], g["sem"], g["con"], g["bank"]
    uT, yT, dts = l["uT"], l["yT"], l["dts"]
    a_raw, b_ssm, c_ssm = l["a_raw"], l["b_ssm"], l["c_ssm"]
    NBC = B * NCH
    lna_d = g["lna_d"]
    with ExitStack() as c:
        win = sb("win", [P, 2, NG, P], c=c)
        wst = sb("wst", [P, 2, NG, P], c=c)
        v = sb("v", [P, 2, NBC, NG], c=c)
        dt, t1 = sb("dt", [P, 2], c=c), sb("t1", [P, 2, NS], c=c)
        asp, bsp, lna, cbs = (sb(n, [P, 2, NS], c=c) for n in ("asp", "bsp", "lna", "cbs"))
        lnac, cbc = sb("lnac", [P, NG], c=c), sb("cbc", [P, NG], c=c)
        lnar = sb("lnar", [P, 2, NG, NS], c=c)
        kex = sb("kex", [P, 2, TC, NS], c=c)
        kpad = sb("kpad", [P, 2, 2 * TC], c=c)
        a32, d0 = sb("a32", [P, NG], c=c), sb("d0", [P, NG, B, NCH], c=c)
        order, aorder, porder = sem("ssm_v", c), sem("ssm_a", c), sem("ssm_p", c)
        lna_out, lna_in = sem("lna_out", c), sem("lna_in", c)
        with nc.Block() as block:
            @block.gpsimd
            def _(pool):
                nc.gpsimd.memset(win[:], 0.0).then_inc(porder, 1)
                nc.gpsimd.memset(d0[:], 0.0).then_inc(porder, 1)
                nc.gpsimd.memset(kpad[:], 0.0).then_inc(porder, 1)

            @block.vector
            def _(dve):
                ch = Chain(dve, order)
                w = ch.link
                w(nc.vector.tensor_tensor(dts[:, 0, :, :], dts[:, 0, :, :], dts[:, 1, :, :], ALU.add))
                w(nc.vector.tensor_reduce(dt[:], dts[:, 0, :, :], AX, ALU.add))
                w(nc.vector.tensor_scalar(dt[:], dt[:], 1.0 / TOK, 0.001, ALU.mult, ALU.max))
                w(nc.vector.tensor_scalar(dt[:], dt[:], 2.0, None, ALU.min))
                w(nc.vector.tensor_scalar(asp[:], a_raw[:], -1.0, None, ALU.mult))
                w(nc.vector.tensor_tensor(asp[:], asp[:], a_raw[:], ALU.max))
                dve.wait_ge(aorder, 2)
                w(nc.vector.tensor_scalar(bsp[:], a_raw[:], 0.0, None, ALU.max))
                w(nc.vector.tensor_tensor(asp[:], bsp[:], asp[:], ALU.add))
                w(nc.vector.tensor_scalar(asp[:], asp[:], -1.0, None, ALU.mult))
                w(nc.vector.tensor_tensor(lna[:], asp[:], dt[:, :, None].broadcast_to([P, 2, NS]), ALU.mult))
                w(nc.vector.tensor_scalar(asp[:], asp[:], 1e-6, None, ALU.add))
                w(nc.vector.reciprocal(asp[:], asp[:]))
                dve.wait_ge(aorder, 3)
                w(nc.vector.tensor_scalar(t1[:], t1[:], -1.0, None, ALU.add))
                w(nc.vector.tensor_tensor(t1[:], t1[:], asp[:], ALU.mult))
                w(nc.vector.tensor_tensor(t1[:], t1[:], b_ssm[:], ALU.mult))
                w(nc.vector.tensor_tensor(cbs[:], t1[:], c_ssm[:], ALU.mult))
                w(nc.vector.transpose(lnac[:], lna[:].rearrange("p k s -> p (k s)")))
                w(nc.vector.transpose(cbc[:], cbs[:].rearrange("p k s -> p (k s)")))
                for k in range(2):
                    w(nc.vector.tensor_tensor(kex[:, k, :, :], lna[:, k, None, :].broadcast_to([P, TC, NS]),
                                              con("ramp0")[:, :, None].broadcast_to([P, TC, NS]), ALU.mult))
                dve.wait_ge(aorder, 4)
                for k in range(2):
                    w(nc.vector.tensor_tensor(kex[:, k, :, :], kex[:, k, :, :], cbs[:, k, None, :].broadcast_to([P, TC, NS]), ALU.mult))
                dve.wait_ge(porder, 3)
                w(nc.vector.tensor_reduce(kpad[:, :, TC:2 * TC], kex[:], AX, ALU.add))
                for k in range(2):
                    w(nc.vector.transpose(v[:, k, :, :], uT[:, k, :].rearrange("p (n r) -> p n r", r=TC)))

            @block.scalar
            def _(act):
                act.wait_ge(order, 6)
                nc.scalar.activation(asp[:], asp[:], ACT.Exp, scale=-1.0).then_inc(aorder, 1)
                act.wait_ge(aorder, 1)
                nc.scalar.activation(asp[:], asp[:], ACT.Ln, bias=1.0).then_inc(aorder, 1)
                act.wait_ge(order, 10)
                nc.scalar.activation(t1[:], lna[:], ACT.Exp).then_inc(aorder, 1)
                act.wait_ge(order, 20)
                nc.scalar.activation(kex[:], kex[:], ACT.Exp).then_inc(aorder, 1)
                act.wait_ge(lna_in, 64)
                act.wait_ge(porder, 3)
                for q in range(4):
                    s = slice(32 * q, 32 * q + 32)
                    for k in range(2):
                        at = q * 32 + k * NS
                        nc.scalar.activation(win[s, k, :, at:at + NS], lnar[s, k, :, :], ACT.Exp,
                                             scale=con("expo")[s, :]).then_inc(aorder, 1)
                act.wait_ge(order, 17)
                nc.scalar.activation(a32[:], lnac[:], ACT.Exp, scale=float(TC)).then_inc(aorder, 1)
                act.wait_ge(aorder, 13)
                nc.scalar.activation(d0[:, :, :, 1:NCH].rearrange("p j b c -> p j b c"),
                                     a32[:, :, None, None].broadcast_to([P, NG, B, NCH - 1]), ACT.Copy).then_inc(aorder, 1)

            @block.sync
            def _(sp):
                sp.wait_ge(order, 10)
                sp.dma_start(lna_d.rearrange("(k p) s -> p k s", k=2), lna[:]).then_inc(lna_out, 16)
                sp.wait_ge(lna_out, 16)
                for q in range(4):
                    src = lna_d.rearrange("(k q j) s -> q k j s", k=2, q=4)[q]
                    sp.dma_start(lnar[32 * q:32 * q + 32], src.partition_broadcast(32)).then_inc(lna_in, 16)

        ex2 = sb("ex2", [P, NG, TC], c=c)
        x2 = sb("x2", [P, 2, TC, NG], c=c)
        wexp, wtr, worder = sem("wexp", c), sem("wtr", c), sem("worder", c)
        with nc.Block() as block:
            @block.gpsimd
            def _(pool):
                nc.gpsimd.memset(wst[:], 0.0).then_inc(worder, 1)

            @block.vector
            def _(dve):
                ch = Chain(dve, wtr)
                ch.link(nc.vector.tensor_tensor(ex2[:], lnac[:, :, None].broadcast_to([P, NG, TC]),
                                                con("ramp1")[:, None, :].broadcast_to([P, NG, TC]), ALU.mult))
                for k in range(2):
                    w = kpad[:, k, :]
                    window = bass.AP(tensor=w.tensor, offset=w.offset + TC, ap=[list(w.ap[0]), [1, TC], [-1, TC]])
                    ch.mark(nc.vector.transpose(x2[:, k, :, :], window))
                dve.wait_ge(wexp, 1)
                ch.link(nc.vector.tensor_tensor(ex2[:], ex2[:], cbc[:, :, None].broadcast_to([P, NG, TC]), ALU.mult))
                dve.wait_ge(worder, 1)
                for q in range(4):
                    s = slice(32 * q, 32 * q + 32)
                    for k in range(2):
                        ch.mark(nc.vector.tensor_scalar(wst[s, k, :, 32 * q:32 * q + 32], ex2[s, :, :],
                                                        con("head")[s, k:k + 1], None, ALU.mult))

            @block.scalar
            def _(act):
                act.wait_ge(wtr, 1)
                nc.scalar.activation(ex2[:], ex2[:], ACT.Exp).then_inc(wexp, 1)

        wtap = sb("wtap", [P, NG, P], c=c)
        state = sb("state", [P, NG, B, NCH], c=c)
        ybuf = sb("ybuf", [P, NBC, NG], c=c)
        in_mm, scanned, y_mm, y_cp, y_tr, tap_clear, taps = (
            sem(n, c) for n in ("in_mm", "scanned", "y_mm", "y_cp", "y_tr", "tap_clear", "taps"))
        with nc.Block() as block:
            @block.gpsimd
            def _(pool):
                nc.gpsimd.memset(wtap[:], 0.0).then_inc(tap_clear, 1)

            @block.tensor
            def _(pe):
                for j in range(NG):
                    for k in range(2):
                        mm = nc.tensor.matmul(bank[j // 8][:, (j % 8) * NBC:(j % 8 + 1) * NBC], win[:, k, j, :],
                                              v[:, k, :, j], start=(k == 0), stop=(k == 1))
                    if j % 8 == 7:
                        mm.then_inc(in_mm, 1)
                for k in range(2):
                    pe.wait_ge(taps, 4 * (k + 1))
                    for m in range(4):
                        n = 4 * k + m
                        pe.wait_ge(scanned, m + 1)
                        if n >= 4:
                            pe.wait_ge(y_cp, n - 3)
                        dst = bank[4 + m][:, :].rearrange("p (j b c) -> p j b c", j=8, b=B)
                        for jj in range(8):
                            j = 8 * m + jj
                            nc.tensor.matmul(bank[4 + m][:, jj * NBC:(jj + 1) * NBC], wtap[:, j, :], v[:, k, :, j],
                                             start=True, stop=True)
                            mm = nc.tensor.matmul(dst[:, jj, :, 1:NCH], wst[:, k, j, :], state[:, j, :, 0:NCH - 1],
                                                  start=False, stop=True, skip_group_check=True)
                        mm.then_inc(y_mm, 1)

            @block.vector
            def _(dve):
                for m in range(4):
                    dve.wait_ge(in_mm, m + 1)
                    js = slice(8 * m, 8 * m + 8)
                    nc.vector.tensor_tensor_scan(state[:, js, :, :].rearrange("p j b c -> p (j b c)"),
                                                 d0[:, js, :, :].rearrange("p j b c -> p (j b c)"),
                                                 bank[m][:, :], 0.0, ALU.mult, ALU.add).then_inc(scanned, 1)
                for k in range(2):
                    for m in range(4):
                        n = 4 * k + m
                        dve.wait_ge(y_mm, n + 1)
                        if k:
                            dve.wait_ge(y_tr, 1)
                        nc.vector.tensor_copy(ybuf[:, :, 8 * m:8 * m + 8].rearrange("p n j -> p j n"),
                                              bank[4 + m][:, :].rearrange("p (j n) -> p j n", j=8)).then_inc(y_cp, 1)
                    dve.wait_ge(y_cp, 4 * k + 4)
                    nc.vector.transpose(yT[:, k, :].rearrange("p (n r) -> p n r", r=TC), ybuf[:]).then_inc(y_tr, 1)

            @block.scalar
            def _(act):
                act.wait_ge(tap_clear, 1)
                for k in range(2):
                    if k:
                        act.wait_ge(y_mm, 4)
                    for q in range(4):
                        s = slice(32 * q, 32 * q + 32)
                        nc.scalar.activation(wtap[s, :, 32 * q:32 * q + 32], x2[s, k, :, :].rearrange("p r j -> p j r"),
                                             ACT.Copy).then_inc(taps, 1)


def final(nc, a, out, g, l):
    sb, sem, con, bank = g["sb"], g["sem"], g["con"], g["bank"]
    xt, xn1, yT, w_outT, out_b, lng, lnb = g["xt"], g["xn1"], l["yT"], l["w_outT"], l["out_b"], l["lng"], l["lnb"]
    with ExitStack() as c:
        z, zg = sb("z", [P, NT, D], c=c), sb("zg", [P, NT, D], c=c)
        st, mv = sb("fst", [P, NT, 6], c=c), sb("fmv", [P, NT, 2], c=c)
        std, rs = sb("fstd", [P, NT], c=c), sb("frs", [P, NT], c=c)
        o_mm, z_done, st_done, var_done, std_done, rs_done, zn_done, zg_done, sum_done, xb_done, stored = (
            sem(n, c) for n in ("o_mm", "z_d", "fst_d", "fvar_d", "fstd_d", "frs_d", "zn_d", "zg_d", "sum_d", "xb_d", "stored"))
        with nc.Block() as block:
            @block.tensor
            def _(pe):
                for m in range(4):
                    for jj in range(4):
                        i = 4 * m + jj
                        dst = bank[m][:, jj * P:(jj + 1) * P]
                        nc.tensor.matmul(dst, con("ones", 1), out_b[:], start=True, stop=False)
                        for k in range(2):
                            mm = nc.tensor.matmul(dst, yT[:, k, i * P:(i + 1) * P], l["w_outT"][:, k, :], start=False, stop=(k == 1))
                    mm.then_inc(o_mm, 1)

            @block.vector
            def _(dve):
                for m in range(4):
                    ts = slice(4 * m, 4 * m + 4)
                    dve.wait_ge(o_mm, m + 1)
                    nc.vector.tensor_tensor(z[:, ts, :].rearrange("p i d -> p (i d)"), bank[m][:, :],
                                            xn1[:, ts, :].rearrange("p i d -> p (i d)"), ALU.add).then_inc(z_done, 1)
                    dve.wait_ge(z_done, m + 1)
                    for i in range(4 * m, 4 * m + 4):
                        nc.vector.bn_stats(st[:, i, :], z[:, i, :]).then_inc(st_done, 1)
                    dve.wait_ge(st_done, 4 * m + 4)
                    for i in range(4 * m, 4 * m + 4):
                        ins = nc.vector.bn_aggr(mv[:, i, :], st[:, i, :])
                    ins.then_inc(var_done, 1)
                for m in range(4):
                    ts = slice(4 * m, 4 * m + 4)
                    dve.wait_ge(std_done, m + 1)
                    nc.vector.reciprocal(rs[:, ts], std[:, ts]).then_inc(rs_done, 1)
                    dve.wait_ge(rs_done, m + 1)
                    for i in range(4 * m, 4 * m + 4):
                        nc.vector.tensor_scalar(z[:, i, :], z[:, i, :], mv[:, i, 0:1], rs[:, i:i + 1],
                                                ALU.subtract, ALU.mult).then_inc(zn_done, 1)
                    dve.wait_ge(zn_done, 4 * m + 4)
                    nc.vector.tensor_tensor(zg[:, ts, :], z[:, ts, :], lng[:, None, :].broadcast_to([P, 4, D]), ALU.mult).then_inc(zg_done, 1)
                    dve.wait_ge(zg_done, m + 1)
                    dve.wait_ge(xb_done, m + 1)
                    nc.vector.tensor_tensor(zg[:, ts, :], zg[:, ts, :], xt[:, ts, :], ALU.add).then_inc(sum_done, 1)

            @block.gpsimd
            def _(pool):
                for m in range(4):
                    ts = slice(4 * m, 4 * m + 4)
                    nc.gpsimd.tensor_tensor(xt[:, ts, :], xt[:, ts, :], lnb[:, None, :].broadcast_to([P, 4, D]), ALU.add).then_inc(xb_done, 1)

            @block.scalar
            def _(act):
                for m in range(4):
                    ts = slice(4 * m, 4 * m + 4)
                    act.wait_ge(var_done, m + 1)
                    nc.scalar.activation(std[:, ts], mv[:, ts, 1], ACT.Sqrt, bias=con("eps5")).then_inc(std_done, 1)

            @block.sync
            def _(sp):
                for m in range(4):
                    sp.wait_ge(sum_done, m + 1)
                    sp.dma_start(out[m].rearrange("(n p) d -> p n d", p=P), zg[:, 4 * m:4 * m + 4, :]).then_inc(stored, 16)
                sp.wait_ge(stored, 64)


_OUT = ((B, L, D), "float32")


def kernel(**inputs):
    import concourse.bacc as bacc
    from concourse.bass_utils import run_bass_kernel_spmd

    nc = bacc.Bacc("TRN2", target_bir_lowering=False, num_devices=1)
    arrays, aps = {}, {}
    for name, v in inputs.items():
        v = np.ascontiguousarray(v)
        arrays[f"in_{name}"] = v
        aps[name] = nc.dram_tensor(f"in_{name}", v.shape, mybir.dt.from_np(v.dtype), kind="ExternalInput").ap()
    arrays["in_constants"] = constants()
    const = nc.dram_tensor("in_constants", arrays["in_constants"].shape, F32, kind="ExternalInput").ap()
    out = nc.dram_tensor("out_0", _OUT[0], F32, kind="ExternalOutput").ap()
    build(nc, aps, const, out)
    r = run_bass_kernel_spmd(nc, [arrays], core_ids=[0])
    return r.results[0]["out_0"]
```

```python
from contextlib import ExitStack

import concourse.bass as bass
import numpy as np
from concourse import mybir

F32 = mybir.dt.float32
U32 = mybir.dt.uint32
ACT = mybir.ActivationFunctionType
ALU = mybir.AluOpType
AX = mybir.AxisListType.X

P = 128
B, L, D = 4, 512, 128
TOK = B * L
NT = TOK // P
TPB = L // P
H, F, K = 2, 128, 16
HD = H * F
STEPS = L // K
RING = 4
RC = 3 * F + 1
BW = 3 * K
NG = 32
TC = 32
NCH = L // TC
NS = 16
NE = 8
EH = 64

CONSTS = [("ident", P), ("twist", P), ("tri", P), ("blk", P), ("inv", P), ("head", 2), ("expo", 1),
          ("ramp1", TC), ("ramp0", TC), ("mask4", 4), ("iota8", NE), ("pick", 4 * P), ("ones", P),
          ("eps6", 1), ("eps5", 1), ("quad", 4), ("headT", P)]


def constant_columns():
    at, n = {}, 0
    for name, width in CONSTS:
        at[name] = (n, n + width)
        n += width
    return at, n


def constants():
    at, n = constant_columns()
    c = np.zeros((P, n), np.float32)
    p, q = np.arange(P)[:, None], np.arange(P)[None, :]

    def put(name, v):
        a, b = at[name]
        c[:, a:b] = v

    same = (p // K) == (q // K)
    put("ident", p == q)
    tw = np.zeros((P, P))
    for dst, src, sign in ((0, 2, 1), (1, 3, -1), (2, 0, -1), (3, 1, 1)):
        for i in range(32):
            tw[32 * src + i, 32 * dst + i] = sign
    put("twist", tw)
    put("tri", same & (p <= q))
    put("blk", same)
    put("inv", 1.0 / (q % K + 1) + 0.0 * p)
    put("head", (p // K) % H == np.arange(H)[None, :])
    put("expo", TC - 1 - p % TC)
    put("ramp1", np.arange(1, TC + 1)[None, :] + 0.0 * p)
    put("ramp0", np.arange(TC)[None, :] + 0.0 * p)
    put("mask4", (p // NS) % 4 == np.arange(4)[None, :])
    put("iota8", np.arange(NE)[None, :] + 0.0 * p)
    pick = np.zeros((P, 4, P))
    for e in range(NE):
        pick[e, e // 2, EH * (e % 2):EH * (e % 2) + EH] = 1
    put("pick", pick.reshape(P, -1))
    put("ones", 1.0)
    put("eps6", 1e-6)
    put("eps5", 1e-5)
    put("quad", p // 32 == np.arange(4)[None, :])
    put("headT", (q // K) % H == p)
    return c


class Chain:

    def __init__(self, eng, sem):
        self.eng, self.sem, self.n = eng, sem, 0

    def mark(self, ins):
        self.n += 1
        ins.then_inc(self.sem, 1)

    def link(self, ins):
        self.mark(ins)
        self.eng.wait_ge(self.sem, self.n)


def build(nc, a, const, out):
    ctx = ExitStack()
    with ctx, nc.allow_non_contiguous_dma(reason="bias columns and token regrouping"):
        at, ncol = constant_columns()
        taken = set()

        def unique(name):
            while name in taken:
                name += "_"
            taken.add(name)
            return name

        def sb(name, shape, dt=F32, c=ctx):
            return c.enter_context(nc.sbuf_tensor(unique(name), shape, dt))

        def sem(name, c=ctx):
            return c.enter_context(nc.semaphore(unique(name)))

        bank = [ctx.enter_context(nc.psum_tensor(f"bank{i}", [P, 512], F32)) for i in range(8)]
        cst = sb("cst", [P, ncol])

        def con(name, rows=P):
            lo, hi = at[name]
            return cst[0:rows, lo:hi]

        rows_d = nc.dram_tensor("rows_scratch", (STEPS, B, H, K, RC + 3), F32).ap()
        attn_d = nc.dram_tensor("attn_scratch", (STEPS, B, H, K, F), F32).ap()

        xt = sb("xt", [P, NT, D])
        ffnT = sb("ffnT", [P, TOK])
        wo = sb("wo", [P, 2, HD])
        wo_bias = sb("wo_bias", [1, HD])
        up = sb("up", [P, 2, D])
        up_bias = sb("up_bias", [1, D])
        lna_d = nc.dram_tensor("lna_scratch", (HD, NS), F32).ap()

        with ExitStack() as late:
            layer0_in(nc, a, const, out, locals())
            ttt(nc, a, locals())
        xn1, xn1T = sb("xn1", [P, NT, D]), sb("xn1T", [P, TOK])
        layer0_out(nc, a, locals())
        layer1(nc, a, out, locals())
    return nc


def layer0_in(nc, a, const, out, g):
    sb, sem, con, bank = g["sb"], g["sem"], g["con"], g["bank"]
    cst, xt, ffnT, rows_d = g["cst"], g["xt"], g["ffnT"], g["rows_d"]
    wo, wo_bias, up, up_bias = g["wo"], g["wo_bias"], g["up"], g["up_bias"]
    with ExitStack() as c:
        xnT = sb("xnT", [P, TOK], c=c)
        hT = sb("hT", [P, 2, TOK], c=c)
        xn = sb("xn", [P, NT, D], c=c)
        down = sb("down", [P, HD], c=c)
        down_b = sb("down_b", [P, 2], c=c)
        w4 = sb("w4", [P, 2, H, RC], c=c)
        wv = sb("wv", [P, 2, HD], c=c)
        lrb = sb("lrb", [P, H], c=c)
        post_w, post_b = sb("post_w", [P, 2], c=c), sb("post_b", [P, 2], c=c)
        ln_w, ln_b = sb("ln_w", [P, 2], c=c), sb("ln_b", [P, 2], c=c)
        wo_raw, up_raw = sb("wo_raw", [P, 2, HD], c=c), sb("up_raw", [P, 2, D], c=c)
        upb_raw = sb("upb_raw", [1, D], c=c)
        cw1, cw2 = sb("cw1", [P, 128], c=c), sb("cw2", [P, 64], c=c)
        cw3, cw4 = sb("cw3", [64, 32], c=c), sb("cw4", [32, 1], c=c)
        cw4r = sb("cw4r", [32, P], c=c)
        cb1, cb2, cb3 = sb("cb1", [P, 1], c=c), sb("cb2", [64, 1], c=c), sb("cb3", [32, 1], c=c)
        cb4, gb3 = sb("cb4", [P, 1], c=c), sb("gb3", [P, 1], c=c)
        gw1, gw2, gw3 = sb("gw1", [P, 64], c=c), sb("gw2", [64, 32], c=c), sb("gw3", [32, 1], c=c)
        gw3r = sb("gw3r", [32, P], c=c)
        gb1, gb2 = sb("gb1", [64, 1], c=c), sb("gb2", [32, 1], c=c)
        arange = sb("arange", [P, 1], c=c)
        half_b4, half_gb3 = sb("half_b4", [P, 1], c=c), sb("half_gb3", [P, 1], c=c)
        stats, mv = sb("stats", [P, NT, 6], c=c), sb("mv", [P, NT, 2], c=c)
        std, rstd = sb("std", [P, NT], c=c), sb("rstd", [P, NT], c=c)

        x_in = [sem(f"x_in{b}", c) for b in range(B)]
        w_in = sem("w_in", c)
        stats_done, std_done, xn_done = sem("stats_done", c), sem("std_done", c), sem("xn_done", c)
        xnT_mm, xnT_done = sem("xnT_mm", c), sem("xnT_done", c)
        v_chain = sem("v_chain", c)
        bias_mm = sem("bias_mm", c)
        weights_ready = sem("weights_ready", c)
        loads = []

        def load(eng, dst, src):
            eng.dma_start(dst, src).then_inc(w_in, 16)
            loads.append(1)

        col = lambda v, n: v.rearrange("(k p) -> p k", k=n)
        with nc.Block() as block:
            @block.sync
            def _(sp):
                for b in range(B):
                    sp.dma_start(xt[:, b * TPB:(b + 1) * TPB, :],
                                 a["L0_attn_x"][b].rearrange("(n p) d -> p n d", p=P)).then_inc(x_in[b], 16)
                sp.dma_start(cst[:], const).then_inc(w_in, 16)
                loads.append(1)
                for h in range(H):
                    hs = slice(h * F, h * F + F)
                    load(sp, w4[:, :, h, 0:F], a["L0_attn_wk"][:, hs].rearrange("(k p) f -> p k f", k=2))
                    load(sp, w4[:, :, h, 2 * F:3 * F], a["L0_attn_wq"][:, hs].rearrange("(k p) f -> p k f", k=2))
                    load(sp, w4[:, :, h, 3 * F], col(a["L0_attn_lr_w"][h, 0], 2))
                load(sp, wv[:], a["L0_attn_wv"].rearrange("(k p) f -> p k f", k=2))
                load(sp, lrb[:], a["L0_attn_lr_b"].partition_broadcast(P))
                for dst, name in ((down_b, "down_b"), (post_w, "post_w"), (post_b, "post_b"), (ln_w, "ln_w"), (ln_b, "ln_b")):
                    load(sp, dst[:], col(a["L0_attn_" + name], 2))
                load(sp, upb_raw[:], a["L0_attn_up_b"].rearrange("(o d) -> o d", o=1))

            @block.scalar
            def _(act):
                load(act, down[:], a["L0_attn_down_w"])
                load(act, wo_raw[:], a["L0_attn_wo"].rearrange("(k p) f -> p k f", k=2))
                load(act, up_raw[:], a["L0_attn_up_w"].rearrange("(k p) f -> p k f", k=2))
                for dst, name in ((cw1, "cn_w1"), (cw2, "cn_w2"), (cw3, "cn_w3"), (cw4, "cn_w4"),
                                  (gw1, "gc_w1"), (gw2, "gc_w2"), (gw3, "gc_w3")):
                    load(act, dst[:], a["L0_ffn_" + name])
                for dst, name in ((cb1, "cn_b1"), (cb2, "cn_b2"), (cb3, "cn_b3"), (gb1, "gc_b1"), (gb2, "gc_b2")):
                    load(act, dst[:], a["L0_ffn_" + name].rearrange("(p o) -> p o", o=1))
                for dst, name in ((cb4, "cn_b4"), (gb3, "gc_b3"), (arange, "adaptive_range")):
                    load(act, dst[:], a["L0_ffn_" + name].partition_broadcast(P))
                act.wait_ge(w_in, 16 * len(loads))
                for b in range(B):
                    act.wait_ge(stats_done, b + 1)
                    s = slice(b * TPB, (b + 1) * TPB)
                    act.activation(std[:, s], mv[:, s, 1], ACT.Sqrt, bias=con("eps5")).then_inc(std_done, 1)

            @block.vector
            def _(dve):
                ch = Chain(dve, v_chain)
                for b in range(B):
                    dve.wait_ge(x_in[b], 16)
                    for i in range(b * TPB, (b + 1) * TPB):
                        ch.mark(nc.vector.bn_stats(stats[:, i, :], xt[:, i, :]))
                    dve.wait_ge(v_chain, ch.n)
                    for i in range(b * TPB, (b + 1) * TPB):
                        last = nc.vector.bn_aggr(mv[:, i, :], stats[:, i, :])
                        if i == (b + 1) * TPB - 1:
                            last.then_inc(stats_done, 1)
                        else:
                            ch.mark(last)
                    dve.wait_ge(stats_done, b + 1)
                for b in range(B):
                    s = slice(b * TPB, (b + 1) * TPB)
                    dve.wait_ge(std_done, b + 1)
                    ch.link(nc.vector.reciprocal(rstd[:, s], std[:, s]))
                    for i in range(b * TPB, (b + 1) * TPB):
                        nc.vector.tensor_scalar(xn[:, i, :], xt[:, i, :], mv[:, i, 0:1], rstd[:, i:i + 1],
                                                ALU.subtract, ALU.mult).then_inc(xn_done, 1)
                dve.wait_ge(w_in, 16 * len(loads))
                for h in range(H):
                    ch.mark(nc.vector.tensor_tensor(w4[:, :, h, F:2 * F], w4[:, :, h, 0:F],
                                                    wv[:, :, h * F:h * F + F], ALU.subtract))
                for k in range(2):
                    ch.mark(nc.vector.tensor_scalar(wo[:, k, :], wo_raw[:, k, :], post_w[:, k:k + 1], None, ALU.mult))
                    ch.mark(nc.vector.tensor_scalar(up[:, k, :], up_raw[:, k, :], ln_w[:, k:k + 1], None, ALU.mult))
                ch.mark(nc.vector.tensor_copy(cw4r[:], cw4[:, 0:1].broadcast_to([32, P])))
                ch.mark(nc.vector.tensor_copy(gw3r[:], gw3[:, 0:1].broadcast_to([32, P])))
                ch.mark(nc.vector.tensor_scalar(half_b4[:], cb4[:], 0.5, None, ALU.mult))
                ch.mark(nc.vector.tensor_scalar(half_gb3[:], gb3[:], 0.5, None, ALU.mult))
                dve.wait_ge(bias_mm, 1)
                ch.mark(nc.vector.tensor_copy(wo_bias[:], bank[6][0:1, 0:HD]))
                dve.wait_ge(bias_mm, 2)
                ch.mark(nc.vector.tensor_tensor(up_bias[:], bank[7][0:1, 0:D], upb_raw[:], ALU.add))
                for b in range(B):
                    dve.wait_ge(xnT_mm, b + 1)
                    ch.mark(nc.vector.tensor_copy(xnT[:, b * L:(b + 1) * L], bank[b][:, :]))

            @block.tensor
            def _(pe):
                pe.wait_ge(w_in, 16 * len(loads))
                for k in range(2):
                    mm = nc.tensor.matmul(bank[6][0:1, 0:HD], post_b[:, k:k + 1], wo_raw[:, k, :],
                                          start=(k == 0), stop=(k == 1))
                mm.then_inc(bias_mm, 1)
                for k in range(2):
                    mm = nc.tensor.matmul(bank[7][0:1, 0:D], ln_b[:, k:k + 1], up_raw[:, k, :],
                                          start=(k == 0), stop=(k == 1))
                mm.then_inc(bias_mm, 1)
                for b in range(B):
                    pe.wait_ge(xn_done, TPB * (b + 1))
                    for i in range(TPB):
                        mm = nc.tensor.transpose(bank[b][:, i * P:(i + 1) * P], xn[:, b * TPB + i, :], con("ident"))
                    mm.then_inc(xnT_mm, 1)

        with ExitStack() as c1:
            sig = sb("sig", [P, 2, 512], c=c1)
            stage = sb("stage", [P, 2, H, RC], c=c1)
            down_mm, sig_done, hT_done = sem("down_mm", c1), sem("sig_done", c1), sem("hT_done", c1)
            proj_mm = [sem(f"proj_mm{h}", c1) for h in range(H)]
            lr_done = sem("lr_done", c1)
            stage_done = [sem(f"stage_done{h}", c1) for h in range(H)]
            stored = [sem(f"rows_stored{p}", c1) for p in range(2)]
            with nc.Block() as block:
                @block.tensor
                def _(pe):
                    for n in range(8):
                        t, m = divmod(n, 2)
                        if n >= 4:
                            pe.wait_ge(hT_done, n - 3)
                        nc.tensor.matmul(bank[n % 4][:, :], down[:, m * P:(m + 1) * P], xnT[:, t * 512:(t + 1) * 512],
                                         start=True, stop=True).then_inc(down_mm, 1)
                    for i in range(NT):
                        pe.wait_ge(hT_done, 8 if i // 4 == 3 else 2 * (i // 4) + 2)
                        if i == 0:
                            pe.wait_ge(hT_done, 4)
                        for h in range(H):
                            if i >= 2:
                                pe.wait_ge(stage_done[h], i - 1)
                                pe.wait_ge(lr_done, 2 * (i - 1))
                            for k in range(2):
                                mm = nc.tensor.matmul(bank[4 + 2 * h + i % 2][:, 0:RC], hT[:, k, i * P:(i + 1) * P],
                                                      w4[:, k, h, :], start=(k == 0), stop=(k == 1))
                            mm.then_inc(proj_mm[h], 1)

                @block.scalar
                def _(act):
                    for n in range(8):
                        act.wait_ge(down_mm, n + 1)
                        if n >= 2:
                            act.wait_ge(hT_done, n - 1)
                        act.activation(sig[:, n % 2, :], bank[n % 4][:, :], ACT.Sigmoid,
                                       bias=down_b[:, n % 2:n % 2 + 1]).then_inc(sig_done, 1)
                    for i in range(NT):
                        act.wait_ge(proj_mm[0], i + 1)
                        if i >= 2:
                            act.wait_ge(stored[i % 2], 32 * (i // 2))
                        act.activation(stage[:, i % 2, 0, 0:3 * F], bank[4 + i % 2][:, 0:3 * F],
                                       ACT.Copy).then_inc(stage_done[0], 1)
                        for h in range(H):
                            if h == 1:
                                act.wait_ge(stage_done[1], i + 1)
                            act.activation(stage[:, i % 2, h, 3 * F:RC], bank[4 + 2 * h + i % 2][:, 3 * F:RC],
                                           ACT.Sigmoid, bias=lrb[:, h:h + 1]).then_inc(lr_done, 1)

                @block.vector
                def _(dve):
                    for n in range(8):
                        t, m = divmod(n, 2)
                        dve.wait_ge(sig_done, n + 1)
                        nc.vector.scalar_tensor_tensor(out=hT[:, m, t * 512:(t + 1) * 512], in0=bank[n % 4][:, :],
                                                       scalar=down_b[:, m:m + 1], in1=sig[:, n % 2, :],
                                                       op0=ALU.add, op1=ALU.mult).then_inc(hT_done, 1)
                    for i in range(NT):
                        dve.wait_ge(proj_mm[1], i + 1)
                        if i >= 2:
                            dve.wait_ge(stored[i % 2], 32 * (i // 2))
                        nc.vector.tensor_copy(stage[:, i % 2, 1, 0:3 * F],
                                              bank[6 + i % 2][:, 0:3 * F]).then_inc(stage_done[1], 1)

                @block.sync
                def _(sp):
                    for i in range(NT):
                        b, t0 = i // TPB, (i % TPB) * (P // K)
                        sp.wait_ge(stage_done[0], i + 1)
                        sp.wait_ge(stage_done[1], i + 1)
                        sp.wait_ge(lr_done, 2 * (i + 1))
                        for h in range(H):
                            sp.dma_start(rows_d[t0:t0 + P // K, b, h, :, 0:RC],
                                         stage[:, i % 2, h, :]).then_inc(stored[i % 2], 16)
                    for p in range(2):
                        sp.wait_ge(stored[p], 32 * (NT // 2))

        with ExitStack() as c1:
            N = 512
            h1, h2 = sb("h1", [P, 4, N], c=c1), sb("h2", [64, 4, N], c=c1)
            h3, tanh = sb("h3", [32, 4, N], c=c1), sb("tanh", [P, 4, N], c=c1)
            coup, move = sb("coup", [P, 4, N], c=c1), sb("move", [P, 4, N], c=c1)
            mean = sb("mean", [P, B], c=c1)
            g1, g2, gf = sb("g1", [64, B], c=c1), sb("g2", [32, B], c=c1), sb("gf", [P, B], c=c1)
            beta, alpha, a0 = sb("beta", [P, 1], c=c1), sb("alpha", [P, B], c=c1), sb("a0", [P, 1], c=c1)
            mean_done, gc_mm, gc_act = sem("mean_done", c1), sem("gc_mm", c1), sem("gc_act", c1)
            layer_mm = [sem(f"cn_mm{n}", c1) for n in range(4)]
            layer_act = [sem(f"cn_act{n}", c1) for n in range(4)]
            twist_mm, moved, coupled, upd = sem("twist_mm", c1), sem("moved", c1), sem("coupled", c1), sem("upd", c1)
            vc = sem("vc", c1)
            CYC = 3
            with nc.Block() as block:
                @block.tensor
                def _(pe):
                    pe.wait_ge(mean_done, 1)
                    nc.tensor.matmul(bank[6][0:64, 0:B], gw1[:], mean[:], start=True, stop=True).then_inc(gc_mm, 1)
                    pe.wait_ge(gc_act, 1)
                    nc.tensor.matmul(bank[6][0:32, 0:B], gw2[:], g1[:], start=True, stop=True).then_inc(gc_mm, 1)
                    pe.wait_ge(gc_act, 2)
                    nc.tensor.matmul(bank[6][:, 0:B], gw3r[:], g2[:], start=True, stop=True).then_inc(gc_mm, 1)
                    for cyc in range(CYC):
                        for n in range(4):
                            for b in range(B):
                                j = cyc * B + b
                                src = (xnT if cyc == 0 else ffnT)[:, b * N:(b + 1) * N]
                                if n == 0:
                                    if cyc:
                                        pe.wait_ge(upd, j - B + 1)
                                    rhs, lhs, m = src, cw1[:], 128
                                    if cyc:
                                        pe.wait_ge(layer_act[3], j - B + 1)
                                else:
                                    pe.wait_ge(layer_act[n - 1], j + 1)
                                    rhs = (h1[:, b, :], h2[:, b, :], h3[:, b, :])[n - 1]
                                    lhs, m = ((cw2[:], 64), (cw3[:], 32), (cw4r[:], 128))[n - 1]
                                nc.tensor.matmul(bank[b][0:m, :], lhs, rhs, start=True, stop=True).then_inc(layer_mm[n], 1)
                                if n == 0:
                                    if j == 0:
                                        pe.wait_ge(gc_act, 3)
                                    nc.tensor.matmul(bank[4 + b][:, :], con("twist"), src, start=True, stop=True).then_inc(twist_mm, 1)

                @block.scalar
                def _(act):
                    act.wait_ge(gc_mm, 1)
                    act.activation(g1[:], bank[6][0:64, 0:B], ACT.Gelu, bias=gb1[:]).then_inc(gc_act, 1)
                    act.wait_ge(gc_mm, 2)
                    act.activation(g2[:], bank[6][0:32, 0:B], ACT.Gelu, bias=gb2[:]).then_inc(gc_act, 1)
                    act.wait_ge(gc_mm, 3)
                    act.activation(gf[:], bank[6][:, 0:B], ACT.Tanh, bias=half_gb3[:], scale=0.5).then_inc(gc_act, 1)
                    for cyc in range(CYC):
                        for n in range(4):
                            for b in range(B):
                                j = cyc * B + b
                                act.wait_ge(layer_mm[n], j + 1)
                                dst, bias, m = ((h1, cb1, 128), (h2, cb2, 64), (h3, cb3, 32), (tanh, half_b4, 128))[n]
                                if n == 3 and cyc:
                                    act.wait_ge(coupled, j - B + 1)
                                if n < 3:
                                    act.activation(dst[:, b, :], bank[b][0:m, :], ACT.Gelu, bias=bias[:]).then_inc(layer_act[n], 1)
                                else:
                                    act.activation(dst[:, b, :], bank[b][0:m, :], ACT.Tanh, bias=bias[:],
                                                   scale=0.5).then_inc(layer_act[n], 1)

                @block.vector
                def _(dve):
                    ch = Chain(dve, vc)
                    ch.link(nc.vector.tensor_reduce(mean[:], xnT[:, :].rearrange("p (b l) -> p b l", b=B), AX, ALU.add))
                    nc.vector.tensor_scalar(mean[:], mean[:], 1.0 / L, None, ALU.mult).then_inc(mean_done, 1)
                    ch.mark(nc.vector.tensor_scalar(beta[:], arange[:], 0.3, None, ALU.mult))
                    dve.wait_ge(gc_act, 3)
                    ch.link(nc.vector.tensor_scalar(alpha[:], gf[:], 0.7, None, ALU.mult))
                    ch.link(nc.vector.tensor_scalar(alpha[:], alpha[:], arange[:, 0:1], 0.1, ALU.mult, ALU.add))
                    for cyc in range(CYC):
                        for b in range(B):
                            j = cyc * B + b
                            src = (xnT if cyc == 0 else ffnT)[:, b * N:(b + 1) * N]
                            dve.wait_ge(layer_act[3], j + 1)
                            if cyc:
                                dve.wait_ge(upd, j - B + 1)
                            nc.vector.tensor_scalar(coup[:, b, :], tanh[:, b, :], beta[:, 0:1], alpha[:, b:b + 1],
                                                    ALU.mult, ALU.add).then_inc(coupled, 1)
                            dve.wait_ge(coupled, j + 1)
                            dve.wait_ge(twist_mm, j + 1)
                            nc.vector.tensor_tensor(move[:, b, :], bank[4 + b][:, :], coup[:, b, :],
                                                    ALU.mult).then_inc(moved, 1)
                            dve.wait_ge(moved, j + 1)
                            nc.vector.tensor_tensor(ffnT[:, b * N:(b + 1) * N], src, move[:, b, :],
                                                    ALU.add).then_inc(upd, 1)


def wait(eng, s, v):
    if not (isinstance(v, int) and v <= 0):
        eng.wait_ge(s, v)


def run_steps(eng, step):
    for t in range(RING):
        step(t, t)
    with eng.Fori(1, STEPS // RING - 1) as lap:
        for p in range(RING):
            step(lap * RING + p, p)
    for p in range(RING):
        step(STEPS - RING + p, p, left=RING - 1 - p)


def ttt(nc, a, g):
    sb, sem, con, bank = g["sb"], g["sem"], g["con"], g["bank"]
    rows_d, attn_d = g["rows_d"], g["attn_d"]
    zbanks, zbar_bank, prep_bank = bank[4:6], bank[6], bank[7]
    R2 = 2 * F
    SLOTS = B * H + 1
    first_slot = lambda b: 0 if b == 0 else b * H + 1
    width = lambda b: 3 if b == 0 else H
    with ExitStack() as c:
        rows = sb("rows", [P, RING, RC], c=c)
        kt, qt = sb("kt", [P, RING, B * BW], c=c), sb("qt", [P, RING, B * BW], c=c)
        kd = sb("kd", [P, 2, P], c=c)
        pm, pair = sb("pm", [P, 2, P], c=c), sb("pair", [P, 2, P], c=c)
        cc, xkm = sb("cc", [P, 2, F], c=c), sb("xkm", [P, 2, B * H, F], c=c)
        xqb, xg, ob = sb("xqb", [P, RING, F], c=c), sb("xg", [P, F], c=c), sb("ob", [P, 2, F], c=c)
        gd = sb("gd", [P, F], c=c)
        w_sb = sb("w_sb", [P, SLOTS, F], c=c)
        w0, w0c = sb("w0", [P, H, F], c=c), sb("w0c", [P, H, F], c=c)
        wmean = sb("wmean", [P, H], c=c)
        head_rows = sb("head_rows", [H, 3 * F], c=c)
        gr, gbr, g2, ggb, bias0 = (sb(n, [P, F], c=c) for n in ("gr", "gbr", "g2", "ggb", "bias0"))
        bmean = sb("bmean", [P, 1], c=c)
        tok, ti = sb("tok", [P, K], c=c), sb("ti", [P, K], c=c)
        tim, blkt = sb("tim", [P, P], c=c), sb("blkt", [P, P], c=c)
        st, mv, std = sb("zst", [P, 6], c=c), sb("zmv", [P, 2], c=c), sb("zstd", [P, 1], c=c)
        bst, bmv, bstd = sb("bst", [P, 6], c=c), sb("bmv", [P, 2], c=c), sb("bstd", [P, 1], c=c)
        r, rr, r2, brs = (sb(n, [P, 1], c=c) for n in ("zr", "zrr", "zr2", "brs"))
        m1s, m1, es, sc, shift = (sb(n, [P, 1], c=c) for n in ("m1s", "m1", "es", "sc", "shift"))
        pz, gy, junk, wz = (sb(n, [P, F], c=c) for n in ("pz", "gy", "junk", "wz"))
        grad, xhb = sb("grad", [P, 2, F], c=c), sb("xhb", [P, 2, F], c=c)

        ld, setup = sem("ttt_loads", c), sem("ttt_setup", c)
        head_mm, zeroed = sem("head_mm", c), sem("zeroed", c)
        rows_in = [sem(f"rows_in{p}", c) for p in range(RING)]
        ob_out = [sem(f"ob_out{p}", c) for p in range(2)]
        tr_mm, kt_done, gram_mm = (sem(n, c) for n in ("tr_mm", "kt_done", "gram_mm"))
        mask_done, pair_done = sem("mask_done", c), sem("pair_done", c)
        z_mm, var_done, std_done, grad_done = (sem(n, c) for n in ("z_mm", "var_done", "std_done", "grad_done"))
        upd_mm, zbar_mm, w_done = (sem(n, c) for n in ("upd_mm", "zbar_mm", "w_done"))
        bvar_done, bstd_done, xhb_done = (sem(n, c) for n in ("bvar_done", "bstd_done", "xhb_done"))
        wz_done, bst_done, brs_done, shift_done = (sem(n, c) for n in ("wz_done", "bst_done", "brs_done", "shift_done"))
        cc_done, xkm_done, xqb_done, ob_done = (sem(n, c) for n in ("cc_done", "xkm_done", "xqb_done", "ob_done"))
        gd_done, xg_done, rr_done = sem("gd_done", c), sem("xg_done", c), sem("rr_done", c)
        v_order, waited = sem("v_order", c), sem("waited", c)

        with nc.Block() as block:
            @block.sync
            def _(sp):
                for n, name in enumerate(("ttt_ln_w", "ttt_ln_b")):
                    sp.dma_start(head_rows[:, n * F:(n + 1) * F], a["L0_attn_" + name]).then_inc(ld, 16)
                sp.dma_start(head_rows[:, 2 * F:3 * F], a["L0_attn_b1"].rearrange("h o f -> h (o f)")).then_inc(ld, 16)
                sp.dma_start(tok[:], a["L0_attn_tok_idx"].partition_broadcast(P)).then_inc(ld, 16)
                sp.dma_start(w0[:], a["L0_attn_W1"].rearrange("h f g -> f h g")).then_inc(ld, 16)

            @block.tensor
            def _(pe):
                pe.wait_ge(ld, 80)
                nc.tensor.matmul(prep_bank[:, 0:3 * F], con("headT", H), head_rows[:], start=True, stop=True).then_inc(head_mm, 1)

            @block.gpsimd
            def _(pool):
                nc.gpsimd.memset(kt[:], 0.0).then_inc(zeroed, 1)
                nc.gpsimd.memset(qt[:], 0.0).then_inc(zeroed, 1)

            @block.vector
            def _(dve):
                ch = Chain(dve, setup)
                dve.wait_ge(ld, 80)
                ch.link(nc.vector.tensor_tensor(ti[:], con("inv")[:, 0:K], tok[:], ALU.add))
                ch.link(nc.vector.tensor_scalar(ti[:], ti[:], 0.0, None, ALU.max))
                ch.mark(nc.vector.tensor_tensor(tim[:].rearrange("p (n k) -> p n k", k=K),
                                                con("tri").rearrange("p (n k) -> p n k", k=K),
                                                ti[:, None, :].broadcast_to([P, P // K, K]), ALU.mult))
                ch.mark(nc.vector.tensor_scalar(blkt[:], con("blk"), ti[:, K - 1:K], None, ALU.mult))
                ch.link(nc.vector.tensor_reduce(wmean[:], w0[:], AX, ALU.add))
                ch.link(nc.vector.tensor_scalar(wmean[:], wmean[:], 1.0 / F, None, ALU.mult))
                for h in range(H):
                    ch.mark(nc.vector.tensor_scalar(w0c[:, h, :], w0[:, h, :], wmean[:, h:h + 1], None, ALU.subtract))
                dve.wait_ge(head_mm, 1)
                ch.mark(nc.vector.tensor_copy(gr[:], prep_bank[:, 0:F]))
                ch.mark(nc.vector.tensor_copy(gbr[:], prep_bank[:, F:2 * F]))
                ch.link(nc.vector.tensor_reduce(bmean[:], prep_bank[:, 2 * F:3 * F], AX, ALU.add))
                ch.mark(nc.vector.tensor_tensor(g2[:], gr[:], gr[:], ALU.mult))
                ch.mark(nc.vector.tensor_tensor(ggb[:], gr[:], gbr[:], ALU.mult))
                ch.link(nc.vector.tensor_scalar(bmean[:], bmean[:], 1.0 / F, None, ALU.mult))
                ch.mark(nc.vector.tensor_scalar(bias0[:], prep_bank[:, 2 * F:3 * F], bmean[:, 0:1], None, ALU.subtract))

        with nc.Block() as block:
            @block.sync
            def _(sp):
                def flat(v):
                    if len(v.shape) == 5:
                        return v.rearrange("t b h j c -> (t b h j) c")
                    return v.rearrange("b h j c -> (b h j) c")

                at = lambda v, t: flat(v[t] if isinstance(t, int) else v[bass.ds(t, 1)])

                def load(s, p):
                    for used in (tr_mm, rr_done, xqb_done, xkm_done, gd_done):
                        wait(sp, used, s - RING + 1)
                    sp.dma_start(rows[:, p, :], at(rows_d, s)[:, 0:RC]).then_inc(rows_in[p], 16)

                def store(t, p):
                    sp.wait_ge(ob_done, t + 1)
                    sp.dma_start(at(attn_d, t), ob[:, p % 2, :]).then_inc(ob_out[p % 2], 16)

                def step(t, p, left=RING):
                    if left >= RING:
                        load(t + RING, p)
                    if not (isinstance(t, int) and t == 0):
                        store(t - 1, (p - 1) % RING)

                for s in range(RING):
                    load(s, s)
                run_steps(sp, step)
                store(STEPS - 1, RING - 1)
                for p in range(2):
                    sp.wait_ge(ob_out[p], 16 * STEPS // 2)

            @block.tensor
            def _(pe):
                def transposes(s, p):
                    pe.wait_ge(rows_in[p], 4 * s + (16 - 4 * p))
                    wait(pe, mask_done, s - 1)
                    wait(pe, pair_done, s - 1)
                    nc.tensor.transpose(prep_bank[:, 0:P], rows[:, p, 0:F], con("ident"))
                    nc.tensor.transpose(prep_bank[:, P:2 * P], rows[:, p, R2:3 * F], con("ident")).then_inc(tr_mm, 1)

                def grams(s, p, pairs=True):
                    dense = lambda v, q: v[:, q, :].rearrange("f (b k j) -> f b k j", b=B, k=3)[:, :, 0:3:2, :]
                    pe.wait_ge(kt_done, s + 2 if pairs else s + 1)
                    mm = nc.tensor.matmul(prep_bank[:, R2:R2 + P], kd[:, p % 2, :], dense(qt, p), start=True, stop=True)
                    if pairs:
                        mm = nc.tensor.matmul(prep_bank[:, R2 + P:R2 + 2 * P], kd[:, p % 2, :], dense(kt, (p + 1) % RING),
                                              start=True, stop=True)
                    mm.then_inc(gram_mm, 1)

                def base(dst, v, p, copied, last_stop=True):
                    pe.wait_ge(w_done, copied + 1)
                    nc.tensor.matmul(dst[:, 0:F], con("ident"), w_sb[:, 2, :], start=True, stop=False, skip_group_check=True)
                    for b in range(B):
                        pe.wait_ge(w_done, copied + b + 1)
                        for h in range(H):
                            at = b * BW + h * K
                            mm = nc.tensor.matmul(dst[32 * b:32 * b + 32, 0:F], v[:, p, at:at + 2 * K],
                                                  w_sb[:, first_slot(b) + h, :], start=False, stop=(h == 1), skip_group_check=True)
                    return mm

                def state_start(t, p, left=RING):
                    if left >= 2:
                        base(zbanks[p % 2], kt, (p + 2) % RING, 4 * (t + 1))
                    wait(pe, xhb_done, t + 1)
                    base(zbar_bank, qt, (p + 1) % RING, 4 * (t + 1))
                    if left >= 2:
                        grams(t + 2, (p + 2) % RING, pairs=left >= 3)

                def step(t, p, left=RING):
                    g_t = grad[:, p % 2, :]
                    pe.wait_ge(grad_done, t + 1)
                    pe.wait_ge(mask_done, t + 1)
                    if left:
                        pe.wait_ge(pair_done, t + 1)
                        nc.tensor.matmul(zbanks[(p + 1) % 2][:, 0:F], pair[:, p % 2, :], g_t, start=False, stop=True,
                                         skip_group_check=True).then_inc(z_mm, 1)
                    nc.tensor.matmul(zbar_bank[:, 0:F], pm[:, p % 2, :], g_t, start=False, stop=True,
                                     skip_group_check=True).then_inc(zbar_mm, 1)
                    if not left:
                        return
                    pe.wait_ge(xkm_done, t + 1)
                    nc.tensor.matmul(bank[0][:, 2 * F:3 * F], blkt[:], g_t, start=False, stop=False, skip_group_check=True)
                    for b in range(B):
                        for h in range(H):
                            mm = nc.tensor.matmul(bank[b][:, h * F:(h + 1) * F], xkm[:, p % 2, b * H + h, :], g_t,
                                                  start=False, stop=False, skip_group_check=True)
                        mm.then_inc(upd_mm, 1)
                        if b == 2 and left >= 3:
                            transposes(t + 3, (p + 3) % RING)
                    state_start(t, p, left)

                for b in range(B):
                    for h in range(H):
                        mm = nc.tensor.matmul(bank[b][:, h * F:(h + 1) * F], con("ident"), w0c[:, h, :],
                                              start=(h == 0), stop=False, skip_group_check=True)
                    if b == 0:
                        mm = nc.tensor.matmul(bank[0][:, 2 * F:3 * F], con("ident"), bias0[:], start=False, stop=False,
                                              skip_group_check=True)
                    mm.then_inc(upd_mm, 1)
                transposes(0, 0)
                pe.wait_ge(kt_done, 1)
                transposes(1, 1)
                base(zbanks[0], kt, 0, 0).then_inc(z_mm, 1)
                grams(0, 0)
                transposes(2, 2)
                state_start(-1, -1)
                run_steps(pe, step)

            @block.scalar
            def _(act):
                def prep(s, p):
                    act.wait_ge(tr_mm, s + 1)
                    for n, v in enumerate((kt, qt)):
                        nc.scalar.activation(v[:, p, :].rearrange("f (b k j) -> f b k j", b=B, k=3)[:, :, 0:3:2, :],
                                             prep_bank[:, n * P:(n + 1) * P].rearrange("f (b h j) -> f b h j", b=B, h=H),
                                             ACT.Copy)
                    nc.scalar.activation(kd[:, p % 2, :], prep_bank[:, 0:P], ACT.Copy).then_inc(kt_done, 1)

                def copy_state(t, b):
                    act.wait_ge(upd_mm, 4 * (t + 1) + b + 1)
                    at, n = first_slot(b), width(b)
                    nc.scalar.activation(w_sb[:, at:at + n, :], bank[b][:, 0:n * F].rearrange("f (h g) -> f h g", h=n),
                                         ACT.Copy).then_inc(w_done, 1)

                def z_deviation(s):
                    act.wait_ge(var_done, s + 1)
                    nc.scalar.activation(std[:], mv[:, 1:2], ACT.Sqrt, bias=con("eps6")).then_inc(std_done, 1)

                def step(t, p, left=RING):
                    if left:
                        z_deviation(t + 1)
                        copy_state(t, 0)
                        copy_state(t, 1)
                    act.wait_ge(bvar_done, t + 1)
                    nc.scalar.activation(bstd[:], bmv[:, 1:2], ACT.Sqrt, bias=con("eps6")).then_inc(bstd_done, 1)
                    if left:
                        copy_state(t, 2)
                        copy_state(t, 3)
                    act.wait_ge(shift_done, t + 1)
                    wait(act, xg_done, t - 1)
                    nc.scalar.activation(xhb[:, p % 2, :], zbar_bank[:, 0:F], ACT.Identity, bias=shift[:, 0:1],
                                         scale=brs[:, 0:1]).then_inc(xhb_done, 1)
                    if left >= 3:
                        prep(t + 3, (p + 3) % RING)

                act.wait_ge(zeroed, 2)
                prep(0, 0)
                for b in range(B):
                    copy_state(-1, b)
                prep(1, 1)
                prep(2, 2)
                z_deviation(0)
                run_steps(act, step)

            @block.gpsimd
            def _(pool):
                def prep(s, p):
                    pool.wait_ge(rows_in[p], 4 * s + (16 - 4 * p))
                    wait(pool, cc_done, s)
                    nc.gpsimd.tensor_tensor(gd[:], gr[:], rows[:, p, F:2 * F], ALU.mult).then_inc(gd_done, 1)
                    pool.wait_ge(gd_done, s + 1)
                    wait(pool, grad_done, s - 1)
                    nc.gpsimd.tensor_tensor(cc[:, p % 2, :], gd[:], ggb[:], ALU.add).then_inc(cc_done, 1)
                    wait(pool, ob_done, s - 3)
                    nc.gpsimd.tensor_tensor(xqb[:, p, :], rows[:, p, R2:3 * F], gbr[:], ALU.add).then_inc(xqb_done, 1)
                    wait(pool, upd_mm, 4 * s)
                    nc.gpsimd.tensor_tensor(xkm[:, p % 2, :, :], rows[:, p, 0:F][:, None, :].broadcast_to([P, B * H, F]),
                                            blkt[:, 0:P:K][:, :, None].broadcast_to([P, B * H, F]), ALU.mult).then_inc(xkm_done, 1)

                def output(t, p):
                    pool.wait_ge(xhb_done, t + 1)
                    wait(pool, ob_done, t)
                    nc.gpsimd.tensor_tensor(xg[:], xhb[:, p % 2, :], gr[:], ALU.mult).then_inc(xg_done, 1)
                    pool.wait_ge(xg_done, t + 1)
                    pool.wait_ge(xqb_done, t + 1)
                    wait(pool, ob_out[p % 2], 8 * t - 8 * (p % 2))
                    nc.gpsimd.tensor_tensor(ob[:, p % 2, :], xg[:], xqb[:, p, :], ALU.add).then_inc(ob_done, 1)

                def step(t, p, left=RING):
                    if not (isinstance(t, int) and t == 0):
                        output(t - 1, (p - 1) % RING)
                    if left >= 2:
                        prep(t + 2, (p + 2) % RING)

                prep(0, 0)
                prep(1, 1)
                run_steps(pool, step)
                output(STEPS - 1, RING - 1)

            @block.vector
            def _(dve):
                MARKS = 8

                def plain():
                    dve.sem_inc(waited, 1)

                def query_mask(s, p):
                    dve.wait_ge(gram_mm, s + 1)
                    wait(dve, zbar_mm, s - 1)
                    nc.vector.scalar_tensor_tensor(out=pm[:, p % 2, :], in0=prep_bank[:, R2:R2 + P], scalar=1.0,
                                                   in1=tim[:], op0=ALU.add, op1=ALU.mult).then_inc(mask_done, 1)

                def pair_mask(s, p):
                    nc.vector.scalar_tensor_tensor(out=pair[:, p % 2, :], in0=prep_bank[:, R2 + P:R2 + 2 * P],
                                                   scalar=1.0, in1=blkt[:], op0=ALU.add, op1=ALU.mult).then_inc(pair_done, 1)

                def zbar_stats(t):
                    dve.wait_ge(zbar_mm, t + 1)
                    nc.vector.bn_stats(bst[:], zbar_bank[:, 0:F]).then_inc(bst_done, 1)

                def zbar_variance(t):
                    dve.wait_ge(bst_done, t + 1)
                    plain()
                    nc.vector.bn_aggr(bmv[:], bst[:]).then_inc(bvar_done, 1)

                def zbar_scale(t):
                    dve.wait_ge(bstd_done, t + 1)
                    nc.vector.reciprocal(brs[:], bstd[:]).then_inc(brs_done, 1)

                def zbar_shift(t):
                    dve.wait_ge(brs_done, t + 1)
                    nc.vector.tensor_scalar(shift[:], bmv[:, 0:1], brs[:, 0:1], -1.0, ALU.mult, ALU.mult).then_inc(shift_done, 1)

                def gradient(s, p, zbar, left):
                    n = [0]

                    def mark(ins):
                        n[0] += 1
                        ins.then_inc(v_order, 1)
                        return n[0]

                    def need(m):
                        dve.wait_ge(v_order, MARKS * s + m)

                    z = zbanks[p % 2][:, 0:F]
                    dve.wait_ge(z_mm, s + 1)
                    stats = mark(nc.vector.bn_stats(st[:], z))
                    if zbar:
                        query_mask(s, p)
                    need(stats)
                    plain()
                    nc.vector.bn_aggr(mv[:], st[:]).then_inc(var_done, 1)
                    mark(nc.vector.tensor_tensor(pz[:], z, g2[:], ALU.mult))
                    if zbar:
                        zbar_stats(s - 1)
                        if left:
                            pair_mask(s, p)
                        zbar_variance(s - 1)
                    dve.wait_ge(std_done, s + 1)
                    need(mark(nc.vector.reciprocal(r[:], std[:])))
                    dve.wait_ge(cc_done, s + 1)
                    mark(nc.vector.scalar_tensor_tensor(out=gy[:], in0=pz[:], scalar=r[:, 0:1], in1=cc[:, p % 2, :],
                                                        op0=ALU.mult, op1=ALU.add, accum_out=m1s[:]))
                    nc.vector.tensor_scalar(rr[:], rows[:, p, 3 * F:RC], r[:, 0:1], 1.0 / F, ALU.mult, ALU.mult).then_inc(rr_done, 1)
                    need(mark(nc.vector.tensor_tensor(r2[:], r[:], r[:], ALU.mult)))
                    if zbar:
                        zbar_scale(s - 1)
                    dot = mark(nc.vector.tensor_tensor_reduce(junk[:], gy[:], z, 1.0, 0.0, ALU.mult, ALU.add, es[:]))
                    mark(nc.vector.tensor_scalar(m1[:], m1s[:], 1.0 / F, None, ALU.mult))
                    if zbar:
                        zbar_shift(s - 1)
                    need(dot)
                    mark(nc.vector.tensor_scalar(sc[:], es[:], r2[:, 0:1], 1.0 / F, ALU.mult, ALU.mult))
                    need(MARKS)
                    assert n[0] == MARKS
                    nc.vector.scalar_tensor_tensor(out=wz[:], in0=z, scalar=sc[:, 0:1], in1=gy[:],
                                                   op0=ALU.mult, op1=ALU.subtract).then_inc(wz_done, 1)
                    dve.wait_ge(wz_done, s + 1)
                    dve.wait_ge(rr_done, s + 1)
                    nc.vector.tensor_scalar(grad[:, p % 2, :], wz[:], m1[:, 0:1], rr[:, 0:1], ALU.add, ALU.mult).then_inc(grad_done, 1)

                def step(t, p, left=RING):
                    if left:
                        gradient(t + 1, (p + 1) % RING, True, left - 1)
                    else:
                        zbar_stats(t)
                        zbar_variance(t)
                        zbar_scale(t)
                        zbar_shift(t)

                query_mask(0, 0)
                pair_mask(0, 0)
                gradient(0, 0, False, RING)
                run_steps(dve, step)


def layer0_out(nc, a, g):
    sb, sem, con, bank = g["sb"], g["sem"], g["con"], g["bank"]
    xt, ffnT, attn_d, xn1, xn1T = g["xt"], g["ffnT"], g["attn_d"], g["xn1"], g["xn1T"]
    wo, wo_bias, up, up_bias = g["wo"], g["wo_bias"], g["up"], g["up_bias"]
    with ExitStack() as c:
        at = sb("at", [P, NT, HD], c=c)
        yn, y2, tT = sb("yn", [P, 2, HD], c=c), sb("y2", [P, 2, HD], c=c), sb("tT", [P, 2, 2, HD], c=c)
        st, mv = sb("st", [P, 3, 6], c=c), sb("mv", [P, 2, 3, 2], c=c)
        std, rs = sb("std", [P, 2, 3], c=c), sb("rs", [P, 2, 3], c=c)
        at_in = [sem(f"at_in{b}", c) for b in range(B)]
        cleared, added, stats, var_done, std_done = (sem(n, c) for n in ("cleared", "added", "st_done", "var_d", "std_d"))
        rs_done, norm_done, tr_mm, cp_done, mm_done = (sem(n, c) for n in ("rs_d", "norm_d", "tr_d", "cp_d", "mm_d"))
        TURNS = NT + 6
        on = lambda n, s: 0 <= n - s < NT
        with nc.Block() as block:
            @block.sync
            def _(sp):
                for i in range(NT):
                    b, t0 = i // TPB, (i % TPB) * (P // K)
                    for h in range(H):
                        sp.dma_start(at[:, i, h * F:(h + 1) * F], attn_d[t0:t0 + P // K, b, h]).then_inc(at_in[b], 16)

            @block.vector
            def _(dve):
                nc.vector.memset(mv[:], 1.0).then_inc(cleared, 1)
                dve.wait_ge(cleared, 1)
                adds = marks = 0
                for n in range(TURNS):
                    p = n % 2
                    if n:
                        dve.wait_ge(mm_done, n)
                    if on(n, 0) and n % TPB == 0:
                        dve.wait_ge(at_in[n // TPB], 32 * TPB)
                    src = [(0, at[:, n, :] if on(n, 0) else None), (2, bank[2 + p][:, 0:HD]), (4, None)]
                    if on(n, 4):
                        i = n - 4
                        nc.vector.tensor_tensor(xt[:, i, :], xt[:, i, :], bank[4 + p][:, 0:D], ALU.add).then_inc(added, 1)
                        adds += 1
                        dve.wait_ge(added, adds)
                        src[2] = (4, xt[:, i, :])
                    for k, (s, v) in enumerate(src):
                        if on(n, s):
                            nc.vector.bn_stats(st[:, k, :], v).then_inc(stats, 1)
                            marks += 1
                    dve.wait_ge(stats, marks)
                    last = [k for k, (s, v) in enumerate(src) if on(n, s)]
                    for k in last:
                        ins = nc.vector.bn_aggr(mv[:, p, k, :], st[:, k, :])
                    if last:
                        ins.then_inc(var_done, 1)
                    else:
                        nc.vector.memset(mv[:, p, 0, :], 1.0).then_inc(var_done, 1)
                    dve.wait_ge(std_done, n + 1)
                    nc.vector.reciprocal(rs[:, p, :], std[:, p, :]).then_inc(rs_done, 1)
                    dve.wait_ge(rs_done, n + 1)
                    dst = (yn[:, p, :], y2[:, p, :], xn1[:, n - 4, :] if on(n, 4) else None)
                    ins = None
                    for k, (s, v) in enumerate(src):
                        if on(n, s):
                            ins = nc.vector.tensor_scalar(dst[k], v, mv[:, p, k, 0:1], rs[:, p, k:k + 1], ALU.subtract, ALU.mult)
                    if ins is None:
                        ins = nc.vector.memset(yn[:, p, :], 0.0)
                    ins.then_inc(norm_done, 1)

            @block.scalar
            def _(act):
                for n in range(TURNS):
                    p = n % 2
                    if n:
                        act.wait_ge(tr_mm, n)
                        ins = None
                        if on(n, 1):
                            ins = nc.scalar.activation(tT[:, p, 0, :], bank[p][:, 0:HD], ACT.Copy)
                        if on(n, 3):
                            ins = nc.scalar.activation(tT[:, p, 1, :], bank[p][:, HD:2 * HD], ACT.Copy)
                        if on(n, 5):
                            i = n - 5
                            ins = nc.scalar.activation(xn1T[:, i * P:(i + 1) * P], bank[6 + p][:, 0:P], ACT.Copy)
                        if ins is not None:
                            ins.then_inc(cp_done, 1)
                        else:
                            act.sem_inc(cp_done, 1)
                    act.wait_ge(var_done, n + 1)
                    nc.scalar.activation(std[:, p, :], mv[:, p, :, 1], ACT.Sqrt, bias=con("eps5")).then_inc(std_done, 1)

            @block.tensor
            def _(pe):
                for n in range(1, TURNS):
                    p = n % 2
                    if n >= 2:
                        pe.wait_ge(cp_done, n - 1)
                    ins = None
                    if on(n, 2):
                        dst = bank[2 + p][:, 0:HD]
                        nc.tensor.matmul(dst, con("ones", 1), wo_bias[:], start=True, stop=False)
                        for k in range(2):
                            ins = nc.tensor.matmul(dst, tT[:, 1 - p, 0, k * P:(k + 1) * P], wo[:, k, :], start=False, stop=(k == 1))
                    if on(n, 4):
                        i = n - 4
                        dst = bank[4 + p][:, 0:D]
                        nc.tensor.matmul(dst, con("ones", 1), up_bias[:], start=True, stop=False)
                        nc.tensor.matmul(dst, ffnT[:, i * P:(i + 1) * P], con("ident"), start=False, stop=False)
                        for k in range(2):
                            ins = nc.tensor.matmul(dst, tT[:, 1 - p, 1, k * P:(k + 1) * P], up[:, k, :], start=False, stop=(k == 1))
                    if ins is not None:
                        ins.then_inc(mm_done, 1)
                    else:
                        pe.sem_inc(mm_done, 1)
                    pe.wait_ge(norm_done, n)
                    ins = None
                    if on(n, 1):
                        for k in range(2):
                            ins = nc.tensor.transpose(bank[p][:, k * P:(k + 1) * P], yn[:, 1 - p, k * P:(k + 1) * P], con("ident"))
                    if on(n, 3):
                        for k in range(2):
                            ins = nc.tensor.transpose(bank[p][:, HD + k * P:HD + (k + 1) * P], y2[:, 1 - p, k * P:(k + 1) * P], con("ident"))
                    if on(n, 5):
                        ins = nc.tensor.transpose(bank[6 + p][:, 0:P], xn1[:, n - 5, :], con("ident"))
                    if ins is not None:
                        ins.then_inc(tr_mm, 1)
                    else:
                        pe.sem_inc(tr_mm, 1)


def layer1(nc, a, out, g):
    sb, sem, con, bank = g["sb"], g["sem"], g["con"], g["bank"]
    xt, xn1, xn1T = g["xt"], g["xn1"], g["xn1T"]
    A = lambda n: a["L1_attn_" + n]
    with ExitStack() as c:
        wT = sb("wT", [P, 3, HD], c=c)
        w_outT = sb("w_outT", [P, 2, D], c=c)
        out_b = sb("out_b", [1, D], c=c)
        uT = sb("uT", [P, 2, TOK], c=c)
        yT = uT
        dts = sb("dts", [P, 2, 2, B], c=c)
        lng, lnb = sb("lng", [P, D], c=c), sb("lnb", [P, D], c=c)
        a_raw, b_ssm, c_ssm = (sb(n, [P, 2, NS], c=c) for n in ("a_raw", "b_ssm", "c_ssm"))
        experts(nc, a, g)
        mixer_in(nc, a, g, locals())
        mixer(nc, a, g, locals())
        final(nc, a, out, g, locals())


def experts(nc, a, g):
    sb, sem, con, bank = g["sb"], g["sem"], g["con"], g["bank"]
    xt, xn1T = g["xt"], g["xn1T"]
    M = lambda n: a["L1_ffn_" + n]
    with ExitStack() as c:
        gate_w, w1 = sb("gate_w", [P, NE], c=c), sb("w1e", [P, 4, P], c=c)
        w2, b1, b2 = sb("w2e", [P, 4, D], c=c), sb("b1e", [P, 4], c=c), sb("b2e", [NE, D], c=c)
        lg, ex, gt = (sb(n, [P, NT, NE], c=c) for n in ("lg", "ex", "gt"))
        mx, sm, top = sb("mx", [P, NT], c=c), sb("sm", [P, NT], c=c), sb("top", [P, NT, 8], c=c)
        idx, idf = sb("idx", [P, NT, 8], U32, c=c), sb("idf", [P, NT, 8], c=c)
        gT = sb("gT", [NE, TOK], c=c)
        he, hg = sb("he", [P, 2, 512], c=c), sb("hg", [P, 4, 512], c=c)
        w_in, gate_mm, ex_done, gates_done, gt_mm, gT_done = (sem(n, c) for n in ("moe_w", "gate_mm", "ex_done", "gates_done", "gt_mm", "gT_done"))
        up_mm, pick_mm, he_done, hg_done, down_mm, y_done = (sem(n, c) for n in ("e_up", "e_pick", "he_done", "hg_done", "e_down", "y_done"))
        mx_done, order = sem("mx_done", c), sem("moe_order", c)
        with nc.Block() as block:
            @block.sync
            def _(sp):
                sp.dma_start(gate_w[:], M("gate_w")).then_inc(w_in, 16)
                for q in range(4):
                    sp.dma_start(w1[:, q, :].rearrange("d (e h) -> d e h", e=2),
                                 M("w1")[2 * q:2 * q + 2].rearrange("e d h -> d e h")).then_inc(w_in, 16)
                sp.dma_start(w2[:], M("w2").rearrange("(q e) h d -> (e h) q d", q=4)).then_inc(w_in, 16)
                sp.dma_start(b1[:], M("b1").rearrange("(q e) h -> (e h) q", q=4)).then_inc(w_in, 16)
                sp.dma_start(b2[:], M("b2")).then_inc(w_in, 16)

            @block.tensor
            def _(pe):
                pe.wait_ge(w_in, 16 * 8)
                for i in range(NT):
                    mm = nc.tensor.matmul(bank[7][:, i * NE:(i + 1) * NE], xn1T[:, i * P:(i + 1) * P], gate_w[:], start=True, stop=True)
                mm.then_inc(gate_mm, 1)
                pe.wait_ge(gates_done, 1)
                for i in range(NT):
                    if i >= 4:
                        pe.wait_ge(gT_done, i // 4)
                    mm = nc.tensor.transpose(bank[6][0:NE, (i % 4) * P:(i % 4 + 1) * P], gt[:, i, :], con("ident"))
                    if i % 4 == 3:
                        mm.then_inc(gt_mm, 1)
                pe.wait_ge(gT_done, 4)
                for t in range(4):
                    tok = slice(t * 512, t * 512 + 512)
                    for q in range(4):
                        n = 4 * t + q
                        if n >= 2:
                            pe.wait_ge(hg_done, n - 1)
                        nc.tensor.matmul(bank[n % 2][:, :], w1[:, q, :], xn1T[:, tok], start=True, stop=True).then_inc(up_mm, 1)
                        nc.tensor.matmul(bank[2 + n % 2][:, :], con("pick", NE)[:, q * P:(q + 1) * P], gT[:, tok],
                                         start=True, stop=True).then_inc(pick_mm, 1)
                    pe.wait_ge(hg_done, 4 * t + 4)
                    if t >= 2:
                        pe.wait_ge(y_done, 4 * (t - 1))
                    for i in range(4):
                        dst = bank[4 + t % 2][:, i * P:(i + 1) * P]
                        nc.tensor.matmul(dst, gT[:, t * 512 + i * P:t * 512 + (i + 1) * P], b2[:], start=True, stop=False)
                        for q in range(4):
                            mm = nc.tensor.matmul(dst, hg[:, q, i * P:(i + 1) * P], w2[:, q, :], start=False, stop=(q == 3))
                    mm.then_inc(down_mm, 1)

            @block.scalar
            def _(act):
                act.wait_ge(mx_done, 1)
                nc.scalar.activation(ex[:], lg[:], ACT.Exp).then_inc(ex_done, 1)
                for t in range(4):
                    for q in range(4):
                        n = 4 * t + q
                        act.wait_ge(up_mm, n + 1)
                        if n >= 2:
                            act.wait_ge(hg_done, n - 1)
                        nc.scalar.activation(he[:, n % 2, :], bank[n % 2][:, :], ACT.Gelu, bias=b1[:, q:q + 1]).then_inc(he_done, 1)

            @block.vector
            def _(dve):
                ch = Chain(dve, order)
                wide = lambda v: v[:, :, None].broadcast_to([P, NT, NE])
                dve.wait_ge(gate_mm, 1)
                logits = bank[7][:, 0:NT * NE].rearrange("p (i e) -> p i e", e=NE)
                ch.link(nc.vector.tensor_reduce(mx[:], logits, AX, ALU.max))
                nc.vector.tensor_tensor(lg[:], logits, wide(mx[:, :]), ALU.subtract).then_inc(mx_done, 1)
                dve.wait_ge(ex_done, 1)
                ch.link(nc.vector.tensor_reduce(sm[:], ex[:], AX, ALU.add))
                ch.link(nc.vector.reciprocal(sm[:], sm[:]))
                ch.link(nc.vector.tensor_tensor(ex[:], ex[:], wide(sm[:, :]), ALU.mult))
                for i in range(NT):
                    ch.mark(nc.vector.max(top[:, i, :], ex[:, i, :]))
                dve.wait_ge(order, ch.n)
                for i in range(NT):
                    ch.mark(nc.vector.max_index(idx[:, i, :], top[:, i, :], ex[:, i, :]))
                dve.wait_ge(order, ch.n)
                ch.link(nc.vector.tensor_copy(idf[:], idx[:]))
                iota = con("iota8")[:, None, :].broadcast_to([P, NT, NE])
                ch.mark(nc.vector.tensor_tensor(lg[:], iota, idf[:, :, 0:1].broadcast_to([P, NT, NE]), ALU.is_equal))
                ch.mark(nc.vector.tensor_tensor(gt[:], iota, idf[:, :, 1:2].broadcast_to([P, NT, NE]), ALU.is_equal))
                ch.link(nc.vector.tensor_tensor(sm[:], top[:, :, 0], top[:, :, 1], ALU.add))
                ch.link(nc.vector.tensor_tensor(gt[:], gt[:], lg[:], ALU.add))
                nc.vector.tensor_tensor(gt[:], gt[:], wide(sm[:, :]), ALU.mult).then_inc(gates_done, 1)
                for k in range(4):
                    dve.wait_ge(gt_mm, k + 1)
                    nc.vector.tensor_copy(gT[:, k * 512:(k + 1) * 512], bank[6][0:NE, :]).then_inc(gT_done, 1)
                for t in range(4):
                    for q in range(4):
                        n = 4 * t + q
                        dve.wait_ge(he_done, n + 1)
                        dve.wait_ge(pick_mm, n + 1)
                        if t:
                            dve.wait_ge(down_mm, t)
                        nc.vector.tensor_tensor(hg[:, q, :], he[:, n % 2, :], bank[2 + n % 2][:, :], ALU.mult).then_inc(hg_done, 1)
                    dve.wait_ge(down_mm, t + 1)
                    rows = xt[:, 4 * t:4 * t + 4, :].rearrange("p i d -> p (i d)")
                    nc.vector.tensor_tensor(rows, rows, bank[4 + t % 2][:, :], ALU.add).then_inc(y_done, 4)


def mixer_in(nc, a, g, l):
    sb, sem, con, bank = g["sb"], g["sem"], g["con"], g["bank"]
    xn1T, wT, w_outT, out_b, uT, dts = g["xn1T"], l["wT"], l["w_outT"], l["out_b"], l["uT"], l["dts"]
    A = l["A"]
    with ExitStack() as c:
        raw, raw_o = sb("raw", [P, 3, 2, D], c=c), sb("raw_o", [P, HD], c=c)
        bx, bg, bd, cb = (sb(n, [P, 2], c=c) for n in ("bx", "bg", "bd", "cb"))
        cw = sb("cw", [P, 2, 3], c=c)
        ub = sb("ub", [P, 2, L + 2], c=c)
        gate = sb("gate", [P, 2, L], c=c)
        c1, c2, c3, df = (sb(n, [P, 2, L], c=c) for n in ("c1", "c2", "c3", "df"))
        ab, rl = sb("ab", [P, 2 * B, L], c=c), sb("rl", [P, L], c=c)
        w_in, w_mm, w_done, pads = (sem(n, c) for n in ("mix_w", "mix_tr", "mix_cp", "pads"))
        u_mm, g_mm, dt_mm = sem("u_mm", c), sem("g_mm", c), sem("dt_mm", c)
        u_done, gate_done, conv_done, diff_done, gd_done, uT_done = (
            sem(n, c) for n in ("u_done", "gate_done", "conv_done", "diff_done", "gated_done", "uT_done"))
        abs_done, relu_done, exp_done, ln_done, order = (sem(n, c) for n in ("abs_done", "relu_done", "exp_done", "ln_done", "mix_order"))
        with nc.Block() as block:
            @block.sync
            def _(sp):
                for n, name in enumerate(("W_x", "W_g", "W_dt")):
                    sp.dma_start(raw[:, n, :, :], A(name).rearrange("(k p) d -> p k d", k=2)).then_inc(w_in, 16)
                sp.dma_start(raw_o[:], A("W_out")).then_inc(w_in, 16)
                for dst, name in ((bx, "b_x"), (bg, "b_g"), (bd, "b_dt"), (cb, "conv_b")):
                    sp.dma_start(dst[:], A(name).rearrange("(k p) -> p k", k=2)).then_inc(w_in, 16)
                sp.dma_start(cw[:], A("conv_w").rearrange("(k p) o w -> p k (o w)", k=2)).then_inc(w_in, 16)
                sp.dma_start(out_b[:], A("b_out").rearrange("(o d) -> o d", o=1)).then_inc(w_in, 16)
                for dst, name in ((l["lng"], "ln_g"), (l["lnb"], "ln_b")):
                    sp.dma_start(dst[:], A(name).partition_broadcast(P)).then_inc(w_in, 16)
                for dst, name in ((l["a_raw"], "A_raw"), (l["b_ssm"], "B_ssm"), (l["c_ssm"], "C_ssm")):
                    sp.dma_start(dst[:], A(name).rearrange("(k p) s -> p k s", k=2)).then_inc(w_in, 16)

            @block.tensor
            def _(pe):
                pe.wait_ge(w_in, 16 * 15)
                for n in range(4):
                    for k in range(2):
                        src = raw[:, n, k, :] if n < 3 else raw_o[:, k * P:(k + 1) * P]
                        mm = nc.tensor.transpose(bank[n][:, k * P:(k + 1) * P], src, con("ident"))
                    mm.then_inc(w_mm, 1)
                pe.wait_ge(w_done, 4)
                for n in range(2 * B):
                    b, k = divmod(n, 2)
                    if n >= 2:
                        pe.wait_ge(u_done, n - 1)
                    nc.tensor.matmul(bank[n % 2][:, :], wT[:, 0, k * P:(k + 1) * P], xn1T[:, b * L:(b + 1) * L],
                                     start=True, stop=True).then_inc(u_mm, 1)
                    if n >= 2:
                        pe.wait_ge(gate_done, n - 1)
                    nc.tensor.matmul(bank[2 + n % 2][:, :], wT[:, 1, k * P:(k + 1) * P], xn1T[:, b * L:(b + 1) * L],
                                     start=True, stop=True).then_inc(g_mm, 1)
                for n in range(2 * B):
                    b, k = divmod(n, 2)
                    if n >= 4:
                        pe.wait_ge(relu_done, n - 3)
                    nc.tensor.matmul(bank[4 + n % 4][:, :], wT[:, 2, k * P:(k + 1) * P], xn1T[:, b * L:(b + 1) * L],
                                     start=True, stop=True).then_inc(dt_mm, 1)

            @block.scalar
            def _(act):
                for n in range(4):
                    act.wait_ge(w_mm, n + 1)
                    dst = wT[:, n, :] if n < 3 else w_outT[:].rearrange("p k d -> p (k d)")
                    nc.scalar.activation(dst, bank[n][:, 0:HD], ACT.Copy).then_inc(w_done, 1)
                act.wait_ge(pads, 1)
                for n in range(2 * B):
                    k = n % 2
                    act.wait_ge(u_mm, n + 1)
                    if n >= 2:
                        act.wait_ge(conv_done, 3 * (n - 1))
                        act.wait_ge(diff_done, n - 1)
                    nc.scalar.activation(ub[:, n % 2, 1:L + 1], bank[n % 2][:, :], ACT.Identity, bias=bx[:, k:k + 1]).then_inc(u_done, 1)
                    act.wait_ge(g_mm, n + 1)
                    if n >= 2:
                        act.wait_ge(gd_done, n - 1)
                    nc.scalar.activation(gate[:, n % 2, :], bank[2 + n % 2][:, :], ACT.Sigmoid, bias=bg[:, k:k + 1]).then_inc(gate_done, 1)
                for n in range(2 * B):
                    b, k = divmod(n, 2)
                    act.wait_ge(dt_mm, n + 1)
                    nc.scalar.activation(ab[:, n, :], bank[4 + n % 4][:, :], ACT.Abs, bias=bd[:, k:k + 1]).then_inc(abs_done, 1)
                    if n:
                        act.wait_ge(relu_done, n)
                    nc.scalar.activation(rl[:], bank[4 + n % 4][:, :], ACT.Relu, bias=bd[:, k:k + 1],
                                         accum_out=dts[:, 0, k, b:b + 1]).then_inc(relu_done, 1)
                for n in range(2 * B):
                    act.wait_ge(abs_done, n + 1)
                    nc.scalar.activation(ab[:, n, :], ab[:, n, :], ACT.Exp, scale=-1.0).then_inc(exp_done, 1)
                for n in range(2 * B):
                    b, k = divmod(n, 2)
                    act.wait_ge(exp_done, n + 1)
                    if n:
                        act.wait_ge(ln_done, n)
                    else:
                        act.wait_ge(relu_done, 2 * B)
                    nc.scalar.activation(rl[:], ab[:, n, :], ACT.Ln, bias=1.0, accum_out=dts[:, 1, k, b:b + 1]).then_inc(ln_done, 1)

            def blend(n):
                b, k = divmod(n, 2)
                nc.vector.wait_ge(gd_done, n + 1)
                nc.vector.tensor_tensor(uT[:, k, b * L:(b + 1) * L], c3[:, n % 2, :], df[:, n % 2, :], ALU.add).then_inc(uT_done, 1)

            @block.vector
            def _(dve):
                nc.vector.memset(ub[:], 0.0).then_inc(pads, 1)
                dve.wait_ge(w_in, 16 * 15)
                for n in range(2 * B):
                    b, k = divmod(n, 2)
                    p = n % 2
                    dve.wait_ge(u_done, n + 1)
                    if n >= 2:
                        dve.wait_ge(uT_done, n - 1)
                    nc.vector.tensor_scalar(c1[:, p, :], ub[:, p, 0:L], cw[:, k, 0:1], cb[:, k:k + 1], ALU.mult, ALU.add).then_inc(conv_done, 1)
                    dve.wait_ge(conv_done, 3 * n + 1)
                    nc.vector.scalar_tensor_tensor(out=c2[:, p, :], in0=ub[:, p, 1:L + 1], scalar=cw[:, k, 1:2], in1=c1[:, p, :],
                                                   op0=ALU.mult, op1=ALU.add).then_inc(conv_done, 1)
                    dve.wait_ge(conv_done, 3 * n + 2)
                    nc.vector.scalar_tensor_tensor(out=c3[:, p, :], in0=ub[:, p, 2:L + 2], scalar=cw[:, k, 2:3], in1=c2[:, p, :],
                                                   op0=ALU.mult, op1=ALU.add).then_inc(conv_done, 1)
                    if n:
                        blend(n - 1)
                blend(2 * B - 1)

            @block.gpsimd
            def _(pool):
                for n in range(2 * B):
                    p = n % 2
                    pool.wait_ge(conv_done, 3 * n + 3)
                    if n >= 2:
                        pool.wait_ge(uT_done, n - 1)
                    nc.gpsimd.tensor_tensor(df[:, p, :], ub[:, p, 1:L + 1], c3[:, p, :], ALU.subtract).then_inc(diff_done, 1)
                    pool.wait_ge(diff_done, n + 1)
                    pool.wait_ge(gate_done, n + 1)
                    nc.gpsimd.tensor_tensor(df[:, p, :], df[:, p, :], gate[:, p, :], ALU.mult).then_inc(gd_done, 1)


def mixer(nc, a, g, l):
    sb, sem, con, bank = g["sb"], g["sem"], g["con"], g["bank"]
    uT, yT, dts = l["uT"], l["yT"], l["dts"]
    a_raw, b_ssm, c_ssm = l["a_raw"], l["b_ssm"], l["c_ssm"]
    NBC = B * NCH
    lna_d = g["lna_d"]
    with ExitStack() as c:
        win = sb("win", [P, 2, NG, P], c=c)
        wst = sb("wst", [P, 2, NG, P], c=c)
        v = sb("v", [P, 2, NBC, NG], c=c)
        dt, t1 = sb("dt", [P, 2], c=c), sb("t1", [P, 2, NS], c=c)
        asp, bsp, lna, cbs = (sb(n, [P, 2, NS], c=c) for n in ("asp", "bsp", "lna", "cbs"))
        lnac, cbc = sb("lnac", [P, NG], c=c), sb("cbc", [P, NG], c=c)
        lnar = sb("lnar", [P, 2, NG, NS], c=c)
        kex = sb("kex", [P, 2, TC, NS], c=c)
        kpad = sb("kpad", [P, 2, 2 * TC], c=c)
        a32, d0 = sb("a32", [P, NG], c=c), sb("d0", [P, NG, B, NCH], c=c)
        order, aorder, porder = sem("ssm_v", c), sem("ssm_a", c), sem("ssm_p", c)
        lna_out, lna_in = sem("lna_out", c), sem("lna_in", c)
        with nc.Block() as block:
            @block.gpsimd
            def _(pool):
                nc.gpsimd.memset(win[:], 0.0).then_inc(porder, 1)
                nc.gpsimd.memset(d0[:], 0.0).then_inc(porder, 1)
                nc.gpsimd.memset(kpad[:], 0.0).then_inc(porder, 1)

            @block.vector
            def _(dve):
                ch = Chain(dve, order)
                w = ch.link
                w(nc.vector.tensor_tensor(dts[:, 0, :, :], dts[:, 0, :, :], dts[:, 1, :, :], ALU.add))
                w(nc.vector.tensor_reduce(dt[:], dts[:, 0, :, :], AX, ALU.add))
                w(nc.vector.tensor_scalar(dt[:], dt[:], 1.0 / TOK, 0.001, ALU.mult, ALU.max))
                w(nc.vector.tensor_scalar(dt[:], dt[:], 2.0, None, ALU.min))
                w(nc.vector.tensor_scalar(asp[:], a_raw[:], -1.0, None, ALU.mult))
                w(nc.vector.tensor_tensor(asp[:], asp[:], a_raw[:], ALU.max))
                dve.wait_ge(aorder, 2)
                w(nc.vector.tensor_scalar(bsp[:], a_raw[:], 0.0, None, ALU.max))
                w(nc.vector.tensor_tensor(asp[:], bsp[:], asp[:], ALU.add))
                w(nc.vector.tensor_scalar(asp[:], asp[:], -1.0, None, ALU.mult))
                w(nc.vector.tensor_tensor(lna[:], asp[:], dt[:, :, None].broadcast_to([P, 2, NS]), ALU.mult))
                w(nc.vector.tensor_scalar(asp[:], asp[:], 1e-6, None, ALU.add))
                w(nc.vector.reciprocal(asp[:], asp[:]))
                dve.wait_ge(aorder, 3)
                w(nc.vector.tensor_scalar(t1[:], t1[:], -1.0, None, ALU.add))
                w(nc.vector.tensor_tensor(t1[:], t1[:], asp[:], ALU.mult))
                w(nc.vector.tensor_tensor(t1[:], t1[:], b_ssm[:], ALU.mult))
                w(nc.vector.tensor_tensor(cbs[:], t1[:], c_ssm[:], ALU.mult))
                w(nc.vector.transpose(lnac[:], lna[:].rearrange("p k s -> p (k s)")))
                w(nc.vector.transpose(cbc[:], cbs[:].rearrange("p k s -> p (k s)")))
                for k in range(2):
                    w(nc.vector.tensor_tensor(kex[:, k, :, :], lna[:, k, None, :].broadcast_to([P, TC, NS]),
                                              con("ramp0")[:, :, None].broadcast_to([P, TC, NS]), ALU.mult))
                dve.wait_ge(aorder, 4)
                for k in range(2):
                    w(nc.vector.tensor_tensor(kex[:, k, :, :], kex[:, k, :, :], cbs[:, k, None, :].broadcast_to([P, TC, NS]), ALU.mult))
                dve.wait_ge(porder, 3)
                w(nc.vector.tensor_reduce(kpad[:, :, TC:2 * TC], kex[:], AX, ALU.add))
                for k in range(2):
                    w(nc.vector.transpose(v[:, k, :, :], uT[:, k, :].rearrange("p (n r) -> p n r", r=TC)))

            @block.scalar
            def _(act):
                act.wait_ge(order, 6)
                nc.scalar.activation(asp[:], asp[:], ACT.Exp, scale=-1.0).then_inc(aorder, 1)
                act.wait_ge(aorder, 1)
                nc.scalar.activation(asp[:], asp[:], ACT.Ln, bias=1.0).then_inc(aorder, 1)
                act.wait_ge(order, 10)
                nc.scalar.activation(t1[:], lna[:], ACT.Exp).then_inc(aorder, 1)
                act.wait_ge(order, 20)
                nc.scalar.activation(kex[:], kex[:], ACT.Exp).then_inc(aorder, 1)
                act.wait_ge(lna_in, 64)
                act.wait_ge(porder, 3)
                for q in range(4):
                    s = slice(32 * q, 32 * q + 32)
                    for k in range(2):
                        at = q * 32 + k * NS
                        nc.scalar.activation(win[s, k, :, at:at + NS], lnar[s, k, :, :], ACT.Exp,
                                             scale=con("expo")[s, :]).then_inc(aorder, 1)
                act.wait_ge(order, 17)
                nc.scalar.activation(a32[:], lnac[:], ACT.Exp, scale=float(TC)).then_inc(aorder, 1)
                act.wait_ge(aorder, 13)
                nc.scalar.activation(d0[:, :, :, 1:NCH].rearrange("p j b c -> p j b c"),
                                     a32[:, :, None, None].broadcast_to([P, NG, B, NCH - 1]), ACT.Copy).then_inc(aorder, 1)

            @block.sync
            def _(sp):
                sp.wait_ge(order, 10)
                sp.dma_start(lna_d.rearrange("(k p) s -> p k s", k=2), lna[:]).then_inc(lna_out, 16)
                sp.wait_ge(lna_out, 16)
                for q in range(4):
                    src = lna_d.rearrange("(k q j) s -> q k j s", k=2, q=4)[q]
                    sp.dma_start(lnar[32 * q:32 * q + 32], src.partition_broadcast(32)).then_inc(lna_in, 16)

        ex2 = sb("ex2", [P, NG, TC], c=c)
        x2 = sb("x2", [P, 2, TC, NG], c=c)
        wexp, wtr, worder = sem("wexp", c), sem("wtr", c), sem("worder", c)
        with nc.Block() as block:
            @block.gpsimd
            def _(pool):
                nc.gpsimd.memset(wst[:], 0.0).then_inc(worder, 1)

            @block.vector
            def _(dve):
                ch = Chain(dve, wtr)
                ch.link(nc.vector.tensor_tensor(ex2[:], lnac[:, :, None].broadcast_to([P, NG, TC]),
                                                con("ramp1")[:, None, :].broadcast_to([P, NG, TC]), ALU.mult))
                for k in range(2):
                    w = kpad[:, k, :]
                    window = bass.AP(tensor=w.tensor, offset=w.offset + TC, ap=[list(w.ap[0]), [1, TC], [-1, TC]])
                    ch.mark(nc.vector.transpose(x2[:, k, :, :], window))
                dve.wait_ge(wexp, 1)
                ch.link(nc.vector.tensor_tensor(ex2[:], ex2[:], cbc[:, :, None].broadcast_to([P, NG, TC]), ALU.mult))
                dve.wait_ge(worder, 1)
                for q in range(4):
                    s = slice(32 * q, 32 * q + 32)
                    for k in range(2):
                        ch.mark(nc.vector.tensor_scalar(wst[s, k, :, 32 * q:32 * q + 32], ex2[s, :, :],
                                                        con("head")[s, k:k + 1], None, ALU.mult))

            @block.scalar
            def _(act):
                act.wait_ge(wtr, 1)
                nc.scalar.activation(ex2[:], ex2[:], ACT.Exp).then_inc(wexp, 1)

        wtap = sb("wtap", [P, NG, P], c=c)
        state = sb("state", [P, NG, B, NCH], c=c)
        ybuf = sb("ybuf", [P, NBC, NG], c=c)
        in_mm, scanned, y_mm, y_cp, y_tr, tap_clear, taps = (
            sem(n, c) for n in ("in_mm", "scanned", "y_mm", "y_cp", "y_tr", "tap_clear", "taps"))
        with nc.Block() as block:
            @block.gpsimd
            def _(pool):
                nc.gpsimd.memset(wtap[:], 0.0).then_inc(tap_clear, 1)

            @block.tensor
            def _(pe):
                for j in range(NG):
                    for k in range(2):
                        mm = nc.tensor.matmul(bank[j // 8][:, (j % 8) * NBC:(j % 8 + 1) * NBC], win[:, k, j, :],
                                              v[:, k, :, j], start=(k == 0), stop=(k == 1))
                    if j % 8 == 7:
                        mm.then_inc(in_mm, 1)
                for k in range(2):
                    pe.wait_ge(taps, 4 * (k + 1))
                    for m in range(4):
                        n = 4 * k + m
                        pe.wait_ge(scanned, m + 1)
                        if n >= 4:
                            pe.wait_ge(y_cp, n - 3)
                        dst = bank[4 + m][:, :].rearrange("p (j b c) -> p j b c", j=8, b=B)
                        for jj in range(8):
                            j = 8 * m + jj
                            nc.tensor.matmul(bank[4 + m][:, jj * NBC:(jj + 1) * NBC], wtap[:, j, :], v[:, k, :, j],
                                             start=True, stop=True)
                            mm = nc.tensor.matmul(dst[:, jj, :, 1:NCH], wst[:, k, j, :], state[:, j, :, 0:NCH - 1],
                                                  start=False, stop=True, skip_group_check=True)
                        mm.then_inc(y_mm, 1)

            @block.vector
            def _(dve):
                for m in range(4):
                    dve.wait_ge(in_mm, m + 1)
                    js = slice(8 * m, 8 * m + 8)
                    nc.vector.tensor_tensor_scan(state[:, js, :, :].rearrange("p j b c -> p (j b c)"),
                                                 d0[:, js, :, :].rearrange("p j b c -> p (j b c)"),
                                                 bank[m][:, :], 0.0, ALU.mult, ALU.add).then_inc(scanned, 1)
                for k in range(2):
                    for m in range(4):
                        n = 4 * k + m
                        dve.wait_ge(y_mm, n + 1)
                        if k:
                            dve.wait_ge(y_tr, 1)
                        nc.vector.tensor_copy(ybuf[:, :, 8 * m:8 * m + 8].rearrange("p n j -> p j n"),
                                              bank[4 + m][:, :].rearrange("p (j n) -> p j n", j=8)).then_inc(y_cp, 1)
                    dve.wait_ge(y_cp, 4 * k + 4)
                    nc.vector.transpose(yT[:, k, :].rearrange("p (n r) -> p n r", r=TC), ybuf[:]).then_inc(y_tr, 1)

            @block.scalar
            def _(act):
                act.wait_ge(tap_clear, 1)
                for k in range(2):
                    if k:
                        act.wait_ge(y_mm, 4)
                    for q in range(4):
                        s = slice(32 * q, 32 * q + 32)
                        nc.scalar.activation(wtap[s, :, 32 * q:32 * q + 32], x2[s, k, :, :].rearrange("p r j -> p j r"),
                                             ACT.Copy).then_inc(taps, 1)


def final(nc, a, out, g, l):
    sb, sem, con, bank = g["sb"], g["sem"], g["con"], g["bank"]
    xt, xn1, yT, w_outT, out_b, lng, lnb = g["xt"], g["xn1"], l["yT"], l["w_outT"], l["out_b"], l["lng"], l["lnb"]
    with ExitStack() as c:
        z, zg = sb("z", [P, NT, D], c=c), sb("zg", [P, NT, D], c=c)
        st, mv = sb("fst", [P, NT, 6], c=c), sb("fmv", [P, NT, 2], c=c)
        std, rs = sb("fstd", [P, NT], c=c), sb("frs", [P, NT], c=c)
        o_mm, z_done, st_done, var_done, std_done, rs_done, zn_done, zg_done, sum_done, xb_done, stored = (
            sem(n, c) for n in ("o_mm", "z_d", "fst_d", "fvar_d", "fstd_d", "frs_d", "zn_d", "zg_d", "sum_d", "xb_d", "stored"))
        with nc.Block() as block:
            @block.tensor
            def _(pe):
                for m in range(4):
                    for jj in range(4):
                        i = 4 * m + jj
                        dst = bank[m][:, jj * P:(jj + 1) * P]
                        nc.tensor.matmul(dst, con("ones", 1), out_b[:], start=True, stop=False)
                        for k in range(2):
                            mm = nc.tensor.matmul(dst, yT[:, k, i * P:(i + 1) * P], l["w_outT"][:, k, :], start=False, stop=(k == 1))
                    mm.then_inc(o_mm, 1)

            @block.vector
            def _(dve):
                for m in range(4):
                    ts = slice(4 * m, 4 * m + 4)
                    dve.wait_ge(o_mm, m + 1)
                    nc.vector.tensor_tensor(z[:, ts, :].rearrange("p i d -> p (i d)"), bank[m][:, :],
                                            xn1[:, ts, :].rearrange("p i d -> p (i d)"), ALU.add).then_inc(z_done, 1)
                    dve.wait_ge(z_done, m + 1)
                    for i in range(4 * m, 4 * m + 4):
                        nc.vector.bn_stats(st[:, i, :], z[:, i, :]).then_inc(st_done, 1)
                    dve.wait_ge(st_done, 4 * m + 4)
                    for i in range(4 * m, 4 * m + 4):
                        ins = nc.vector.bn_aggr(mv[:, i, :], st[:, i, :])
                    ins.then_inc(var_done, 1)
                for m in range(4):
                    ts = slice(4 * m, 4 * m + 4)
                    dve.wait_ge(std_done, m + 1)
                    nc.vector.reciprocal(rs[:, ts], std[:, ts]).then_inc(rs_done, 1)
                    dve.wait_ge(rs_done, m + 1)
                    for i in range(4 * m, 4 * m + 4):
                        nc.vector.tensor_scalar(z[:, i, :], z[:, i, :], mv[:, i, 0:1], rs[:, i:i + 1],
                                                ALU.subtract, ALU.mult).then_inc(zn_done, 1)
                    dve.wait_ge(zn_done, 4 * m + 4)
                    nc.vector.tensor_tensor(zg[:, ts, :], z[:, ts, :], lng[:, None, :].broadcast_to([P, 4, D]), ALU.mult).then_inc(zg_done, 1)
                    dve.wait_ge(zg_done, m + 1)
                    dve.wait_ge(xb_done, m + 1)
                    nc.vector.tensor_tensor(zg[:, ts, :], zg[:, ts, :], xt[:, ts, :], ALU.add).then_inc(sum_done, 1)

            @block.gpsimd
            def _(pool):
                for m in range(4):
                    ts = slice(4 * m, 4 * m + 4)
                    nc.gpsimd.tensor_tensor(xt[:, ts, :], xt[:, ts, :], lnb[:, None, :].broadcast_to([P, 4, D]), ALU.add).then_inc(xb_done, 1)

            @block.scalar
            def _(act):
                for m in range(4):
                    ts = slice(4 * m, 4 * m + 4)
                    act.wait_ge(var_done, m + 1)
                    nc.scalar.activation(std[:, ts], mv[:, ts, 1], ACT.Sqrt, bias=con("eps5")).then_inc(std_done, 1)

            @block.sync
            def _(sp):
                for m in range(4):
                    sp.wait_ge(sum_done, m + 1)
                    sp.dma_start(out[m].rearrange("(n p) d -> p n d", p=P), zg[:, 4 * m:4 * m + 4, :]).then_inc(stored, 16)
                sp.wait_ge(stored, 64)


_OUT = ((B, L, D), "float32")


def kernel(**inputs):
    import concourse.bacc as bacc
    from concourse.bass_utils import run_bass_kernel_spmd

    nc = bacc.Bacc("TRN2", target_bir_lowering=False, num_devices=1)
    arrays, aps = {}, {}
    for name, v in inputs.items():
        v = np.ascontiguousarray(v)
        arrays[f"in_{name}"] = v
        aps[name] = nc.dram_tensor(f"in_{name}", v.shape, mybir.dt.from_np(v.dtype), kind="ExternalInput").ap()
    arrays["in_constants"] = constants()
    const = nc.dram_tensor("in_constants", arrays["in_constants"].shape, F32, kind="ExternalInput").ap()
    out = nc.dram_tensor("out_0", _OUT[0], F32, kind="ExternalOutput").ap()
    build(nc, aps, const, out)
    r = run_bass_kernel_spmd(nc, [arrays], core_ids=[0])
    return r.results[0]["out_0"]
```

```python
from contextlib import ExitStack

import concourse.bass as bass
import numpy as np
from concourse import mybir

F32 = mybir.dt.float32
U32 = mybir.dt.uint32
ACT = mybir.ActivationFunctionType
ALU = mybir.AluOpType
AX = mybir.AxisListType.X

P = 128
B, L, D = 4, 512, 128
TOK = B * L
NT = TOK // P
TPB = L // P
H, F, K = 2, 128, 16
HD = H * F
STEPS = L // K
RING = 4
RC = 3 * F + 1
BW = 3 * K
NG = 32
TC = 32
NCH = L // TC
NS = 16
NE = 8
EH = 64

CONSTS = [("ident", P), ("twist", P), ("tri", P), ("blk", P), ("inv", P), ("head", 2), ("expo", 1),
          ("ramp1", TC), ("ramp0", TC), ("iota8", NE), ("pick", 4 * P), ("ones", P),
          ("eps6", 1), ("eps5", 1), ("headT", P)]


def constant_columns():
    at, n = {}, 0
    for name, width in CONSTS:
        at[name] = (n, n + width)
        n += width
    return at, n


def constants():
    at, n = constant_columns()
    c = np.zeros((P, n), np.float32)
    p, q = np.arange(P)[:, None], np.arange(P)[None, :]

    def put(name, v):
        a, b = at[name]
        c[:, a:b] = v

    same = (p // K) == (q // K)
    put("ident", p == q)
    tw = np.zeros((P, P))
    for dst, src, sign in ((0, 2, 1), (1, 3, -1), (2, 0, -1), (3, 1, 1)):
        for i in range(32):
            tw[32 * src + i, 32 * dst + i] = sign
    put("twist", tw)
    put("tri", same & (p <= q))
    put("blk", same)
    put("inv", 1.0 / (q % K + 1) + 0.0 * p)
    put("head", (p // K) % H == np.arange(H)[None, :])
    put("expo", TC - 1 - p % TC)
    put("ramp1", np.arange(1, TC + 1)[None, :] + 0.0 * p)
    put("ramp0", np.arange(TC)[None, :] + 0.0 * p)
    put("iota8", np.arange(NE)[None, :] + 0.0 * p)
    pick = np.zeros((P, 4, P))
    for e in range(NE):
        pick[e, e // 2, EH * (e % 2):EH * (e % 2) + EH] = 1
    put("pick", pick.reshape(P, -1))
    put("ones", 1.0)
    put("eps6", 1e-6)
    put("eps5", 1e-5)
    put("headT", (q // K) % H == p)
    return c


class Chain:

    def __init__(self, eng, sem):
        self.eng, self.sem, self.n = eng, sem, 0

    def mark(self, ins):
        self.n += 1
        ins.then_inc(self.sem, 1)

    def link(self, ins):
        self.mark(ins)
        self.eng.wait_ge(self.sem, self.n)


def build(nc, a, const, out):
    ctx = ExitStack()
    with ctx, nc.allow_non_contiguous_dma(reason="bias columns and token regrouping"):
        at, ncol = constant_columns()
        taken = set()

        def unique(name):
            while name in taken:
                name += "_"
            taken.add(name)
            return name

        def sb(name, shape, dt=F32, c=ctx):
            return c.enter_context(nc.sbuf_tensor(unique(name), shape, dt))

        def sem(name, c=ctx):
            return c.enter_context(nc.semaphore(unique(name)))

        bank = [ctx.enter_context(nc.psum_tensor(f"bank{i}", [P, 512], F32)) for i in range(8)]
        cst = sb("cst", [P, ncol])

        def con(name, rows=P):
            lo, hi = at[name]
            return cst[0:rows, lo:hi]

        rows_d = nc.dram_tensor("rows_scratch", (STEPS, B, H, K, RC + 3), F32).ap()
        attn_d = nc.dram_tensor("attn_scratch", (STEPS, B, H, K, F), F32).ap()

        xt = sb("xt", [P, NT, D])
        ffnT = sb("ffnT", [P, TOK])
        region1 = sb("region1", [P, 2 * B * L])
        take = lambda lo, n, rows=P: region1[0:rows, lo:lo + n]
        wo = take(4 * HD, 2 * HD).rearrange("p (k f) -> p k f", k=2)
        up = take(6 * HD, 2 * D).rearrange("p (k f) -> p k f", k=2)
        wo_bias = take(7 * HD, HD, 1)
        lna_d = nc.dram_tensor("lna_scratch", (HD, NS), F32).ap()

        layer0_in(nc, a, const, out, locals())
        xn1, xn1T = sb("xn1", [P, NT, D]), sb("xn1T", [P, TOK])
        m1 = Layer1(nc, sb, sem, ffnT, region1)
        with ExitStack() as until_layer1:
            att = sb("att", [P, NT, HD], c=until_layer1)
            at_in = [sem(f"at_in{q}", until_layer1) for q in range(TPB)]

            def load_quarter(eng, q):
                for b in range(B):
                    for h in range(H):
                        eng.dma_start(att[:, b * TPB + q, h * F:(h + 1) * F],
                                      attn_d[q * (P // K):(q + 1) * (P // K), b, h]).then_inc(at_in[q], 16)

            ttt(nc, a, locals())
            layer0_out(nc, a, locals())
        layer1(nc, a, out, locals())
    return nc


def layer0_in(nc, a, const, out, g):
    sb, sem, con, bank = g["sb"], g["sem"], g["con"], g["bank"]
    cst, xt, ffnT, rows_d = g["cst"], g["xt"], g["ffnT"], g["rows_d"]
    wo, wo_bias, up = g["wo"], g["wo_bias"], g["up"]
    with ExitStack() as c:
        xnT = sb("xnT", [P, TOK], c=c)
        hT = sb("hT", [P, 2, TOK], c=c)
        xn = sb("xn", [P, NT, D], c=c)
        down = sb("down", [P, HD], c=c)
        down_b = sb("down_b", [P, 2], c=c)
        w4 = sb("w4", [P, 2, H, RC], c=c)
        wv = sb("wv", [P, 2, HD], c=c)
        lrb = sb("lrb", [P, H], c=c)
        post_w, post_b = sb("post_w", [P, 2], c=c), sb("post_b", [P, 2], c=c)
        ln_w, ln_b = sb("ln_w", [P, 2], c=c), sb("ln_b", [P, 2], c=c)
        wo_raw, up_raw = sb("wo_raw", [P, 2, HD], c=c), sb("up_raw", [P, 2, D], c=c)
        upb_raw, up_bias = sb("upb_raw", [P, 1], c=c), sb("up_bias", [P, 1], c=c)
        cw1, cw2 = sb("cw1", [P, 128], c=c), sb("cw2", [P, 64], c=c)
        cw3d, cw4 = sb("cw3d", [P, 64], c=c), sb("cw4", [64, 1], c=c)
        cw4d = sb("cw4d", [64, 2, P], c=c)
        cb1, cb2d, cb3d = sb("cb1", [P, 1], c=c), sb("cb2d", [P, 1], c=c), sb("cb3d", [64, 1], c=c)
        cb4, gb3 = sb("cb4", [P, 1], c=c), sb("gb3", [P, 1], c=c)
        gw1, gw2, gw3 = sb("gw1", [P, 64], c=c), sb("gw2", [64, 32], c=c), sb("gw3", [32, 1], c=c)
        gw3r = sb("gw3r", [32, P], c=c)
        gb1, gb2 = sb("gb1", [64, 1], c=c), sb("gb2", [32, 1], c=c)
        arange = sb("arange", [P, 1], c=c)
        half_b4, half_gb3 = sb("half_b4", [P, 1], c=c), sb("half_gb3", [P, 1], c=c)
        stats, mv = sb("stats", [P, NT, 6], c=c), sb("mv", [P, NT, 2], c=c)
        std, rstd = sb("std", [P, NT], c=c), sb("rstd", [P, NT], c=c)

        x_in = [sem(f"x_in{b}", c) for b in range(B)]
        cst_in, down_in, proj_in, late_in = (sem(n, c) for n in ("cst_in", "down_in", "proj_in", "late_in"))
        stats_done, std_done, xn_done = sem("stats_done", c), sem("std_done", c), sem("xn_done", c)
        xnT_mm = sem("xnT_mm", c)
        v_chain, cleared = sem("v_chain", c), sem("in_cleared", c)
        bias_mm, w4_done = sem("bias_mm", c), sem("w4_done", c)
        loads = {down_in: 0, proj_in: 0, late_in: 0}

        def load(eng, group, dst, src):
            eng.dma_start(dst, src).then_inc(group, 16)
            loads[group] += 16

        col = lambda v, n: v.rearrange("(k p) -> p k", k=n)
        with nc.Block() as block:
            @block.sync
            def _(sp):
                sp.dma_start(cst[:], const).then_inc(cst_in, 16)
                for b in range(B):
                    sp.dma_start(xt[:, b * TPB:(b + 1) * TPB, :],
                                 a["L0_attn_x"][b].rearrange("(n p) d -> p n d", p=P)).then_inc(x_in[b], 16)
                for h in range(H):
                    hs = slice(h * F, h * F + F)
                    load(sp, proj_in, w4[:, :, h, 0:F], a["L0_attn_wk"][:, hs].rearrange("(k p) f -> p k f", k=2))
                    load(sp, proj_in, w4[:, :, h, 2 * F:3 * F], a["L0_attn_wq"][:, hs].rearrange("(k p) f -> p k f", k=2))
                    load(sp, proj_in, w4[:, :, h, 3 * F], col(a["L0_attn_lr_w"][h, 0], 2))
                load(sp, proj_in, wv[:], a["L0_attn_wv"].rearrange("(k p) f -> p k f", k=2))
                load(sp, proj_in, lrb[:], a["L0_attn_lr_b"].partition_broadcast(P))

            @block.scalar
            def _(act):
                load(act, down_in, down[:], a["L0_attn_down_w"])
                load(act, down_in, down_b[:], col(a["L0_attn_down_b"], 2))
                act.wait_ge(cst_in, 16)
                for b in range(B):
                    act.wait_ge(stats_done, b + 1)
                    s = slice(b * TPB, (b + 1) * TPB)
                    act.activation(std[:, s], mv[:, s, 1], ACT.Sqrt, bias=con("eps5")).then_inc(std_done, 1)

            @block.vector
            def _(dve):
                ch = Chain(dve, v_chain)
                nc.vector.memset(cw4d[:], 0.0).then_inc(cleared, 1)
                nc.vector.memset(cw3d[:], 0.0).then_inc(cleared, 1)
                dve.wait_ge(cleared, 2)
                for b in range(B):
                    dve.wait_ge(x_in[b], 16)
                    for i in range(b * TPB, (b + 1) * TPB):
                        ch.mark(nc.vector.bn_stats(stats[:, i, :], xt[:, i, :]))
                    dve.wait_ge(v_chain, ch.n)
                    for i in range(b * TPB, (b + 1) * TPB):
                        last = nc.vector.bn_aggr(mv[:, i, :], stats[:, i, :])
                        if i == (b + 1) * TPB - 1:
                            last.then_inc(stats_done, 1)
                        else:
                            ch.mark(last)
                    dve.wait_ge(stats_done, b + 1)
                for b in range(B):
                    s = slice(b * TPB, (b + 1) * TPB)
                    dve.wait_ge(std_done, b + 1)
                    ch.link(nc.vector.reciprocal(rstd[:, s], std[:, s]))
                    for i in range(b * TPB, (b + 1) * TPB):
                        nc.vector.tensor_scalar(xn[:, i, :], xt[:, i, :], mv[:, i, 0:1], rstd[:, i:i + 1],
                                                ALU.subtract, ALU.mult).then_inc(xn_done, 1)
                for b in range(B):
                    dve.wait_ge(xnT_mm, b + 1)
                    ch.mark(nc.vector.tensor_copy(xnT[:, b * L:(b + 1) * L], bank[b][:, :]))

            @block.tensor
            def _(pe):
                pe.wait_ge(cst_in, 16)
                for b in range(B):
                    pe.wait_ge(xn_done, TPB * (b + 1))
                    for i in range(TPB):
                        mm = nc.tensor.transpose(bank[b][:, i * P:(i + 1) * P], xn[:, b * TPB + i, :], con("ident"))
                    mm.then_inc(xnT_mm, 1)

        with ExitStack() as c1:
            sig = sb("sig", [P, 2, 512], c=c1)
            stage = sb("stage", [P, 2, H, RC], c=c1)
            down_mm, sig_done, hT_done = sem("down_mm", c1), sem("sig_done", c1), sem("hT_done", c1)
            proj_mm = [sem(f"proj_mm{h}", c1) for h in range(H)]
            lr_done = sem("lr_done", c1)
            stage_done = [sem(f"stage_done{h}", c1) for h in range(H)]
            stored = [sem(f"rows_stored{p}", c1) for p in range(2)]
            with nc.Block() as block:
                @block.sync
                def _(sp):
                    load(sp, late_in, wo_raw[:], a["L0_attn_wo"].rearrange("(k p) f -> p k f", k=2))
                    load(sp, late_in, up_raw[:], a["L0_attn_up_w"].rearrange("(k p) f -> p k f", k=2))
                    for dst, name in ((post_w, "post_w"), (post_b, "post_b"), (ln_w, "ln_w"), (ln_b, "ln_b")):
                        load(sp, late_in, dst[:], col(a["L0_attn_" + name], 2))
                    load(sp, late_in, upb_raw[:], a["L0_attn_up_b"].rearrange("(d o) -> d o", o=1))
                    for dst, name in ((cw1, "cn_w1"), (cw2, "cn_w2"), (gw1, "gc_w1"), (gw2, "gc_w2"), (gw3, "gc_w3")):
                        load(sp, late_in, dst[:], a["L0_ffn_" + name])
                    for k in range(2):
                        load(sp, late_in, cw3d[64 * k:64 * k + 64, 32 * k:32 * k + 32], a["L0_ffn_cn_w3"])
                        load(sp, late_in, cw4[32 * k:32 * k + 32, :], a["L0_ffn_cn_w4"])
                        for dst, name, m in ((cb2d, "cn_b2", 64), (cb3d, "cn_b3", 32)):
                            load(sp, late_in, dst[m * k:m * k + m, :], a["L0_ffn_" + name].rearrange("(p o) -> p o", o=1))
                    for dst, name in ((cb1, "cn_b1"), (gb1, "gc_b1"), (gb2, "gc_b2")):
                        load(sp, late_in, dst[:], a["L0_ffn_" + name].rearrange("(p o) -> p o", o=1))
                    for dst, name in ((cb4, "cn_b4"), (gb3, "gc_b3"), (arange, "adaptive_range")):
                        load(sp, late_in, dst[:], a["L0_ffn_" + name].partition_broadcast(P))
                    for i in range(NT):
                        b, t0 = i // TPB, (i % TPB) * (P // K)
                        sp.wait_ge(stage_done[0], i + 1)
                        sp.wait_ge(stage_done[1], i + 1)
                        sp.wait_ge(lr_done, 2 * (i + 1))
                        for h in range(H):
                            sp.dma_start(rows_d[t0:t0 + P // K, b, h, :, 0:RC],
                                         stage[:, i % 2, h, :]).then_inc(stored[i % 2], 16)
                    for p in range(2):
                        sp.wait_ge(stored[p], 32 * (NT // 2))

                @block.tensor
                def _(pe):
                    pe.wait_ge(down_in, loads[down_in])
                    for n in range(8):
                        t, m = divmod(n, 2)
                        if n >= 4:
                            pe.wait_ge(hT_done, n - 3)
                        nc.tensor.matmul(bank[n % 4][:, :], down[:, m * P:(m + 1) * P], xnT[:, t * 512:(t + 1) * 512],
                                         start=True, stop=True).then_inc(down_mm, 1)
                    for i in range(NT):
                        pe.wait_ge(hT_done, 8 if i // 4 == 3 else 2 * (i // 4) + 2)
                        if i == 0:
                            pe.wait_ge(hT_done, 4)
                            pe.wait_ge(w4_done, H)
                        for h in range(H):
                            if i >= 2:
                                pe.wait_ge(stage_done[h], i - 1)
                                pe.wait_ge(lr_done, 2 * (i - 1))
                            for k in range(2):
                                mm = nc.tensor.matmul(bank[4 + 2 * h + i % 2][:, 0:RC], hT[:, k, i * P:(i + 1) * P],
                                                      w4[:, k, h, :], start=(k == 0), stop=(k == 1))
                            mm.then_inc(proj_mm[h], 1)
                    pe.wait_ge(late_in, loads[late_in])
                    for k in range(2):
                        mm = nc.tensor.matmul(bank[0][0:1, 0:HD], post_b[:, k:k + 1], wo_raw[:, k, :],
                                              start=(k == 0), stop=(k == 1))
                    mm.then_inc(bias_mm, 1)
                    for k in range(2):
                        mm = nc.tensor.matmul(bank[1][0:D, 0:1], up_raw[:, k, :], ln_b[:, k:k + 1],
                                              start=(k == 0), stop=(k == 1))
                    mm.then_inc(bias_mm, 1)

                @block.scalar
                def _(act):
                    act.wait_ge(down_in, loads[down_in])
                    act.wait_ge(proj_in, loads[proj_in])
                    for n in range(8):
                        act.wait_ge(down_mm, n + 1)
                        if n >= 2:
                            act.wait_ge(hT_done, n - 1)
                        act.activation(sig[:, n % 2, :], bank[n % 4][:, :], ACT.Sigmoid,
                                       bias=down_b[:, n % 2:n % 2 + 1]).then_inc(sig_done, 1)
                    for i in range(NT):
                        act.wait_ge(proj_mm[0], i + 1)
                        if i >= 2:
                            act.wait_ge(stored[i % 2], 32 * (i // 2))
                        act.activation(stage[:, i % 2, 0, 0:3 * F], bank[4 + i % 2][:, 0:3 * F],
                                       ACT.Copy).then_inc(stage_done[0], 1)
                        for h in range(H):
                            if h == 1:
                                act.wait_ge(stage_done[1], i + 1)
                            act.activation(stage[:, i % 2, h, 3 * F:RC], bank[4 + 2 * h + i % 2][:, 3 * F:RC],
                                           ACT.Sigmoid, bias=lrb[:, h:h + 1]).then_inc(lr_done, 1)

                @block.vector
                def _(dve):
                    ch = Chain(dve, v_chain)
                    dve.wait_ge(down_in, loads[down_in])
                    for n in range(8):
                        t, m = divmod(n, 2)
                        dve.wait_ge(sig_done, n + 1)
                        if n == 2:
                            dve.wait_ge(proj_in, loads[proj_in])
                            for h in range(H):
                                nc.vector.tensor_tensor(w4[:, :, h, F:2 * F], w4[:, :, h, 0:F],
                                                        wv[:, :, h * F:h * F + F], ALU.subtract).then_inc(w4_done, 1)
                        nc.vector.scalar_tensor_tensor(out=hT[:, m, t * 512:(t + 1) * 512], in0=bank[n % 4][:, :],
                                                       scalar=down_b[:, m:m + 1], in1=sig[:, n % 2, :],
                                                       op0=ALU.add, op1=ALU.mult).then_inc(hT_done, 1)
                    for i in range(NT):
                        dve.wait_ge(proj_mm[1], i + 1)
                        if i >= 2:
                            dve.wait_ge(stored[i % 2], 32 * (i // 2))
                        nc.vector.tensor_copy(stage[:, i % 2, 1, 0:3 * F],
                                              bank[6 + i % 2][:, 0:3 * F]).then_inc(stage_done[1], 1)
                    dve.wait_ge(late_in, loads[late_in])
                    for k in range(2):
                        ch.mark(nc.vector.tensor_scalar(wo[:, k, :], wo_raw[:, k, :], post_w[:, k:k + 1], None, ALU.mult))
                        ch.mark(nc.vector.tensor_scalar(up[:, k, :], up_raw[:, k, :], ln_w[:, k:k + 1], None, ALU.mult))
                        s = slice(32 * k, 32 * k + 32)
                        ch.mark(nc.vector.tensor_copy(cw4d[s, k, :], cw4[s, 0:1].broadcast_to([32, P])))
                    ch.mark(nc.vector.tensor_copy(gw3r[:], gw3[:, 0:1].broadcast_to([32, P])))
                    ch.mark(nc.vector.tensor_scalar(half_b4[:], cb4[:], 0.5, None, ALU.mult))
                    ch.mark(nc.vector.tensor_scalar(half_gb3[:], gb3[:], 0.5, None, ALU.mult))
                    dve.wait_ge(bias_mm, 1)
                    ch.mark(nc.vector.tensor_copy(wo_bias, bank[0][0:1, 0:HD]))
                    dve.wait_ge(bias_mm, 2)
                    ch.mark(nc.vector.tensor_tensor(up_bias[:], bank[1][0:D, 0:1], upb_raw[:], ALU.add))

        with ExitStack() as c1:
            N = 512
            CYC = 3
            h1, h2 = sb("h1", [P, B, N], c=c1), sb("h2", [P, 2, N], c=c1)
            h3, tanh = sb("h3", [64, 2, N], c=c1), sb("tanh", [P, B, N], c=c1)
            coup, move, turn = sb("coup", [P, B, N], c=c1), sb("move", [P, 2, N], c=c1), sb("turn", [P, 2, N], c=c1)
            x1, tw0, tw1 = sb("x1", [P, TOK], c=c1), sb("tw0", [P, TOK], c=c1), sb("tw1", [P, TOK], c=c1)
            xs = (xnT, x1, xnT, ffnT)
            tws = (tw0, tw1, tw0)
            mean = sb("mean", [P, B], c=c1)
            g1, g2, gf = sb("g1", [64, B], c=c1), sb("g2", [32, B], c=c1), sb("gf", [P, B], c=c1)
            beta, alpha = sb("beta", [P, 1], c=c1), sb("alpha", [P, B], c=c1)
            mean_done, gc_mm, gc_act = sem("mean_done", c1), sem("gc_mm", c1), sem("gc_act", c1)
            layer_mm = [sem(f"cn_mm{n}", c1) for n in range(4)]
            layer_act = [sem(f"cn_act{n}", c1) for n in range(4)]
            twist_mm, twisted, coefs_done, coupled = (sem(n, c1) for n in ("twist_mm", "twisted", "coefs_done", "coupled"))
            moved, upd, turned, turn_done = (sem(n, c1) for n in ("moved", "upd", "turned", "turn_done"))
            vc = sem("vc", c1)
            cols = lambda b: slice(b * N, (b + 1) * N)
            with nc.Block() as block:
                wide = lambda b: bank[b]
                narrow = lambda pair: bank[4 + pair]

                @block.tensor
                def _(pe):
                    def first(cyc, b):
                        j = cyc * B + b
                        if cyc:
                            pe.wait_ge(upd, j - B + 1)
                            pe.wait_ge(layer_act[3], j - B + 1)
                        nc.tensor.matmul(wide(b)[:, :], cw1[:], xs[cyc][:, cols(b)], start=True, stop=True).then_inc(layer_mm[0], 1)

                    def second(cyc, b):
                        j, pair = cyc * B + b, b // 2
                        pe.wait_ge(layer_act[0], j + 1)
                        if cyc and b % 2 == 0:
                            pe.wait_ge(layer_act[2], 2 * (cyc - 1) + pair + 1)
                        at = 64 * (b % 2)
                        nc.tensor.matmul(narrow(pair)[at:at + 64, :], cw2[:], h1[:, b, :], start=True, stop=True).then_inc(layer_mm[1], 1)

                    def third(cyc, pair):
                        pe.wait_ge(layer_act[1], 2 * cyc + pair + 1)
                        nc.tensor.matmul(narrow(pair)[0:64, :], cw3d[:], h2[:, pair, :], start=True, stop=True).then_inc(layer_mm[2], 1)

                    def fourth(cyc, b):
                        pair = b // 2
                        pe.wait_ge(layer_act[2], 2 * cyc + pair + 1)
                        nc.tensor.matmul(wide(b)[:, :], cw4d[:, b % 2, :], h3[:, pair, :], start=True, stop=True).then_inc(layer_mm[3], 1)

                    for b in range(B):
                        first(0, b)
                    for b in range(B):
                        if b >= 2:
                            pe.wait_ge(twisted, b - 1)
                        nc.tensor.matmul(bank[6 + b % 2][:, :], con("twist"), xnT[:, cols(b)], start=True, stop=True).then_inc(twist_mm, 1)
                    pe.wait_ge(mean_done, 1)
                    pe.wait_ge(twisted, 3)
                    nc.tensor.matmul(bank[6][0:64, 0:B], gw1[:], mean[:], start=True, stop=True).then_inc(gc_mm, 1)
                    for b in range(2):
                        second(0, b)
                    pe.wait_ge(gc_act, 1)
                    nc.tensor.matmul(bank[6][0:32, 0:B], gw2[:], g1[:], start=True, stop=True).then_inc(gc_mm, 1)
                    for b in range(2, B):
                        second(0, b)
                    pe.wait_ge(gc_act, 2)
                    nc.tensor.matmul(bank[6][:, 0:B], gw3r[:], g2[:], start=True, stop=True).then_inc(gc_mm, 1)
                    for cyc in range(CYC):
                        third(cyc, 0)
                        third(cyc, 1)
                        for b in range(B):
                            fourth(cyc, b)
                        if cyc + 1 < CYC:
                            for b in range(2):
                                first(cyc + 1, b)
                            for b in range(2):
                                second(cyc + 1, b)
                            for b in range(2, B):
                                first(cyc + 1, b)
                            for b in range(2, B):
                                second(cyc + 1, b)

                @block.scalar
                def _(act):
                    def gelu(dst, src, bias, mm, count, done):
                        act.wait_ge(mm, count)
                        act.activation(dst, src, ACT.Gelu, bias=bias).then_inc(done, 1)

                    def hidden1(cyc, b):
                        gelu(h1[:, b, :], wide(b)[:, :], cb1[:], layer_mm[0], cyc * B + b + 1, layer_act[0])

                    def hidden2(cyc, pair):
                        gelu(h2[:, pair, :], narrow(pair)[:, :], cb2d[:], layer_mm[1], cyc * B + 2 * pair + 2, layer_act[1])

                    def hidden3(cyc, pair):
                        gelu(h3[:, pair, :], narrow(pair)[0:64, :], cb3d[:], layer_mm[2], 2 * cyc + pair + 1, layer_act[2])

                    def couple(cyc, b):
                        j = cyc * B + b
                        act.wait_ge(layer_mm[3], j + 1)
                        if cyc:
                            act.wait_ge(coupled, j - B + 1)
                        act.activation(tanh[:, b, :], wide(b)[:, :], ACT.Tanh, bias=half_b4[:], scale=0.5).then_inc(layer_act[3], 1)
                        act.wait_ge(layer_act[3], j + 1)
                        act.wait_ge(coefs_done, 1)
                        if cyc:
                            act.wait_ge(moved, j - B + 1)
                            act.wait_ge(turned, j - B + 1)
                        act.activation(coup[:, b, :], tanh[:, b, :], ACT.Identity, bias=alpha[:, b:b + 1],
                                       scale=beta[:, 0:1]).then_inc(coupled, 1)

                    for b in range(B):
                        hidden1(0, b)
                    act.wait_ge(twist_mm, 1)
                    for b in range(B):
                        act.wait_ge(twist_mm, b + 1)
                        act.activation(tw0[:, cols(b)], bank[6 + b % 2][:, :], ACT.Copy).then_inc(twisted, 1)
                    gelu(g1[:], bank[6][0:64, 0:B], gb1[:], gc_mm, 1, gc_act)
                    hidden2(0, 0)
                    gelu(g2[:], bank[6][0:32, 0:B], gb2[:], gc_mm, 2, gc_act)
                    hidden2(0, 1)
                    act.wait_ge(gc_mm, 3)
                    act.activation(gf[:], bank[6][:, 0:B], ACT.Tanh, bias=half_gb3[:], scale=0.5).then_inc(gc_act, 1)
                    for cyc in range(CYC):
                        for pair in range(2):
                            hidden3(cyc, pair)
                        for b in range(B):
                            couple(cyc, b)
                        if cyc + 1 < CYC:
                            for pair in range(2):
                                for b in (2 * pair, 2 * pair + 1):
                                    hidden1(cyc + 1, b)
                                hidden2(cyc + 1, pair)

                @block.vector
                def _(dve):
                    ch = Chain(dve, vc)
                    ch.link(nc.vector.tensor_reduce(mean[:], xnT[:, :].rearrange("p (b l) -> p b l", b=B), AX, ALU.add))
                    nc.vector.tensor_scalar(mean[:], mean[:], 1.0 / L, None, ALU.mult).then_inc(mean_done, 1)
                    ch.mark(nc.vector.tensor_scalar(beta[:], arange[:], 0.3, None, ALU.mult))
                    dve.wait_ge(gc_act, 3)
                    ch.link(nc.vector.tensor_scalar(alpha[:], gf[:], 0.7, None, ALU.mult))
                    nc.vector.tensor_scalar(alpha[:], alpha[:], arange[:, 0:1], 0.1, ALU.mult, ALU.add).then_inc(coefs_done, 1)
                    for cyc in range(CYC):
                        for b in range(B):
                            j = cyc * B + b
                            dve.wait_ge(coupled, j + 1)
                            if cyc:
                                dve.wait_ge(turn_done, j - B + 1)
                            else:
                                dve.wait_ge(twisted, b + 1)
                            nc.vector.tensor_tensor(move[:, b % 2, :], tws[cyc][:, cols(b)], coup[:, b, :],
                                                    ALU.mult).then_inc(moved, 1)
                            dve.wait_ge(moved, j + 1)
                            if cyc == 1:
                                dve.wait_ge(turned, b + 1)
                            if cyc + 1 < CYC:
                                ins = nc.vector.tensor_tensor(xs[cyc + 1][:, cols(b)], xs[cyc][:, cols(b)], move[:, b % 2, :], ALU.add)
                            else:
                                ins = nc.vector.scalar_tensor_tensor(out=ffnT[:, cols(b)], in0=xs[cyc][:, cols(b)],
                                                                     scalar=up_bias[:, 0:1], in1=move[:, b % 2, :],
                                                                     op0=ALU.add, op1=ALU.add)
                            ins.then_inc(upd, 1)

                @block.gpsimd
                def _(pool):
                    for cyc in range(CYC):
                        for b in range(B):
                            j = cyc * B + b
                            if cyc + 1 == CYC:
                                pool.sem_inc(turned, 1)
                                continue
                            pool.wait_ge(coupled, j + 1)
                            if cyc:
                                pool.wait_ge(upd, j - B + 1)
                            nc.gpsimd.tensor_tensor(turn[:, b % 2, :], xs[cyc][:, cols(b)], coup[:, b, :], ALU.mult).then_inc(turned, 1)
                            pool.wait_ge(turned, j + 1)
                            if cyc:
                                pool.wait_ge(moved, j - B + 1)
                            nc.gpsimd.tensor_tensor(tws[cyc + 1][:, cols(b)], tws[cyc][:, cols(b)], turn[:, b % 2, :],
                                                    ALU.subtract).then_inc(turn_done, 1)


def wait(eng, s, v):
    if not (isinstance(v, int) and v <= 0):
        eng.wait_ge(s, v)


def run_steps(eng, step):
    for t in range(RING):
        step(t, t)
    with eng.Fori(1, STEPS // RING - 1) as lap:
        for p in range(RING):
            step(lap * RING + p, p)
    for p in range(RING):
        step(STEPS - RING + p, p, left=RING - 1 - p)


def ttt(nc, a, g):
    sb, sem, con, bank = g["sb"], g["sem"], g["con"], g["bank"]
    rows_d, attn_d = g["rows_d"], g["attn_d"]
    zbanks, zbar_bank, prep_bank = bank[4:6], bank[6], bank[7]
    R2 = 2 * F
    SLOTS = B * H + 1
    first_slot = lambda b: 0 if b == 0 else b * H + 1
    width = lambda b: 3 if b == 0 else H
    with ExitStack() as c:
        rows = sb("rows", [P, RING, RC], c=c)
        kt, qt = sb("kt", [P, RING, B * BW], c=c), sb("qt", [P, RING, B * BW], c=c)
        kd = sb("kd", [P, 2, P], c=c)
        pm, pair = sb("pm", [P, 2, P], c=c), sb("pair", [P, 2, P], c=c)
        cc, xkm = sb("cc", [P, 2, F], c=c), sb("xkm", [P, 2, B * H, F], c=c)
        xqb, xg, ob = sb("xqb", [P, RING, F], c=c), sb("xg", [P, F], c=c), sb("ob", [P, 2, F], c=c)
        gd = sb("gd", [P, F], c=c)
        w_sb = sb("w_sb", [P, SLOTS, F], c=c)
        w0, w0c = sb("w0", [P, H, F], c=c), sb("w0c", [P, H, F], c=c)
        wmean = sb("wmean", [P, H], c=c)
        head_rows = sb("head_rows", [H, 3 * F], c=c)
        gr, gbr, g2, ggb, bias0 = (sb(n, [P, F], c=c) for n in ("gr", "gbr", "g2", "ggb", "bias0"))
        bmean = sb("bmean", [P, 1], c=c)
        tok, ti = sb("tok", [P, K], c=c), sb("ti", [P, K], c=c)
        tim, blkt = sb("tim", [P, P], c=c), sb("blkt", [P, P], c=c)
        st, mv, std = sb("zst", [P, 6], c=c), sb("zmv", [P, 2], c=c), sb("zstd", [P, 1], c=c)
        bst, bmv, bstd = sb("bst", [P, 6], c=c), sb("bmv", [P, 2], c=c), sb("bstd", [P, 1], c=c)
        r, rr, r2, brs = (sb(n, [P, 1], c=c) for n in ("zr", "zrr", "zr2", "brs"))
        m1s, m1, es, sc, shift = (sb(n, [P, 1], c=c) for n in ("m1s", "m1", "es", "sc", "shift"))
        pz, gy, junk, wz = (sb(n, [P, F], c=c) for n in ("pz", "gy", "junk", "wz"))
        grad, xhb = sb("grad", [P, 2, F], c=c), sb("xhb", [P, 2, F], c=c)

        ld, setup = sem("ttt_loads", c), sem("ttt_setup", c)
        head_mm, zeroed = sem("head_mm", c), sem("zeroed", c)
        rows_in = [sem(f"rows_in{p}", c) for p in range(RING)]
        ob_out = [sem(f"ob_out{p}", c) for p in range(2)]
        tr_mm, kt_done, gram_mm = (sem(n, c) for n in ("tr_mm", "kt_done", "gram_mm"))
        mask_done, pair_done = sem("mask_done", c), sem("pair_done", c)
        z_mm, var_done, std_done, grad_done = (sem(n, c) for n in ("z_mm", "var_done", "std_done", "grad_done"))
        upd_mm, zbar_mm, w_done = (sem(n, c) for n in ("upd_mm", "zbar_mm", "w_done"))
        bvar_done, bstd_done, xhb_done = (sem(n, c) for n in ("bvar_done", "bstd_done", "xhb_done"))
        bst_done, brs_done, shift_done = (sem(n, c) for n in ("bst_done", "brs_done", "shift_done"))
        cc_done, xkm_done, xqb_done, ob_done = (sem(n, c) for n in ("cc_done", "xkm_done", "xqb_done", "ob_done"))
        gd_done, xg_done, rr_done = sem("gd_done", c), sem("xg_done", c), sem("rr_done", c)
        v_order, waited = sem("v_order", c), sem("waited", c)

        with nc.Block() as block:
            @block.sync
            def _(sp):
                for n, name in enumerate(("ttt_ln_w", "ttt_ln_b")):
                    sp.dma_start(head_rows[:, n * F:(n + 1) * F], a["L0_attn_" + name]).then_inc(ld, 16)
                sp.dma_start(head_rows[:, 2 * F:3 * F], a["L0_attn_b1"].rearrange("h o f -> h (o f)")).then_inc(ld, 16)
                sp.dma_start(tok[:], a["L0_attn_tok_idx"].partition_broadcast(P)).then_inc(ld, 16)
                sp.dma_start(w0[:], a["L0_attn_W1"].rearrange("h f g -> f h g")).then_inc(ld, 16)
                for t in range(RING):
                    sp.dma_start(rows[:, t, :], rows_d[t].rearrange("b h j c -> (b h j) c")[:, 0:RC]).then_inc(rows_in[t], 16)

            @block.tensor
            def _(pe):
                pe.wait_ge(ld, 80)
                nc.tensor.matmul(prep_bank[:, 0:3 * F], con("headT", H), head_rows[:], start=True, stop=True).then_inc(head_mm, 1)

            @block.gpsimd
            def _(pool):
                nc.gpsimd.memset(kt[:], 0.0).then_inc(zeroed, 1)
                nc.gpsimd.memset(qt[:], 0.0).then_inc(zeroed, 1)

            @block.vector
            def _(dve):
                ch = Chain(dve, setup)
                dve.wait_ge(ld, 80)
                ch.link(nc.vector.tensor_tensor(ti[:], con("inv")[:, 0:K], tok[:], ALU.add))
                ch.link(nc.vector.tensor_scalar(ti[:], ti[:], 0.0, None, ALU.max))
                ch.mark(nc.vector.tensor_tensor(tim[:].rearrange("p (n k) -> p n k", k=K),
                                                con("tri").rearrange("p (n k) -> p n k", k=K),
                                                ti[:, None, :].broadcast_to([P, P // K, K]), ALU.mult))
                ch.mark(nc.vector.tensor_scalar(blkt[:], con("blk"), ti[:, K - 1:K], None, ALU.mult))
                ch.link(nc.vector.tensor_reduce(wmean[:], w0[:], AX, ALU.add))
                ch.link(nc.vector.tensor_scalar(wmean[:], wmean[:], 1.0 / F, None, ALU.mult))
                for h in range(H):
                    ch.mark(nc.vector.tensor_scalar(w0c[:, h, :], w0[:, h, :], wmean[:, h:h + 1], None, ALU.subtract))
                dve.wait_ge(head_mm, 1)
                ch.mark(nc.vector.tensor_copy(gr[:], prep_bank[:, 0:F]))
                ch.mark(nc.vector.tensor_copy(gbr[:], prep_bank[:, F:2 * F]))
                ch.link(nc.vector.tensor_reduce(bmean[:], prep_bank[:, 2 * F:3 * F], AX, ALU.add))
                ch.mark(nc.vector.tensor_tensor(g2[:], gr[:], gr[:], ALU.mult))
                ch.mark(nc.vector.tensor_tensor(ggb[:], gr[:], gbr[:], ALU.mult))
                ch.link(nc.vector.tensor_scalar(bmean[:], bmean[:], 1.0 / F, None, ALU.mult))
                ch.mark(nc.vector.tensor_scalar(bias0[:], prep_bank[:, 2 * F:3 * F], bmean[:, 0:1], None, ALU.subtract))

        with nc.Block() as block:
            @block.sync
            def _(sp):
                def flat(v):
                    if len(v.shape) == 5:
                        return v.rearrange("t b h j c -> (t b h j) c")
                    return v.rearrange("b h j c -> (b h j) c")

                at = lambda v, t: flat(v[t] if isinstance(t, int) else v[bass.ds(t, 1)])

                def load(s, p):
                    for used in (tr_mm, rr_done, xqb_done, xkm_done, gd_done):
                        wait(sp, used, s - RING + 1)
                    sp.dma_start(rows[:, p, :], at(rows_d, s)[:, 0:RC]).then_inc(rows_in[p], 16)

                def store(t, p):
                    sp.wait_ge(ob_done, t + 1)
                    sp.dma_start(at(attn_d, t), ob[:, p % 2, :]).then_inc(ob_out[p % 2], 16)

                def step(t, p, left=RING):
                    if left >= RING:
                        load(t + RING, p)
                    if not (isinstance(t, int) and t == 0):
                        store(t - 1, (p - 1) % RING)
                    if 0 < left < TPB:
                        if left == TPB - 1:
                            for parity in range(2):
                                sp.wait_ge(ob_out[parity], 16 * (STEPS - P // K) // 2)
                        g["load_quarter"](sp, TPB - 1 - left)

                run_steps(sp, step)
                store(STEPS - 1, RING - 1)
                for p in range(2):
                    sp.wait_ge(ob_out[p], 16 * STEPS // 2)

            @block.tensor
            def _(pe):
                def transposes(s, p):
                    pe.wait_ge(rows_in[p], 4 * s + (16 - 4 * p))
                    wait(pe, mask_done, s - 1)
                    wait(pe, pair_done, s - 1)
                    nc.tensor.transpose(prep_bank[:, 0:P], rows[:, p, 0:F], con("ident"))
                    nc.tensor.transpose(prep_bank[:, P:2 * P], rows[:, p, R2:3 * F], con("ident")).then_inc(tr_mm, 1)

                def grams(s, p, pairs=True):
                    dense = lambda v, q: v[:, q, :].rearrange("f (b k j) -> f b k j", b=B, k=3)[:, :, 0:3:2, :]
                    pe.wait_ge(kt_done, s + 2 if pairs else s + 1)
                    mm = nc.tensor.matmul(prep_bank[:, R2:R2 + P], kd[:, p % 2, :], dense(qt, p), start=True, stop=True)
                    if pairs:
                        mm = nc.tensor.matmul(prep_bank[:, R2 + P:R2 + 2 * P], kd[:, p % 2, :], dense(kt, (p + 1) % RING),
                                              start=True, stop=True)
                    mm.then_inc(gram_mm, 1)

                def base(dst, v, p, copied, last_stop=True):
                    pe.wait_ge(w_done, copied + 1)
                    nc.tensor.matmul(dst[:, 0:F], con("ident"), w_sb[:, 2, :], start=True, stop=False, skip_group_check=True)
                    for b in range(B):
                        pe.wait_ge(w_done, copied + b + 1)
                        for h in range(H):
                            at = b * BW + h * K
                            mm = nc.tensor.matmul(dst[32 * b:32 * b + 32, 0:F], v[:, p, at:at + 2 * K],
                                                  w_sb[:, first_slot(b) + h, :], start=False, stop=(h == 1), skip_group_check=True)
                    return mm

                def state_start(t, p, left=RING):
                    if left >= 2:
                        base(zbanks[p % 2], kt, (p + 2) % RING, 4 * (t + 1))
                    wait(pe, xhb_done, t + 1)
                    base(zbar_bank, qt, (p + 1) % RING, 4 * (t + 1))
                    if left >= 2:
                        grams(t + 2, (p + 2) % RING, pairs=left >= 3)

                def step(t, p, left=RING):
                    g_t = grad[:, p % 2, :]
                    pe.wait_ge(grad_done, t + 1)
                    pe.wait_ge(mask_done, t + 1)
                    if left:
                        pe.wait_ge(pair_done, t + 1)
                        nc.tensor.matmul(zbanks[(p + 1) % 2][:, 0:F], pair[:, p % 2, :], g_t, start=False, stop=True,
                                         skip_group_check=True).then_inc(z_mm, 1)
                    nc.tensor.matmul(zbar_bank[:, 0:F], pm[:, p % 2, :], g_t, start=False, stop=True,
                                     skip_group_check=True).then_inc(zbar_mm, 1)
                    if not left:
                        return
                    pe.wait_ge(xkm_done, t + 1)
                    nc.tensor.matmul(bank[0][:, 2 * F:3 * F], blkt[:], g_t, start=False, stop=False, skip_group_check=True)
                    for b in range(B):
                        for h in range(H):
                            mm = nc.tensor.matmul(bank[b][:, h * F:(h + 1) * F], xkm[:, p % 2, b * H + h, :], g_t,
                                                  start=False, stop=False, skip_group_check=True)
                        mm.then_inc(upd_mm, 1)
                        if b == 2 and left >= 3:
                            transposes(t + 3, (p + 3) % RING)
                    state_start(t, p, left)

                for b in range(B):
                    for h in range(H):
                        mm = nc.tensor.matmul(bank[b][:, h * F:(h + 1) * F], con("ident"), w0c[:, h, :],
                                              start=(h == 0), stop=False, skip_group_check=True)
                    if b == 0:
                        mm = nc.tensor.matmul(bank[0][:, 2 * F:3 * F], con("ident"), bias0[:], start=False, stop=False,
                                              skip_group_check=True)
                    mm.then_inc(upd_mm, 1)
                transposes(0, 0)
                pe.wait_ge(kt_done, 1)
                transposes(1, 1)
                base(zbanks[0], kt, 0, 0).then_inc(z_mm, 1)
                grams(0, 0)
                transposes(2, 2)
                state_start(-1, -1)
                run_steps(pe, step)

            @block.scalar
            def _(act):
                def prep(s, p):
                    act.wait_ge(tr_mm, s + 1)
                    for n, v in enumerate((kt, qt)):
                        nc.scalar.activation(v[:, p, :].rearrange("f (b k j) -> f b k j", b=B, k=3)[:, :, 0:3:2, :],
                                             prep_bank[:, n * P:(n + 1) * P].rearrange("f (b h j) -> f b h j", b=B, h=H),
                                             ACT.Copy)
                    nc.scalar.activation(kd[:, p % 2, :], prep_bank[:, 0:P], ACT.Copy).then_inc(kt_done, 1)

                def copy_state(t, b):
                    act.wait_ge(upd_mm, 4 * (t + 1) + b + 1)
                    at, n = first_slot(b), width(b)
                    nc.scalar.activation(w_sb[:, at:at + n, :], bank[b][:, 0:n * F].rearrange("f (h g) -> f h g", h=n),
                                         ACT.Copy).then_inc(w_done, 1)

                def z_deviation(s):
                    act.wait_ge(var_done, s + 1)
                    nc.scalar.activation(std[:], mv[:, 1:2], ACT.Sqrt, bias=con("eps6")).then_inc(std_done, 1)

                def step(t, p, left=RING):
                    if left:
                        z_deviation(t + 1)
                        copy_state(t, 0)
                        copy_state(t, 1)
                    act.wait_ge(bvar_done, t + 1)
                    nc.scalar.activation(bstd[:], bmv[:, 1:2], ACT.Sqrt, bias=con("eps6")).then_inc(bstd_done, 1)
                    if left:
                        copy_state(t, 2)
                        copy_state(t, 3)
                    act.wait_ge(shift_done, t + 1)
                    wait(act, xg_done, t - 1)
                    nc.scalar.activation(xhb[:, p % 2, :], zbar_bank[:, 0:F], ACT.Identity, bias=shift[:, 0:1],
                                         scale=brs[:, 0:1]).then_inc(xhb_done, 1)
                    if left >= 3:
                        prep(t + 3, (p + 3) % RING)

                act.wait_ge(zeroed, 2)
                prep(0, 0)
                for b in range(B):
                    copy_state(-1, b)
                prep(1, 1)
                prep(2, 2)
                z_deviation(0)
                run_steps(act, step)

            @block.gpsimd
            def _(pool):
                def prep(s, p):
                    pool.wait_ge(rows_in[p], 4 * s + (16 - 4 * p))
                    wait(pool, cc_done, s)
                    nc.gpsimd.tensor_tensor(gd[:], gr[:], rows[:, p, F:2 * F], ALU.mult).then_inc(gd_done, 1)
                    pool.wait_ge(gd_done, s + 1)
                    wait(pool, grad_done, s - 1)
                    nc.gpsimd.tensor_tensor(cc[:, p % 2, :], gd[:], ggb[:], ALU.add).then_inc(cc_done, 1)
                    wait(pool, ob_done, s - 3)
                    nc.gpsimd.tensor_tensor(xqb[:, p, :], rows[:, p, R2:3 * F], gbr[:], ALU.add).then_inc(xqb_done, 1)
                    wait(pool, upd_mm, 4 * s)
                    nc.gpsimd.tensor_tensor(xkm[:, p % 2, :, :], rows[:, p, 0:F][:, None, :].broadcast_to([P, B * H, F]),
                                            blkt[:, 0:P:K][:, :, None].broadcast_to([P, B * H, F]), ALU.mult).then_inc(xkm_done, 1)

                def output(t, p):
                    pool.wait_ge(xhb_done, t + 1)
                    wait(pool, ob_done, t)
                    nc.gpsimd.tensor_tensor(xg[:], xhb[:, p % 2, :], gr[:], ALU.mult).then_inc(xg_done, 1)
                    pool.wait_ge(xg_done, t + 1)
                    pool.wait_ge(xqb_done, t + 1)
                    wait(pool, ob_out[p % 2], 8 * t - 8 * (p % 2))
                    nc.gpsimd.tensor_tensor(ob[:, p % 2, :], xg[:], xqb[:, p, :], ALU.add).then_inc(ob_done, 1)

                def step(t, p, left=RING):
                    if not (isinstance(t, int) and t == 0):
                        output(t - 1, (p - 1) % RING)
                    if left >= 2:
                        prep(t + 2, (p + 2) % RING)

                prep(0, 0)
                prep(1, 1)
                run_steps(pool, step)
                output(STEPS - 1, RING - 1)

            @block.vector
            def _(dve):
                MARKS = 9

                def plain():
                    dve.sem_inc(waited, 1)

                def query_mask(s, p):
                    dve.wait_ge(gram_mm, s + 1)
                    wait(dve, zbar_mm, s - 1)
                    nc.vector.scalar_tensor_tensor(out=pm[:, p % 2, :], in0=prep_bank[:, R2:R2 + P], scalar=1.0,
                                                   in1=tim[:], op0=ALU.add, op1=ALU.mult).then_inc(mask_done, 1)

                def pair_mask(s, p):
                    nc.vector.scalar_tensor_tensor(out=pair[:, p % 2, :], in0=prep_bank[:, R2 + P:R2 + 2 * P],
                                                   scalar=1.0, in1=blkt[:], op0=ALU.add, op1=ALU.mult).then_inc(pair_done, 1)

                def zbar_stats(t):
                    dve.wait_ge(zbar_mm, t + 1)
                    nc.vector.bn_stats(bst[:], zbar_bank[:, 0:F]).then_inc(bst_done, 1)

                def zbar_variance(t):
                    dve.wait_ge(bst_done, t + 1)
                    plain()
                    nc.vector.bn_aggr(bmv[:], bst[:]).then_inc(bvar_done, 1)

                def zbar_scale(t):
                    dve.wait_ge(bstd_done, t + 1)
                    nc.vector.reciprocal(brs[:], bstd[:]).then_inc(brs_done, 1)

                def zbar_shift(t):
                    dve.wait_ge(brs_done, t + 1)
                    nc.vector.tensor_scalar(shift[:], bmv[:, 0:1], brs[:, 0:1], -1.0, ALU.mult, ALU.mult).then_inc(shift_done, 1)

                def gradient(s, p, zbar, left):
                    n = [0]

                    def mark(ins):
                        n[0] += 1
                        ins.then_inc(v_order, 1)
                        return n[0]

                    def need(m):
                        dve.wait_ge(v_order, MARKS * s + m)

                    z = zbanks[p % 2][:, 0:F]
                    dve.wait_ge(z_mm, s + 1)
                    stats = mark(nc.vector.bn_stats(st[:], z))
                    if zbar:
                        query_mask(s, p)
                    need(stats)
                    plain()
                    nc.vector.bn_aggr(mv[:], st[:]).then_inc(var_done, 1)
                    mark(nc.vector.tensor_tensor(pz[:], z, g2[:], ALU.mult))
                    if zbar:
                        zbar_stats(s - 1)
                        if left:
                            pair_mask(s, p)
                        zbar_variance(s - 1)
                    dve.wait_ge(std_done, s + 1)
                    need(mark(nc.vector.reciprocal(r[:], std[:])))
                    dve.wait_ge(cc_done, s + 1)
                    mark(nc.vector.scalar_tensor_tensor(out=gy[:], in0=pz[:], scalar=r[:, 0:1], in1=cc[:, p % 2, :],
                                                        op0=ALU.mult, op1=ALU.add, accum_out=m1s[:]))
                    nc.vector.tensor_scalar(rr[:], rows[:, p, 3 * F:RC], r[:, 0:1], 1.0 / F, ALU.mult, ALU.mult).then_inc(rr_done, 1)
                    need(mark(nc.vector.tensor_tensor(r2[:], r[:], r[:], ALU.mult)))
                    if zbar:
                        zbar_scale(s - 1)
                    dot = mark(nc.vector.tensor_tensor_reduce(junk[:], gy[:], z, 1.0, 0.0, ALU.mult, ALU.add, es[:]))
                    mark(nc.vector.tensor_scalar(m1[:], m1s[:], 1.0 / F, None, ALU.mult))
                    if zbar:
                        zbar_shift(s - 1)
                    need(dot)
                    mark(nc.vector.tensor_scalar(sc[:], es[:], r2[:, 0:1], 1.0 / F, ALU.mult, ALU.mult))
                    need(MARKS - 1)
                    mark(nc.vector.scalar_tensor_tensor(out=wz[:], in0=z, scalar=sc[:, 0:1], in1=gy[:],
                                                        op0=ALU.mult, op1=ALU.subtract))
                    assert n[0] == MARKS
                    need(MARKS)
                    dve.wait_ge(rr_done, s + 1)
                    nc.vector.tensor_scalar(grad[:, p % 2, :], wz[:], m1[:, 0:1], rr[:, 0:1], ALU.add, ALU.mult).then_inc(grad_done, 1)

                def step(t, p, left=RING):
                    if left:
                        gradient(t + 1, (p + 1) % RING, True, left - 1)
                    else:
                        zbar_stats(t)
                        zbar_variance(t)
                        zbar_scale(t)
                        zbar_shift(t)

                query_mask(0, 0)
                pair_mask(0, 0)
                gradient(0, 0, False, RING)
                run_steps(dve, step)


def layer0_out(nc, a, g):
    sb, sem, con, bank = g["sb"], g["sem"], g["con"], g["bank"]
    xt, ffnT, attn_d, xn1, xn1T = g["xt"], g["ffnT"], g["attn_d"], g["xn1"], g["xn1T"]
    wo, wo_bias, up = g["wo"], g["wo_bias"], g["up"]
    with ExitStack() as c:
        yn, y2, tT = sb("yn", [P, 2, HD], c=c), sb("y2", [P, 2, HD], c=c), sb("tT", [P, 2, 2, HD], c=c)
        st, mv = sb("st", [P, 3, 6], c=c), sb("mv", [P, 2, 3, 2], c=c)
        std, rs, shift = sb("std", [P, 2, 3], c=c), sb("rs", [P, 2, 3], c=c), sb("oshift", [P, 2, 2], c=c)
        act_norms = sem("act_norms", c)
        at, at_in = g["att"], g["at_in"]
        tile = lambda n: (n % B) * TPB + n // B
        stats, var_done, std_done = (sem(n, c) for n in ("st_done", "var_d", "std_d"))
        rs_done, norm_done, tr_mm, cp_done, mm_done = (sem(n, c) for n in ("rs_d", "norm_d", "tr_d", "cp_d", "mm_d"))
        TURNS = NT + 7
        LAST_SUM = NT + 4
        on = lambda n, s: 0 <= n - s < NT
        with nc.Block() as block:
            @block.sync
            def _(sp):
                g["load_quarter"](sp, TPB - 1)
                g["m1"].load(sp, a)

            @block.gpsimd
            def _(pool):
                g["m1"].clear(nc)

            @block.vector
            def _(dve):
                nc.vector.memset(mv[:], 1.0).then_inc(stats, 1)
                dve.wait_ge(stats, 1)
                marks = 1
                for n in range(TURNS):
                    p = n % 2
                    if n >= 2:
                        dve.wait_ge(mm_done, min(n - 1, LAST_SUM))
                    if on(n, 0) and n % B == 0:
                        dve.wait_ge(at_in[n // B], 16 * B * H)
                    ix = tile(n - 6) if on(n, 6) else 0
                    norms = ((0, at[:, tile(n) if on(n, 0) else 0, :]), (3, bank[3 - p][:, 0:HD]), (6, xt[:, ix, :]))
                    for part, ks in enumerate(((0, 1), (2,))):
                        ks = [k for k in ks if on(n, norms[k][0])]
                        if part and ks:
                            nc.vector.tensor_tensor(xt[:, ix, :], xt[:, ix, :], bank[5 - p][:, 0:D], ALU.add).then_inc(stats, 1)
                            marks += 1
                            dve.wait_ge(stats, marks)
                        for k in ks:
                            nc.vector.bn_stats(st[:, k, :], norms[k][1]).then_inc(stats, 1)
                            marks += 1
                        dve.wait_ge(stats, marks)
                        for k in ks:
                            ins = nc.vector.bn_aggr(mv[:, p, k, :], st[:, k, :])
                        if not ks:
                            ins = nc.vector.memset(mv[:, p, 2 * part, :], 1.0)
                        ins.then_inc(var_done, 1)
                    dve.wait_ge(std_done, 2 * n + 1)
                    nc.vector.reciprocal(rs[:, p, 0:2], std[:, p, 0:2]).then_inc(rs_done, 1)
                    dve.wait_ge(rs_done, 3 * n + 1)
                    nc.vector.scalar_tensor_tensor(out=shift[:, p, :], in0=mv[:, p, 0:2, 0], scalar=-1.0, in1=rs[:, p, 0:2],
                                                   op0=ALU.mult, op1=ALU.mult).then_inc(rs_done, 1)
                    dve.wait_ge(std_done, 2 * n + 2)
                    nc.vector.reciprocal(rs[:, p, 2:3], std[:, p, 2:3]).then_inc(rs_done, 1)
                    dve.wait_ge(rs_done, 3 * n + 3)
                    if on(n, 6):
                        nc.vector.tensor_scalar(xn1[:, ix, :], xt[:, ix, :], mv[:, p, 2, 0:1], rs[:, p, 2:3],
                                                ALU.subtract, ALU.mult).then_inc(norm_done, 1)

            @block.scalar
            def _(act):
                for n in range(TURNS):
                    p = n % 2
                    def deviation(part, ks):
                        act.wait_ge(var_done, 2 * n + 1 + part)
                        nc.scalar.activation(std[:, p, ks], mv[:, p, ks, 1], ACT.Sqrt, bias=con("eps5")).then_inc(std_done, 1)

                    deviation(0, slice(0, 2))
                    if n:
                        act.wait_ge(tr_mm, n)
                        if on(n, 1):
                            ins = nc.scalar.activation(tT[:, p, 0, :], bank[p][:, 0:HD], ACT.Copy)
                        if on(n, 4):
                            ins = nc.scalar.activation(tT[:, p, 1, :], bank[p][:, HD:2 * HD], ACT.Copy)
                        if on(n, 7):
                            i = tile(n - 7)
                            ins = nc.scalar.activation(xn1T[:, i * P:(i + 1) * P], bank[6 + p][:, 0:P], ACT.Copy)
                        ins.then_inc(cp_done, 1)
                    deviation(1, slice(2, 3))
                    act.wait_ge(rs_done, 3 * n + 2)
                    if on(n, 0):
                        nc.scalar.activation(yn[:, p, :], at[:, tile(n), :], ACT.Identity, bias=shift[:, p, 0:1],
                                             scale=rs[:, p, 0:1]).then_inc(act_norms, 1)
                    if on(n, 3):
                        nc.scalar.activation(y2[:, p, :], bank[3 - p][:, 0:HD], ACT.Identity, bias=shift[:, p, 1:2],
                                             scale=rs[:, p, 1:2]).then_inc(act_norms, 1)

            @block.tensor
            def _(pe):
                for n in range(1, TURNS):
                    p = n % 2
                    pe.wait_ge(act_norms, min(n, NT) + max(0, min(n - 3, NT)))
                    if n >= 7:
                        pe.wait_ge(norm_done, n - 6)
                    if n >= 3:
                        pe.wait_ge(cp_done, n - 2)
                    ins = None
                    if on(n, 1):
                        for k in range(2):
                            ins = nc.tensor.transpose(bank[p][:, k * P:(k + 1) * P], yn[:, 1 - p, k * P:(k + 1) * P], con("ident"))
                    if on(n, 4):
                        for k in range(2):
                            ins = nc.tensor.transpose(bank[p][:, HD + k * P:HD + (k + 1) * P], y2[:, 1 - p, k * P:(k + 1) * P], con("ident"))
                    if on(n, 7):
                        ins = nc.tensor.transpose(bank[6 + p][:, 0:P], xn1[:, tile(n - 7), :], con("ident"))
                    ins.then_inc(tr_mm, 1)
                    if n >= 2:
                        pe.wait_ge(cp_done, n - 1)
                    ins = None
                    if on(n, 2):
                        dst = bank[2 + p][:, 0:HD]
                        nc.tensor.matmul(dst, con("ones", 1), wo_bias, start=True, stop=False)
                        for k in range(2):
                            ins = nc.tensor.matmul(dst, tT[:, 1 - p, 0, k * P:(k + 1) * P], wo[:, k, :], start=False, stop=(k == 1))
                    if on(n, 5):
                        i = tile(n - 5)
                        dst = bank[4 + p][:, 0:D]
                        nc.tensor.matmul(dst, ffnT[:, i * P:(i + 1) * P], con("ident"), start=True, stop=False)
                        for k in range(2):
                            ins = nc.tensor.matmul(dst, tT[:, 1 - p, 1, k * P:(k + 1) * P], up[:, k, :], start=False, stop=(k == 1))
                    if ins is not None:
                        ins.then_inc(mm_done, 1)
                    elif n == 1:
                        pe.sem_inc(mm_done, 1)


class Layer1:

    def __init__(self, nc, sb, sem, ffnT, region1):
        self.w_in, self.cleared = sem("l1_weights"), sem("l1_cleared")
        self.gate_w, self.w1 = sb("gate_w", [P, NE]), sb("w1e", [P, 4, P])
        self.w2, self.b1, self.b2 = sb("w2e", [P, 4, D]), sb("b1e", [P, 4]), sb("b2e", [NE, D])
        self.region1 = region1
        self.raw = self.region1[:, 0:3 * HD].rearrange("p (n k d) -> p n k d", n=3, k=2)
        self.raw_o = self.region1[:, 3 * HD:4 * HD]
        self.wT, self.w_outT = sb("wT", [P, 3, HD]), sb("w_outT", [P, 2, D])
        self.bx, self.bg, self.bd, self.cb = (sb(n, [P, 2]) for n in ("bx", "bg", "bd", "cb"))
        self.cw = sb("cw", [P, 2, 3])
        self.out_b, self.lng, self.lnb = sb("out_b", [P, D]), sb("lng", [P, D]), sb("lnb", [P, D])
        self.a_raw, self.b_ssm, self.c_ssm = (sb(n, [P, 2, NS]) for n in ("a_raw", "b_ssm", "c_ssm"))
        self.win = sb("win", [P, 2, NG, P])
        self.wst = sb("wst", [P, 2, NG, P])
        self.d0 = sb("d0", [P, NG, B, NCH])
        self.kpad = sb("kpad", [P, 2, 2 * TC])
        self.gT = ffnT
        self.loads = 0

    def load(self, eng, a):
        def get(dst, src):
            eng.dma_start(dst, src).then_inc(self.w_in, 16)
            self.loads += 1

        M, A = lambda n: a["L1_ffn_" + n], lambda n: a["L1_attn_" + n]
        get(self.gate_w[:], M("gate_w"))
        for q in range(4):
            get(self.w1[:, q, :].rearrange("d (e h) -> d e h", e=2), M("w1")[2 * q:2 * q + 2].rearrange("e d h -> d e h"))
        get(self.w2[:], M("w2").rearrange("(q e) h d -> (e h) q d", q=4))
        get(self.b1[:], M("b1").rearrange("(q e) h -> (e h) q", q=4))
        get(self.b2[:], M("b2"))
        for n, name in enumerate(("W_x", "W_g", "W_dt")):
            get(self.raw[:, n, :, :], A(name).rearrange("(k p) d -> p k d", k=2))
        get(self.raw_o, A("W_out"))
        for dst, name in ((self.bx, "b_x"), (self.bg, "b_g"), (self.bd, "b_dt"), (self.cb, "conv_b")):
            get(dst[:], A(name).rearrange("(k p) -> p k", k=2))
        get(self.cw[:], A("conv_w").rearrange("(k p) o w -> p k (o w)", k=2))
        for dst, name in ((self.out_b, "b_out"), (self.lng, "ln_g"), (self.lnb, "ln_b")):
            get(dst[:], A(name).partition_broadcast(P))
        for dst, name in ((self.a_raw, "A_raw"), (self.b_ssm, "B_ssm"), (self.c_ssm, "C_ssm")):
            get(dst[:], A(name).rearrange("(k p) s -> p k s", k=2))

    def clear(self, nc):
        for v in (self.win, self.wst, self.d0, self.kpad):
            nc.gpsimd.memset(v[:], 0.0).then_inc(self.cleared, 1)


def layer1(nc, a, out, g):
    sb, sem, con, bank, m1 = g["sb"], g["sem"], g["con"], g["bank"], g["m1"]
    xt, xn1, xn1T, lna_d = g["xt"], g["xn1"], g["xn1T"], g["lna_d"]
    gT, win, wst, d0, kpad, wT, w_outT = m1.gT, m1.win, m1.wst, m1.d0, m1.kpad, m1.wT, m1.w_outT
    a_raw, b_ssm, c_ssm, cw, cb = m1.a_raw, m1.b_ssm, m1.c_ssm, m1.cw, m1.cb
    NBC = B * NCH
    NU = 2 * B
    with ExitStack() as c:
        uT = sb("uT", [P, 2, TOK], c=c)
        yT = uT
        gt, mx, sm = sb("gt", [P, NT, NE], c=c), sb("mx", [P, NT], c=c), sb("sm", [P, NT], c=c)
        idx = sb("idx", [P, NT, 8], U32, c=c)
        he = sb("he", [P, 8, 512], c=c)
        region1 = m1.region1
        gate = region1[:, :].rearrange("p (n l) -> p n l", n=NU)
        v = region1[:, :].rearrange("p (k n j) -> p k n j", k=2, n=NBC)
        region2 = sb("region2", [P, NU * L], c=c)
        ab = region2[:, :].rearrange("p (n l) -> p n l", n=NU)
        wtap = region2[:, 0:NG * P].rearrange("p (j c) -> p j c", j=NG)
        W = 2 * (L + 2)
        region3 = sb("region3", [P, W + 4 * L], c=c)
        ub = region3[:, 0:W].rearrange("p (n l) -> p n l", n=2)
        cv, df = (region3[:, W + 2 * L * i:W + 2 * L * (i + 1)].rearrange("p (n l) -> p n l", n=2) for i in range(2))
        lg, ex, top, idf = (he[:, 0, NT * 8 * i:NT * 8 * (i + 1)].rearrange("p (i e) -> p i e", e=8) for i in range(4))
        x2 = region3[:, 0:2 * TC * NG].rearrange("p (k r j) -> p k r j", k=2, r=TC)
        ex2 = region3[:, 2 * TC * NG:3 * TC * NG].rearrange("p (j r) -> p j r", j=NG)
        state_flat = uT[:, 1, :]
        state = state_flat.rearrange("p (j b c) -> p j b c", j=NG, b=B)
        region4 = sb("region4", [P, NBC * NG], c=c)
        lnar = region4[:, 0:2 * NG * NS].rearrange("p (k j s) -> p k j s", k=2, j=NG)
        kex = region4[:, 2 * NG * NS:2 * NG * NS + 2 * TC * NS].rearrange("p (k t s) -> p k t s", k=2, t=TC)
        ybuf = region4[:, :].rearrange("p (n j) -> p n j", n=NBC)
        z = win[:, 0, 0:NT, :]
        zg = win[:, 0, NT:2 * NT, :]
        rl = he[:, 7, :]
        dtr, dtl = sb("dtr", [P, 2, B], c=c), sb("dtl", [P, 2], c=c)
        dt, t1 = sb("dt", [P, 2], c=c), sb("t1", [P, 2, NS], c=c)
        asp, bsp, lna, cbs = (sb(n, [P, 2, NS], c=c) for n in ("asp", "bsp", "lna", "cbs"))
        lnac, cbc, a32 = sb("lnac", [P, NG], c=c), sb("cbc", [P, NG], c=c), sb("a32", [P, NG], c=c)
        st, mv = sb("fst", [P, NT, 6], c=c), sb("fmv", [P, NT, 2], c=c)
        std, rs, shift = sm, mx, gt[:, :, 0]

        S = lambda *names: tuple(sem(n, c) for n in names)
        gate_mm, mx_done, ex_done, gates_done, gt_mm, gT_done, moe_order = S(
            "gate_mm", "mx_done", "ex_done", "gates_done", "gt_mm", "gT_done", "moe_order")
        up_mm, pick_mm, he_done, gated, down_mm, y_done = S("e_up", "e_pick", "he_done", "gated", "e_down", "y_done")
        w_mm, w_done, pads, u_mm, g_mm, dt_mm = S("mix_tr", "mix_cp", "pads", "u_mm", "g_mm", "dt_mm")
        u_done, gate_done, conv_done, diff_done, blend_in, uT_done = S(
            "u_done", "gate_done", "conv_done", "diff_done", "blend_in", "uT_done")
        abs_done, relu_done, exp_done, ln_done = S("abs_done", "relu_done", "exp_done", "ln_done")
        a_stage, lna_done, t1_done, kex_stage = S("a_stage", "lna_done", "t1_done", "kex_stage")
        v_order, lna_out, lna_in, lnac_done, win_done, a32_done, d0_done = S(
            "ssm_v", "lna_out", "lna_in", "lnac_done", "win_done", "a32_done", "d0_done")
        v_done, x2_done, ex2_stage, wst_done, taps = S(
            "v_done", "x2_done", "ex2_stage", "wst_done", "taps")
        in_mm, scanned, y_mm, y_cp, y_tr = S("in_mm", "scanned", "y_mm", "y_cp", "y_tr")
        pool_stage, o_mm, var_done, std_done, shift_done, zn_done, stored = S(
            "pool_stage", "o_mm", "fvar_done", "fstd_done", "fshift_done",
            "zn_done", "stored")
        sum_done = [sem(f"sum_done_{e}", c) for e in ("pool", "vector")]
        half = lambda k: slice(k * P, (k + 1) * P)
        row = lambda b: slice(b * L, (b + 1) * L)
        quad = lambda q: slice(32 * q, 32 * q + 32)
        out_banks, down_banks = bank[0:4], (bank[2], bank[0], bank[1], bank[4])


        def scale_add(nc, eng, m):
            ts = slice(4 * m, 4 * m + 4)
            tt = nc.gpsimd.tensor_tensor if m < 2 else nc.vector.tensor_tensor
            eng.wait_ge(zn_done, 4 * m + 4)
            mine = sum_done[m // 2]
            tt(zg[:, ts, :], z[:, ts, :], m1.lng[:, None, :].broadcast_to([P, 4, D]), ALU.mult).then_inc(mine, 1)
            eng.wait_ge(mine, 2 * (m % 2) + 1)
            eng.wait_ge(y_done, m + 1)
            tt(zg[:, ts, :], zg[:, ts, :], xt[:, ts, :], ALU.add).then_inc(mine, 1)

        with nc.Block() as block:
            @block.tensor
            def _(pe):
                def unit(t, q):
                    n = 4 * t + q
                    tok = slice(t * 512, t * 512 + 512)
                    if n >= 2:
                        pe.wait_ge(he_done, n - 1)
                    else:
                        pe.wait_ge(relu_done, NU - 1 + n)
                    nc.tensor.matmul(bank[4 + n % 2][:, :], m1.w1[:, q, :], xn1T[:, tok], start=True, stop=True).then_inc(up_mm, 1)
                    pe.wait_ge(gT_done, 4)
                    if n >= 2:
                        pe.wait_ge(gated, n - 1)
                    nc.tensor.matmul(bank[6 + n % 2][:, :], con("pick", NE)[:, q * P:(q + 1) * P], gT[0:NE, tok],
                                     start=True, stop=True).then_inc(pick_mm, 1)

                def down(t):
                    pe.wait_ge(gated, 4 * t + 4)
                    s, v = ((gate_done, NU), (u_done, NU), (u_done, NU), (he_done, 16))[t]
                    pe.wait_ge(s, v)
                    for i in range(4):
                        dst = down_banks[t][:, i * P:(i + 1) * P]
                        nc.tensor.matmul(dst, gT[0:NE, t * 512 + i * P:t * 512 + (i + 1) * P], m1.b2[:], start=True, stop=False)
                        for q in range(4):
                            mm = nc.tensor.matmul(dst, he[:, (4 * t + q) % 8, i * P:(i + 1) * P], m1.w2[:, q, :], start=False, stop=(q == 3))
                    mm.then_inc(down_mm, 1)

                def chunk_in(m):
                    for jj in range(8):
                        for k in range(2):
                            mm = nc.tensor.matmul(bank[m][:, jj * NBC:(jj + 1) * NBC], win[:, k, 8 * m + jj, :],
                                                  v[:, k, :, 8 * m + jj], start=(k == 0), stop=(k == 1))
                    mm.then_inc(in_mm, 1)

                def chunk_out(n):
                    k, m = divmod(n, 4)
                    pe.wait_ge(taps, 4 * (n + 1))
                    pe.wait_ge(scanned, 4)
                    if n >= 2:
                        pe.wait_ge(y_cp, n - 1)
                    dst = bank[2 + n % 2]
                    for jj in range(8):
                        j = 8 * m + jj
                        nc.tensor.matmul(dst[:, jj * NBC:(jj + 1) * NBC], wtap[:, j, :], v[:, k, :, j], start=True, stop=False)
                        mm = nc.tensor.matmul(dst[:, jj * NBC:(jj + 1) * NBC], wst[:, k, j, :],
                                              state_flat[:, j * NBC:(j + 1) * NBC], start=False, stop=True)
                    mm.then_inc(y_mm, 1)

                def u_product(n):
                    b, k = divmod(n, 2)
                    if n >= 2:
                        pe.wait_ge(u_done, n - 1)
                    nc.tensor.matmul(bank[n % 2][:, :], wT[:, 0, half(k)], xn1T[:, row(b)], start=True, stop=True).then_inc(u_mm, 1)

                def gate_product(n):
                    b, k = divmod(n, 2)
                    if n >= 2:
                        pe.wait_ge(gate_done, n - 1)
                    nc.tensor.matmul(bank[2 + n % 2][:, :], wT[:, 1, half(k)], xn1T[:, row(b)], start=True, stop=True).then_inc(g_mm, 1)

                def dt_product(n):
                    b, k = divmod(n, 2)
                    if n >= 2:
                        pe.wait_ge(relu_done, n - 1)
                    nc.tensor.matmul(bank[4 + n % 2][:, :], wT[:, 2, half(k)], xn1T[:, row(b)], start=True, stop=True).then_inc(dt_mm, 1)

                def out_product(k, m):
                    for jj in range(4):
                        mm = nc.tensor.matmul(out_banks[m][:, half(jj)], yT[:, k, half(4 * m + jj)], w_outT[:, k, :],
                                              start=(k == 0 and jj == 0), stop=(k == 1), skip_group_check=True)
                    if k:
                        mm.then_inc(o_mm, 1)

                pe.wait_ge(m1.w_in, 16 * m1.loads)
                for n in range(4):
                    for k in range(2):
                        src = m1.raw[:, n, k, :] if n < 3 else m1.raw_o[:, half(k)]
                        mm = nc.tensor.transpose(bank[n][:, half(k)], src, con("ident"))
                    mm.then_inc(w_mm, 1)
                pe.wait_ge(w_done, 4)
                u_product(0)
                u_product(1)
                for n in range(4):
                    gate_product(n)
                for i in range(NT):
                    mm = nc.tensor.matmul(bank[7][:, i * NE:(i + 1) * NE], xn1T[:, i * P:(i + 1) * P], m1.gate_w[:], start=True, stop=True)
                mm.then_inc(gate_mm, 1)
                u_product(2)
                for n in range(4, NU):
                    gate_product(n)
                u_product(3)
                def turn_gates(i):
                    for k in range(4):
                        mm = nc.tensor.transpose(bank[6 + i % 2][0:NE, k * P:(k + 1) * P], gt[:, 4 * i + k, :], con("ident"))
                    mm.then_inc(gt_mm, 1)

                for n in range(NU):
                    dt_product(n)
                    if n == 1:
                        u_product(4)
                        pe.wait_ge(gates_done, 1)
                        turn_gates(0)
                        turn_gates(1)
                    if n == 3:
                        pe.wait_ge(gT_done, 1)
                        turn_gates(2)
                        pe.wait_ge(gT_done, 2)
                        turn_gates(3)
                    if n == 5:
                        u_product(5)
                u_product(6)
                unit(0, 0)
                u_product(7)
                for q in range(1, 4):
                    unit(0, q)
                unit(1, 0)
                down(0)
                for q in range(1, 4):
                    unit(1, q)
                unit(2, 0)
                down(1)
                for q in range(1, 4):
                    unit(2, q)
                down(2)
                pe.wait_ge(win_done, 8)
                pe.wait_ge(v_done, 2)
                pe.wait_ge(y_done, 3)
                for m in range(4):
                    chunk_in(m)
                unit(3, 0)
                unit(3, 1)
                pe.wait_ge(wst_done, 8)
                for n in range(8):
                    chunk_out(n)
                pe.wait_ge(y_tr, 1)
                out_product(0, 0)
                out_product(0, 1)
                unit(3, 2)
                pe.wait_ge(y_cp, 8)
                out_product(0, 2)
                out_product(0, 3)
                unit(3, 3)
                pe.wait_ge(y_tr, 2)
                for m in range(4):
                    out_product(1, m)
                down(3)

            @block.scalar
            def _(act):
                def hidden(t, q):
                    n = 4 * t + q
                    act.wait_ge(up_mm, n + 1)
                    if t >= 2:
                        act.wait_ge(down_mm, t - 1)
                    nc.scalar.activation(he[:, n % 8, :], bank[4 + n % 2][:, :], ACT.Gelu, bias=m1.b1[:, q:q + 1]).then_inc(he_done, 1)

                def u_tile(n):
                    act.wait_ge(u_mm, n + 1)
                    if n >= 2:
                        act.wait_ge(conv_done, 3 * (n - 1))
                        act.wait_ge(diff_done, n - 1)
                    nc.scalar.activation(ub[:, n % 2, 1:L + 1], bank[n % 2][:, :], ACT.Identity, bias=m1.bx[:, n % 2:n % 2 + 1]).then_inc(u_done, 1)

                def tap_blocks(n):
                    k, m = divmod(n, 4)
                    js = slice(8 * m, 8 * m + 8)
                    for q in range(4):
                        nc.scalar.activation(wtap[quad(q), js, quad(q)], x2[quad(q), k, :, js].rearrange("p r j -> p j r"),
                                             ACT.Copy).then_inc(taps, 1)

                def result(n):
                    m = n % 4
                    act.wait_ge(y_mm, n + 1)
                    if n == 0:
                        act.wait_ge(kex_stage, 4)
                    if n == 4:
                        act.wait_ge(y_tr, 1)
                    nc.scalar.activation(ybuf[:, :, 8 * m:8 * m + 8].rearrange("p n j -> p j n"),
                                         bank[2 + n % 2][:, :].rearrange("p (j n) -> p j n", j=8), ACT.Copy).then_inc(y_cp, 1)

                act.wait_ge(a_stage, 1)
                nc.scalar.activation(asp[:], asp[:], ACT.Exp, scale=-1.0).then_inc(a_stage, 1)
                for n in range(4):
                    act.wait_ge(w_mm, n + 1)
                    dst = wT[:, n, :] if n < 3 else w_outT[:].rearrange("p k d -> p (k d)")
                    nc.scalar.activation(dst, bank[n][:, 0:HD], ACT.Copy).then_inc(w_done, 1)
                act.wait_ge(pads, 1)
                u_tile(0)
                u_tile(1)
                for n in range(NU):
                    act.wait_ge(g_mm, n + 1)
                    nc.scalar.activation(gate[:, n, :], bank[2 + n % 2][:, :], ACT.Sigmoid, bias=m1.bg[:, n % 2:n % 2 + 1]).then_inc(gate_done, 1)
                    if n == 3:
                        act.wait_ge(mx_done, 1)
                        nc.scalar.activation(ex, lg, ACT.Exp).then_inc(ex_done, 1)
                        u_tile(2)
                u_tile(3)
                for n in range(NU):
                    b, k = divmod(n, 2)
                    act.wait_ge(dt_mm, n + 1)
                    nc.scalar.activation(ab[:, n, :], bank[4 + n % 2][:, :], ACT.Abs, bias=m1.bd[:, k:k + 1]).then_inc(abs_done, 1)
                    if n:
                        act.wait_ge(relu_done, n)
                    nc.scalar.activation(rl, bank[4 + n % 2][:, :], ACT.Relu, bias=m1.bd[:, k:k + 1],
                                         accum_out=dtr[:, k, b:b + 1]).then_inc(relu_done, 1)
                    if n in (2, 5):
                        u_tile(4 + n // 5)
                u_tile(6)
                hidden(0, 0)
                hidden(0, 1)
                u_tile(7)
                hidden(0, 2)
                hidden(0, 3)
                act.wait_ge(abs_done, NU)
                nc.scalar.activation(ab, ab, ACT.Exp, scale=-1.0).then_inc(exp_done, 1)
                act.wait_ge(a_stage, 2)
                nc.scalar.activation(asp[:], asp[:], ACT.Ln, bias=1.0).then_inc(a_stage, 1)
                act.wait_ge(exp_done, 1)
                for k in range(2):
                    nc.scalar.activation(ab[:, k:NU:2, :], ab[:, k:NU:2, :], ACT.Ln, bias=1.0, accum_out=dtl[:, k:k + 1]).then_inc(ln_done, 1)
                act.wait_ge(lna_done, 1)
                nc.scalar.activation(t1[:], lna[:], ACT.Exp).then_inc(t1_done, 1)
                act.wait_ge(kex_stage, 2)
                nc.scalar.activation(kex, kex, ACT.Exp).then_inc(kex_stage, 1)
                for t in (1, 2):
                    for q in range(4):
                        hidden(t, q)
                act.wait_ge(lna_in, 64)
                act.wait_ge(m1.cleared, 4)
                for q in range(4):
                    for k in range(2):
                        at = q * 32 + k * NS
                        nc.scalar.activation(win[quad(q), k, :, at:at + NS], lnar[quad(q), k, :, :], ACT.Exp,
                                             scale=con("expo")[quad(q), :]).then_inc(win_done, 1)
                act.wait_ge(ex2_stage, 1)
                nc.scalar.activation(ex2, ex2, ACT.Exp).then_inc(ex2_stage, 1)
                act.wait_ge(lnac_done, 1)
                nc.scalar.activation(a32[:], lnac[:], ACT.Exp, scale=float(TC)).then_inc(a32_done, 1)
                act.wait_ge(a32_done, 1)
                nc.scalar.activation(d0[:, :, :, 1:NCH], a32[:, :, None, None].broadcast_to([P, NG, B, NCH - 1]), ACT.Copy).then_inc(d0_done, 1)
                act.wait_ge(x2_done, 2)
                act.wait_ge(pool_stage, 3)
                for n in range(4):
                    tap_blocks(n)
                act.wait_ge(ex2_stage, 3)
                for q in range(4):
                    nc.scalar.activation(wst[quad(q), 0, :, quad(q)], ex2[quad(q), :, :], ACT.Identity,
                                         scale=con("head")[quad(q), 0:1]).then_inc(wst_done, 1)
                hidden(3, 0)
                hidden(3, 1)
                for n in range(8):
                    result(n)
                    if n < 4:
                        tap_blocks(4 + n)
                hidden(3, 2)
                hidden(3, 3)
                for m in range(4):
                    ts = slice(4 * m, 4 * m + 4)
                    act.wait_ge(var_done, m + 1)
                    nc.scalar.activation(std[:, ts], mv[:, ts, 1], ACT.Sqrt, bias=con("eps5")).then_inc(std_done, 1)
                    act.wait_ge(shift_done, m + 1)
                    for i in range(4 * m, 4 * m + 4):
                        nc.scalar.activation(z[:, i, :], z[:, i, :], ACT.Identity, bias=shift[:, i:i + 1], scale=rs[:, i:i + 1]).then_inc(zn_done, 1)

            @block.vector
            def _(dve):
                ch = Chain(dve, moe_order)
                wide = lambda x: x[:, :, None].broadcast_to([P, NT, NE])

                def gates():
                    logits = bank[7][:, 0:NT * NE].rearrange("p (i e) -> p i e", e=NE)
                    dve.wait_ge(gate_mm, 1)
                    ch.link(nc.vector.tensor_reduce(mx[:], logits, AX, ALU.max))
                    nc.vector.tensor_tensor(lg, logits, wide(mx[:, :]), ALU.subtract).then_inc(mx_done, 1)
                    dve.wait_ge(ex_done, 1)
                    ch.link(nc.vector.tensor_reduce(sm[:], ex, AX, ALU.add))
                    ch.link(nc.vector.reciprocal(sm[:], sm[:]))
                    ch.link(nc.vector.tensor_tensor(ex, ex, wide(sm[:, :]), ALU.mult))
                    for i in range(NT):
                        ch.mark(nc.vector.max(top[:, i, :], ex[:, i, :]))
                    dve.wait_ge(moe_order, ch.n)
                    for i in range(NT):
                        ch.mark(nc.vector.max_index(idx[:, i, :], top[:, i, :], ex[:, i, :]))
                    dve.wait_ge(moe_order, ch.n)
                    ch.link(nc.vector.tensor_copy(idf, idx[:]))
                    iota = con("iota8")[:, None, :].broadcast_to([P, NT, NE])
                    ch.mark(nc.vector.tensor_tensor(lg, iota, idf[:, :, 0:1].broadcast_to([P, NT, NE]), ALU.is_equal))
                    ch.mark(nc.vector.tensor_tensor(gt[:], iota, idf[:, :, 1:2].broadcast_to([P, NT, NE]), ALU.is_equal))
                    ch.link(nc.vector.tensor_tensor(sm[:], top[:, :, 0], top[:, :, 1], ALU.add))
                    ch.link(nc.vector.tensor_tensor(gt[:], gt[:], lg, ALU.add))
                    nc.vector.tensor_tensor(gt[:], gt[:], wide(sm[:, :]), ALU.mult).then_inc(gates_done, 1)

                def gate_rows(k):
                    dve.wait_ge(gt_mm, k + 1)
                    nc.vector.tensor_copy(gT[0:NE, k * 512:(k + 1) * 512], bank[6 + k % 2][0:NE, :]).then_inc(gT_done, 1)

                def apply_gate(n):
                    dve.wait_ge(he_done, n + 1)
                    dve.wait_ge(pick_mm, n + 1)
                    nc.vector.tensor_tensor(he[:, n % 8, :], he[:, n % 8, :], bank[6 + n % 2][:, :], ALU.mult).then_inc(gated, 1)

                def add_experts(t):
                    dve.wait_ge(down_mm, t + 1)
                    dve.wait_ge(pool_stage, 1)
                    rows = xt[:, 4 * t:4 * t + 4, :].rearrange("p i d -> p (i d)")
                    nc.vector.tensor_tensor(rows, rows, down_banks[t][:, :], ALU.add).then_inc(y_done, 1)

                def conv(n):
                    b, k = divmod(n, 2)
                    p = n % 2
                    dve.wait_ge(u_done, n + 1)
                    if n >= 2:
                        dve.wait_ge(uT_done, n - 1)
                    nc.vector.tensor_scalar(cv[:, p, :], ub[:, p, 0:L], cw[:, k, 0:1], cb[:, k:k + 1], ALU.mult, ALU.add).then_inc(conv_done, 1)
                    dve.wait_ge(conv_done, 3 * n + 1)
                    nc.vector.scalar_tensor_tensor(out=cv[:, p, :], in0=ub[:, p, 1:L + 1], scalar=cw[:, k, 1:2], in1=cv[:, p, :],
                                                   op0=ALU.mult, op1=ALU.add).then_inc(conv_done, 1)
                    dve.wait_ge(conv_done, 3 * n + 2)
                    nc.vector.scalar_tensor_tensor(out=cv[:, p, :], in0=ub[:, p, 2:L + 2], scalar=cw[:, k, 2:3], in1=cv[:, p, :],
                                                   op0=ALU.mult, op1=ALU.add).then_inc(conv_done, 1)

                def blend(n):
                    b, k = divmod(n, 2)
                    dve.wait_ge(blend_in, n + 1)
                    nc.vector.tensor_tensor(uT[:, k, row(b)], cv[:, n % 2, :], df[:, n % 2, :], ALU.add).then_inc(uT_done, 1)

                sc = Chain(dve, v_order)
                w = sc.link
                nc.vector.memset(ub, 0.0).then_inc(pads, 1)
                dve.wait_ge(m1.w_in, 16 * m1.loads)
                w(nc.vector.tensor_scalar(asp[:], a_raw[:], -1.0, None, ALU.mult))
                nc.vector.tensor_tensor(asp[:], asp[:], a_raw[:], ALU.max).then_inc(a_stage, 1)
                w(nc.vector.tensor_scalar(bsp[:], a_raw[:], 0.0, None, ALU.max))
                conv(0)
                conv(1)
                gates()
                blend(0)
                for n in range(2, NU):
                    conv(n)
                    blend(n - 1)
                    if n in (2, 3):
                        gate_rows(2 * n - 4)
                        gate_rows(2 * n - 3)
                    if n >= 6:
                        apply_gate(2 * n - 12)
                        apply_gate(2 * n - 11)
                blend(NU - 1)
                dve.wait_ge(uT_done, NU)
                for k in range(2):
                    nc.vector.transpose(v[:, k, :, :], uT[:, k, :].rearrange("p (n r) -> p n r", r=TC)).then_inc(v_done, 1)
                w(nc.vector.tensor_reduce(dt[:], dtr[:], AX, ALU.add))
                dve.wait_ge(ln_done, 2)
                dve.wait_ge(a_stage, 3)
                sc.mark(nc.vector.tensor_tensor(asp[:], bsp[:], asp[:], ALU.add))
                w(nc.vector.tensor_tensor(dt[:], dt[:], dtl[:], ALU.add))
                sc.mark(nc.vector.tensor_scalar(asp[:], asp[:], -1.0, None, ALU.mult))
                w(nc.vector.tensor_scalar(dt[:], dt[:], 1.0 / TOK, 0.001, ALU.mult, ALU.max))
                w(nc.vector.tensor_scalar(dt[:], dt[:], 2.0, None, ALU.min))
                nc.vector.tensor_tensor(lna[:], asp[:], dt[:, :, None].broadcast_to([P, 2, NS]), ALU.mult).then_inc(lna_done, 1)
                dve.wait_ge(lna_done, 1)
                nc.vector.transpose(lnac[:], lna[:].rearrange("p k s -> p (k s)")).then_inc(lnac_done, 1)
                for k in range(2):
                    nc.vector.tensor_tensor(kex[:, k, :, :], lna[:, k, None, :].broadcast_to([P, TC, NS]),
                                            con("ramp0")[:, :, None].broadcast_to([P, TC, NS]), ALU.mult).then_inc(kex_stage, 1)
                w(nc.vector.tensor_scalar(asp[:], asp[:], 1e-6, None, ALU.add))
                w(nc.vector.reciprocal(asp[:], asp[:]))
                apply_gate(4)
                add_experts(0)
                dve.wait_ge(t1_done, 1)
                w(nc.vector.tensor_scalar(t1[:], t1[:], -1.0, None, ALU.add))
                w(nc.vector.tensor_tensor(t1[:], t1[:], asp[:], ALU.mult))
                w(nc.vector.tensor_tensor(t1[:], t1[:], b_ssm[:], ALU.mult))
                w(nc.vector.tensor_tensor(cbs[:], t1[:], c_ssm[:], ALU.mult))
                sc.mark(nc.vector.transpose(cbc[:], cbs[:].rearrange("p k s -> p (k s)")))
                apply_gate(5)
                dve.wait_ge(lnac_done, 1)
                nc.vector.tensor_tensor(ex2, lnac[:, :, None].broadcast_to([P, NG, TC]),
                                        con("ramp1")[:, None, :].broadcast_to([P, NG, TC]), ALU.mult).then_inc(ex2_stage, 1)
                apply_gate(6)
                dve.wait_ge(kex_stage, 3)
                for k in range(2):
                    w(nc.vector.tensor_tensor(kex[:, k, :, :], kex[:, k, :, :], cbs[:, k, None, :].broadcast_to([P, TC, NS]), ALU.mult))
                    apply_gate(7 + k)
                add_experts(1)
                dve.wait_ge(m1.cleared, 4)
                nc.vector.tensor_reduce(kpad[:, :, TC:2 * TC], kex, AX, ALU.add).then_inc(kex_stage, 1)
                apply_gate(9)
                dve.wait_ge(kex_stage, 4)
                for k in range(2):
                    pad = kpad[:, k, :]
                    window = bass.AP(tensor=pad.tensor, offset=pad.offset + TC, ap=[list(pad.ap[0]), [1, TC], [-1, TC]])
                    nc.vector.transpose(x2[:, k, :, :], window).then_inc(x2_done, 1)
                    apply_gate(10 + k)
                add_experts(2)
                dve.wait_ge(ex2_stage, 2)
                nc.vector.tensor_tensor(ex2, ex2, cbc[:, :, None].broadcast_to([P, NG, TC]), ALU.mult).then_inc(ex2_stage, 1)
                dve.wait_ge(ex2_stage, 3)

                dve.wait_ge(d0_done, 1)
                for m in range(4):
                    js = slice(8 * m, 8 * m + 8)
                    dve.wait_ge(in_mm, m + 1)
                    n = 8 * NBC - (m == 3)
                    w(nc.vector.tensor_tensor_scan(state_flat[:, 8 * m * NBC + 1:8 * m * NBC + 1 + n],
                                                   d0[:, js, :, :].rearrange("p j b c -> p (j b c)")[:, 0:n],
                                                   bank[m][:, 0:n], 0.0, ALU.mult, ALU.add))
                    nc.vector.memset(state[:, js, :, 0], 0.0).then_inc(scanned, 1)
                    nc.vector.tensor_scalar(wst[quad(m), 1, :, quad(m)], ex2[quad(m), :, :],
                                            con("head")[quad(m), 1:2], None, ALU.mult).then_inc(wst_done, 1)
                apply_gate(12)
                apply_gate(13)
                dve.wait_ge(y_cp, 4)
                nc.vector.transpose(yT[:, 0, :].rearrange("p (n r) -> p n r", r=TC), ybuf).then_inc(y_tr, 1)
                dve.wait_ge(y_cp, 8)
                nc.vector.transpose(yT[:, 1, :].rearrange("p (n r) -> p n r", r=TC), ybuf).then_inc(y_tr, 1)
                apply_gate(14)
                apply_gate(15)
                for m in range(5):
                    if m == 4:
                        add_experts(3)
                    if m < 4:
                        ts = slice(4 * m, 4 * m + 4)
                        dve.wait_ge(o_mm, m + 1)
                        if m == 0:
                            dve.wait_ge(pool_stage, 2)
                        w(nc.vector.tensor_tensor(z[:, ts, :].rearrange("p i d -> p (i d)"), out_banks[m][:, :],
                                                  xn1[:, ts, :].rearrange("p i d -> p (i d)"), ALU.add))
                        for i in range(4 * m, 4 * m + 4):
                            sc.mark(nc.vector.bn_stats(st[:, i, :], z[:, i, :]))
                        dve.wait_ge(v_order, sc.n)
                        for i in range(4 * m, 4 * m + 4):
                            ins = nc.vector.bn_aggr(mv[:, i, :], st[:, i, :])
                        ins.then_inc(var_done, 1)
                    if m:
                        ts = slice(4 * m - 4, 4 * m)
                        dve.wait_ge(std_done, m)
                        w(nc.vector.reciprocal(rs[:, ts], std[:, ts]))
                        w(nc.vector.tensor_tensor(shift[:, ts], mv[:, ts, 0], rs[:, ts], ALU.mult))
                        nc.vector.tensor_scalar(shift[:, ts], shift[:, ts], -1.0, None, ALU.mult).then_inc(shift_done, 1)
                for m in range(2, 4):
                    scale_add(nc, dve, m)

            @block.gpsimd
            def _(pool):
                pool.wait_ge(m1.w_in, 16 * m1.loads)
                nc.gpsimd.tensor_tensor(xt[:], xt[:], m1.lnb[:, None, :].broadcast_to([P, NT, D]), ALU.add).then_inc(pool_stage, 1)
                for n in range(NU):
                    p = n % 2
                    pool.wait_ge(conv_done, 3 * n + 3)
                    if n >= 2:
                        pool.wait_ge(uT_done, n - 1)
                    nc.gpsimd.tensor_tensor(df[:, p, :], ub[:, p, 1:L + 1], cv[:, p, :], ALU.subtract).then_inc(diff_done, 1)
                    pool.wait_ge(diff_done, n + 1)
                    pool.wait_ge(gate_done, n + 1)
                    nc.gpsimd.tensor_tensor(df[:, p, :], df[:, p, :], gate[:, n, :], ALU.mult).then_inc(blend_in, 1)
                nc.gpsimd.tensor_tensor(xn1[:], xn1[:], m1.out_b[:, None, :].broadcast_to([P, NT, D]), ALU.add).then_inc(pool_stage, 1)
                pool.wait_ge(ln_done, 2)
                nc.gpsimd.memset(region2[:], 0.0).then_inc(pool_stage, 1)
                for m in range(2):
                    scale_add(nc, pool, m)

            @block.sync
            def _(sp):
                sp.wait_ge(lna_done, 1)
                sp.dma_start(lna_d.rearrange("(k p) s -> p k s", k=2), lna[:]).then_inc(lna_out, 16)
                sp.wait_ge(lna_out, 16)
                for q in range(4):
                    src = lna_d.rearrange("(k q j) s -> q k j s", k=2, q=4)[q]
                    sp.dma_start(lnar[quad(q)], src.partition_broadcast(32)).then_inc(lna_in, 16)
                for m in (0, 2, 1, 3):
                    sp.wait_ge(sum_done[m // 2], 2 * (m % 2) + 2)
                    sp.dma_start(out[m].rearrange("(n p) d -> p n d", p=P), zg[:, 4 * m:4 * m + 4, :]).then_inc(stored, 16)
                sp.wait_ge(stored, 64)


_OUT = ((B, L, D), "float32")


def kernel(**inputs):
    import concourse.bacc as bacc
    from concourse.bass_utils import run_bass_kernel_spmd

    nc = bacc.Bacc("TRN2", target_bir_lowering=False, num_devices=1)
    arrays, aps = {}, {}
    for name, v in inputs.items():
        v = np.ascontiguousarray(v)
        arrays[f"in_{name}"] = v
        aps[name] = nc.dram_tensor(f"in_{name}", v.shape, mybir.dt.from_np(v.dtype), kind="ExternalInput").ap()
    arrays["in_constants"] = constants()
    const = nc.dram_tensor("in_constants", arrays["in_constants"].shape, F32, kind="ExternalInput").ap()
    out = nc.dram_tensor("out_0", _OUT[0], F32, kind="ExternalOutput").ap()
    build(nc, aps, const, out)
    r = run_bass_kernel_spmd(nc, [arrays], core_ids=[0])
    return r.results[0]["out_0"]
```
